# Optimizing a Trainium2 kernel written in Bass

```python
import numpy as np
import jax
import jax.numpy as jnp

def _softmax(x, axis=-1):
    return jax.nn.softmax(x, axis=axis)

def _gelu(x):
    return jax.nn.gelu(x, approximate=True)

def _silu(x):
    return jax.nn.silu(x)

def _sigmoid(x):
    return jax.nn.sigmoid(x)

def _layernorm(x, axis=-1, eps=1e-05):
    m = jnp.mean(x, axis=axis, keepdims=True)
    v = jnp.var(x, axis=axis, keepdims=True)
    return (x - m) / jnp.sqrt(v + eps)

def _scatter_add(tgt, idx, src, axis=0):
    return tgt.at[idx].add(src)

def _segment_sum(src, seg, n):
    return jax.ops.segment_sum(src, seg, n)
kernel_name = 'mk_seq_postln_d1_jaxref_r8_7c2ab9'

def setup_inputs(seed: int=0):
    np.random.seed(seed)
    _w = jnp.asarray

    def _L0_attn_setup():
        import math
        import jax, jax.numpy as jnp
        import numpy as np
        H, G = (16, 4)

        def alibi_bias(S, n_heads, dtype):
            n = 2 ** int(math.floor(math.log2(n_heads)))
            m0 = 2.0 ** (-8.0 / n)
            slopes = m0 ** np.arange(1, n + 1)
            if n < n_heads:
                m1 = 2.0 ** (-4.0 / n)
                slopes = np.concatenate([slopes, m1 ** np.arange(1, 1 + 2 * (n_heads - n), 2)])
            i = jnp.arange(S)[:, None]
            j = jnp.arange(S)[None, :]
            dist = jnp.sqrt(jnp.maximum(i - j, 0).astype(dtype))
            bias = -jnp.asarray(slopes, dtype)[:, None, None] * dist[None]
            return jnp.where((j <= i)[None], bias, jnp.asarray(-jnp.inf, dtype))
        key = jax.random.key(seed)
        ks = jax.random.split(key, 5)
        B, S, Hd = (2, 256, 256)
        D = Hd // H
        return {'x': jax.random.normal(ks[0], (B, S, Hd), jnp.float32), 'Wq': jax.random.normal(ks[1], (Hd, Hd), jnp.float32) * 0.02, 'Wk': jax.random.normal(ks[2], (G * D, Hd), jnp.float32) * 0.02, 'Wv': jax.random.normal(ks[3], (G * D, Hd), jnp.float32) * 0.02, 'Wo': jax.random.normal(ks[4], (Hd, Hd), jnp.float32) * 0.02}
    _L0_attn_in = _L0_attn_setup()

    def _L0_ffn_setup():
        import jax, jax.numpy as jnp
        import numpy as np
        B, S, DIM = (4, 64, 256)
        E, INTER = (32, 128)
        G, TOPK_G, TOPK = (8, 4, 6)
        ROUTE_SCALE = 2.5
        SHARED_INTER = 2 * INTER

        def _gate(xf, gate_w):
            scores = jax.nn.sigmoid(xf @ gate_w.T)
            gs = scores.reshape(-1, G, E // G)
            group_scores = gs.max(axis=-1)
            _, gidx = jax.lax.top_k(group_scores, TOPK_G)
            gmask = jnp.any(jnp.arange(G)[None, None, :] == gidx[:, :, None], axis=1)
            masked = jnp.where(gmask[:, :, None], gs, -jnp.inf).reshape(-1, E)
            _, idx = jax.lax.top_k(masked, TOPK)
            w = jnp.take_along_axis(scores, idx, axis=1)
            w = w / jnp.sum(w, axis=-1, keepdims=True) * ROUTE_SCALE
            return (w, idx)
        key = jax.random.key(seed)
        ks = jax.random.split(key, 8)
        sd = 0.02
        return {'x': jax.random.normal(ks[0], (B, S, DIM), jnp.float32), 'gate_w': jax.random.normal(ks[1], (E, DIM), jnp.float32) * sd, 'w11': jax.random.normal(ks[2], (E, INTER, DIM), jnp.float32) * sd, 'w33': jax.random.normal(ks[3], (E, INTER, DIM), jnp.float32) * sd, 'w22': jax.random.normal(ks[4], (E, DIM, INTER), jnp.float32) * sd, 'sw1': jax.random.normal(ks[5], (SHARED_INTER, DIM), jnp.float32) * sd, 'sw2': jax.random.normal(ks[6], (DIM, SHARED_INTER), jnp.float32) * sd, 'sw3': jax.random.normal(ks[7], (SHARED_INTER, DIM), jnp.float32) * sd}
    _L0_ffn_in = _L0_ffn_setup()
    _d = {'L0_attn_x': _L0_attn_in['x'], 'L0_attn_Wq': _L0_attn_in['Wq'], 'L0_attn_Wk': _L0_attn_in['Wk'], 'L0_attn_Wv': _L0_attn_in['Wv'], 'L0_attn_Wo': _L0_attn_in['Wo'], 'L0_ffn_gate_w': _L0_ffn_in['gate_w'], 'L0_ffn_w11': _L0_ffn_in['w11'], 'L0_ffn_w33': _L0_ffn_in['w33'], 'L0_ffn_w22': _L0_ffn_in['w22'], 'L0_ffn_sw1': _L0_ffn_in['sw1'], 'L0_ffn_sw2': _L0_ffn_in['sw2'], 'L0_ffn_sw3': _L0_ffn_in['sw3']}
    _x0 = _d['L0_attn_x']
    _d['L0_attn_x'] = jax.random.normal(jax.random.fold_in(jax.random.key(seed), 1), (8, 256, 256), dtype=_x0.dtype)
    del _x0
    return _d

def reference(L0_attn_x, L0_attn_Wq, L0_attn_Wk, L0_attn_Wv, L0_attn_Wo, L0_ffn_gate_w, L0_ffn_w11, L0_ffn_w33, L0_ffn_w22, L0_ffn_sw1, L0_ffn_sw2, L0_ffn_sw3):

    def _L0_attn_ref(x, Wq, Wk, Wv, Wo):
        import math
        import jax, jax.numpy as jnp
        import numpy as np
        H, G = (16, 4)

        def alibi_bias(S, n_heads, dtype):
            n = 2 ** int(math.floor(math.log2(n_heads)))
            m0 = 2.0 ** (-8.0 / n)
            slopes = m0 ** np.arange(1, n + 1)
            if n < n_heads:
                m1 = 2.0 ** (-4.0 / n)
                slopes = np.concatenate([slopes, m1 ** np.arange(1, 1 + 2 * (n_heads - n), 2)])
            i = jnp.arange(S)[:, None]
            j = jnp.arange(S)[None, :]
            dist = jnp.sqrt(jnp.maximum(i - j, 0).astype(dtype))
            bias = -jnp.asarray(slopes, dtype)[:, None, None] * dist[None]
            return jnp.where((j <= i)[None], bias, jnp.asarray(-jnp.inf, dtype))
        B, S, Hd = x.shape
        D = Hd // H
        rep = H // G
        q = (x @ Wq.T).reshape(B, S, G, rep, D)
        k = (x @ Wk.T).reshape(B, S, G, D)
        v = (x @ Wv.T).reshape(B, S, G, D)
        scale = 1.0 / math.sqrt(D)
        bias = alibi_bias(S, H, x.dtype).reshape(G, rep, S, S)
        scores = jnp.einsum('bqgrd,bkgd->bgrqk', q, k) * scale + bias
        attn = jax.nn.softmax(scores, axis=-1)
        o = jnp.einsum('bgrqk,bkgd->bqgrd', attn, v).reshape(B, S, Hd)
        return o @ Wo.T

    def _L0_ffn_ref(x, gate_w, w11, w33, w22, sw1, sw2, sw3):
        import jax, jax.numpy as jnp
        import numpy as np
        B, S, DIM = (4, 64, 256)
        E, INTER = (32, 128)
        G, TOPK_G, TOPK = (8, 4, 6)
        ROUTE_SCALE = 2.5
        SHARED_INTER = 2 * INTER

        def _gate(xf, gate_w):
            scores = jax.nn.sigmoid(xf @ gate_w.T)
            gs = scores.reshape(-1, G, E // G)
            group_scores = gs.max(axis=-1)
            _, gidx = jax.lax.top_k(group_scores, TOPK_G)
            gmask = jnp.any(jnp.arange(G)[None, None, :] == gidx[:, :, None], axis=1)
            masked = jnp.where(gmask[:, :, None], gs, -jnp.inf).reshape(-1, E)
            _, idx = jax.lax.top_k(masked, TOPK)
            w = jnp.take_along_axis(scores, idx, axis=1)
            w = w / jnp.sum(w, axis=-1, keepdims=True) * ROUTE_SCALE
            return (w, idx)
        xf = x.reshape(-1, DIM)
        T = xf.shape[0]
        w, idx = _gate(xf, gate_w)
        c = jnp.zeros((T, E), xf.dtype).at[jnp.arange(T)[:, None], idx].add(w)
        g = jnp.einsum('td,eid->tei', xf, w11)
        u = jnp.einsum('td,eid->tei', xf, w33)
        act = jax.nn.silu(g) * u
        y = jnp.einsum('tei,te,edi->td', act, c, w22)
        shared = jax.nn.silu(xf @ sw1.T) * (xf @ sw3.T) @ sw2.T
        return (y + shared).reshape(x.shape)
    x = L0_attn_x
    x = _layernorm(x + _L0_attn_ref(x, L0_attn_Wq, L0_attn_Wk, L0_attn_Wv, L0_attn_Wo), axis=-1)
    x = _layernorm(x + _L0_ffn_ref(x, L0_ffn_gate_w, L0_ffn_w11, L0_ffn_w33, L0_ffn_w22, L0_ffn_sw1, L0_ffn_sw2, L0_ffn_sw3), axis=-1)
    return x

_drawn_inputs = setup_inputs


def setup_inputs(seed=0):
    import zlib

    import numpy as np

    out = dict(_drawn_inputs(seed))
    spreads = {}
    factors = {'L0_attn_Wq': 8.0,
     'L0_attn_Wk': 8.0,
     'L0_attn_Wv': 3.035,
     'L0_attn_Wo': 3.036,
     'L0_ffn_gate_w': 5.151,
     'L0_ffn_w11': 4.68,
     'L0_ffn_w33': 4.624,
     'L0_ffn_w22': 4.637,
     'L0_ffn_sw1': 3.393,
     'L0_ffn_sw2': 3.38,
     'L0_ffn_sw3': 3.367}
    for name, (base, spread) in spreads.items():
        noise = np.random.default_rng([zlib.crc32(name.encode()), seed]).standard_normal(out[name].shape)
        drawn = base * np.exp(spread * noise) if base else spread * noise
        out[name] = jnp.asarray(drawn.astype(out[name].dtype))
    for name, factor in factors.items():
        out[name] = (out[name] * factor).astype(out[name].dtype)
    return out
```

```python
from contextlib import ExitStack

import concourse.bass as bass
from concourse import mybir

F32 = mybir.dt.float32
F32R = mybir.dt.float32r
BF16 = mybir.dt.bfloat16
I32 = mybir.dt.int32
U32 = mybir.dt.uint32
ALU = mybir.AluOpType
ACT = mybir.ActivationFunctionType
AX = mybir.AxisListType

P = 128
BATCH, SEQ, DIM = 8, 256, 256
TOKENS = BATCH * SEQ
TILES = TOKENS // P
KC = DIM // P
HEADS, GROUPS, HD = 16, 4, 16
REP = HEADS // GROUPS
PAIRS = HEADS // 2
QSCALE = 0.25
EXPERTS, INTER = 32, 128
RGROUPS, TOPG, TOPK = 8, 4, 6
ROUTE_SCALE = 2.5
EPS = 1e-5
ROW = DIM + 2
REGION = TOKENS + P
SLOTS = TOKENS * TOPK // P + EXPERTS
NO_ROW = 1 << 20
LN_STEPS = 10
GATE_STEPS = 24
F_STEPS = 9
W_LOADED = 16 * 10
SET_UP = 9
BIG = 3.0e38
UNROLL = 8

C_ID, C_TRI, C_IOTA, C_REG, C_SLOT, C_END = 0, 128, 256, 288, 320, 321


def need(eng, semaphore, value):
    if not isinstance(value, int) or value > 0:
        eng.wait_ge(semaphore, value)


def need_apart(eng, semaphore, value, passed):
    need(eng, semaphore, value)
    if not isinstance(value, int):
        eng.sem_inc(passed, 1)


def build(nc, xT, x, wq, wk, wv, wo, bias, consts, gate_w, w13, w2, sw1, sw3, sw2, out):
    ctx, early = ExitStack(), ExitStack()
    with ctx:
        def sb(name, shape, dt=F32, where=ctx):
            return where.enter_context(nc.sbuf_tensor(name, shape, dt))

        def sem(name):
            return ctx.enter_context(nc.semaphore(name))

        def dram(name, shape, dt=F32):
            return nc.dram_tensor(name, shape, dt, kind="Internal").ap()

        q_scratch = dram("q_scratch", [HEADS, 2, HD, SEQ])
        k_scratch = dram("k_scratch", [GROUPS, 4, HD, SEQ])
        routed = dram("routed", [EXPERTS * REGION + P, ROW])
        expert_out = dram("expert_out", [TOKENS * TOPK, DIM])

        x_sum = sb("x_sum", [P, TILES, DIM])
        x1T_all = sb("x1T_all", [P, KC, TOKENS])
        cst = sb("cst", [P, C_END])
        ident = cst[:, C_ID:C_ID + P]
        iota = cst[:, C_IOTA:C_IOTA + EXPERTS]
        tri = sb("tri", [P, P], BF16)
        ones_b = sb("ones_b", [P, P], BF16)
        ones32 = sb("ones32", [P, 32])
        wo_sb = sb("wo_sb", [P, GROUPS, DIM])
        gw_sb = sb("gw_sb", [P, KC, P])
        sw1_sb = sb("sw1_sb", [P, KC, DIM])
        sw3_sb = sb("sw3_sb", [P, KC, DIM])
        sw2_sb = sb("sw2_sb", [P, KC, DIM])
        attn_T = [sb(f"attn_T{i}", [P, GROUPS, SEQ]) for i in range(2)]
        resid = sb("resid", [P, 2, DIM])
        x1 = [sb(f"x1_{i}", [P, 2, DIM]) for i in range(2)]
        x1T = [sb(f"x1T_{i}", [P, KC, SEQ]) for i in range(2)]
        rows = sb("rows", [P, 2, TOPK, ROW])
        codes = sb("codes", [P, TILES, TOPK], I32)
        empty = sb("empty", [P, ROW])
        bn = sb("bn", [P, 2, 6])
        mv = sb("mv", [P, 2, 2])
        small = sb("small", [P, 8, 2])
        e_neg = sb("e_neg", [P, 2, EXPERTS])
        e_one = sb("e_one", [P, 2, EXPERTS])
        score = sb("score", [P, 2, EXPERTS])
        g_score = sb("g_score", [P, 2, RGROUPS])
        g_top = sb("g_top", [P, 2, 8])
        g_idx = sb("g_idx", [P, 2, 8], U32)
        g_eq = sb("g_eq", [P, 2, RGROUPS, TOPG])
        g_mask = sb("g_mask", [P, 2, RGROUPS])
        g_pen = sb("g_pen", [P, 2, RGROUPS])
        masked = sb("masked", [P, 2, EXPERTS])
        top = sb("top", [P, 2, 8])
        top_idx = sb("top_idx", [P, 2, 8], U32)
        top_sum = sb("top_sum", [P, 2])
        top_inv = sb("top_inv", [P, 2])
        weight = sb("weight", [P, 2, TOPK])
        onehot = sb("onehot", [P, 2, TOPK, EXPERTS])
        picked = sb("picked", [P, 2, TOPK, EXPERTS])
        chosen = sb("chosen", [P, 2, EXPERTS], BF16)
        seen = [[sb(f"seen{i}{j}", [P, EXPERTS], BF16) for j in range(2)] for i in range(2)]
        rank = sb("rank", [P, 2, TOPK])
        position = sb("position", [P, 2, TOPK], I32)
        cnt_i = sb("cnt_i", [P, EXPERTS], I32)
        cnt_s = sb("cnt_s", [P, EXPERTS], I32)
        per_e = sb("per_e", [P, EXPERTS])
        upto = sb("upto", [P, EXPERTS])
        one_row = sb("one_row", [P, EXPERTS])
        before = sb("before", [P, EXPERTS])
        used = sb("used", [P, EXPERTS])
        fin = sb("fin", [P, 8])
        tail_at = sb("tail_at", [1, EXPERTS], I32)
        slot_tab = sb("slot_tab", [1, 2, P], I32)

        bias_sb = sb("bias_sb", [P, HEADS, SEQ], F32, early)
        wq_sb = sb("wq_sb", [P, KC, DIM], F32, early)
        wk_sb = sb("wk_sb", [P, KC, GROUPS * HD], F32, early)
        wv_sb = sb("wv_sb", [P, KC, P], F32, early)
        xt = [sb(f"xt{i}", [P, KC, SEQ], F32, early) for i in range(2)]
        xn = [sb(f"xn{i}", [P, 2, DIM], F32, early) for i in range(2)]
        q_hi = sb("q_hi", [P, 2, SEQ], F32R, early)
        q_lo = sb("q_lo", [P, 2, SEQ], F32R, early)
        k_hi = sb("k_hi", [GROUPS * HD, SEQ], F32R, early)
        k_lo = sb("k_lo", [GROUPS * HD, SEQ], F32R, early)
        q_pack = [sb(f"q_pack{i}", [P, PAIRS, SEQ], F32R, early) for i in range(2)]
        k_pack = [sb(f"k_pack{i}", [P, GROUPS, 2, SEQ], F32R, early) for i in range(2)]
        v_sb = [sb(f"v_sb{i}", [P, 2, P], F32, early) for i in range(2)]
        s_neg = [sb(f"s_neg{i}", [P, 2, SEQ], F32, early) for i in range(4)]
        m_neg = sb("m_neg", [P, 4, 2], F32, early)
        probs = [[sb(f"probs{i}{q}", [P, REP, (q + 1) * P], F32, early) for q in range(2)] for i in range(2)]
        pT0 = [sb(f"pT0_{i}", [P, REP, SEQ], F32, early) for i in range(2)]
        pT1 = [sb(f"pT1_{i}", [P, REP, P], F32, early) for i in range(2)]
        l_inv = sb("l_inv", [P, SEQ], F32, early)
        early.close()

        late = ctx
        out_t = out.rearrange("b s d -> (b s) d").rearrange("(t p) d -> t p d", p=P)
        w13_sb = sb("w13_sb", [P, EXPERTS, KC, 2 * INTER], F32, late)
        w2_sb = sb("w2_sb", [P, EXPERTS, DIM], F32, late)
        sh_g = [sb(f"sh_g{m}", [P, 512], F32, late) for m in range(2)]
        sh_a = [sb(f"sh_a{m}", [P, 512], F32, late) for m in range(2)]
        xg = [sb(f"xg{i}", [P, ROW], F32, late) for i in range(UNROLL)]
        xgT = [sb(f"xgT{i}", [P, KC, P], F32, late) for i in range(2)]
        eg = [sb(f"eg{i}", [P, INTER], F32, late) for i in range(2)]
        ea = [sb(f"ea{i}", [P, INTER], F32, late) for i in range(2)]
        eaT = [sb(f"eaT{i}", [P, INTER], F32, late) for i in range(2)]
        rows_y = [x1T_all[:, i, 0:TOPK * DIM] for i in range(2)]
        y_sum = attn_T[1][:, 0, :]
        f_out = [attn_T[0][:, i, :] for i in range(2)]
        ey = [sb(f"ey{i}", [P, DIM], F32, late) for i in range(4)]

        bank = [ctx.enter_context(nc.psum_tensor(f"bank{i}", [P, 512], F32)) for i in range(8)]
        S_BANK, T_BANK, O_BANK, L_BANK, KV_BANK, Q_BANK = bank[0:2], bank[2:4], bank[4], bank[5], bank[6], bank[7]

        w_loaded = sem("w_loaded")
        late_loaded = sem("late_loaded")
        xt_loaded = [sem(f"xt_loaded{i}") for i in range(2)]
        xn_loaded = [sem(f"xn_loaded{i}") for i in range(2)]
        set_up = sem("set_up")
        pool_set_up = sem("pool_set_up")
        dve_passed, pool_passed, sp_passed = sem("dve_passed"), sem("pool_passed"), sem("sp_passed")
        q_projected, q_hi_ready, q_lo_ready = sem("q_projected"), sem("q_hi_ready"), sem("q_lo_ready")
        kv_projected, k_hi_ready, k_lo_ready = sem("kv_projected"), sem("k_hi_ready"), sem("k_lo_ready")
        v_copied = sem("v_copied")
        qk_stored = sem("qk_stored")
        qk_packed = [sem(f"qk_packed{i}") for i in range(2)]
        scores_ready, biased, probs_ready = sem("scores_ready"), sem("biased"), sem("probs_ready")
        pt_ready, pt_copied, pv_done = sem("pt_ready"), sem("pt_copied"), sem("pv_done")
        l_inv_ready, normed, wo_done = sem("l_inv_ready"), sem("normed"), sem("wo_done")
        ln_step, ln_root, x1_ready = sem("ln_step"), sem("ln_root"), sem("x1_ready")
        x1t_ready, x1t_copied, x1t_kept = sem("x1t_ready"), sem("x1t_copied"), sem("x1t_kept")
        logits_ready, gate_exp, gate_step, ranks_ready = (
            sem("logits_ready"), sem("gate_exp"), sem("gate_step"), sem("ranks_ready"))
        picks, first_copied = sem("picks"), sem("first_copied")
        rows_copied, scattered = sem("rows_copied"), sem("scattered")
        counts_ready, fin_step, slots_turned, tails_written = (
            sem("counts_ready"), sem("fin_step"), sem("slots_turned"), sem("tails_written"))
        sh_up, sh_silu, sh_act, sh_down, sh_added = (
            sem("sh_up"), sem("sh_silu"), sem("sh_act"), sem("sh_down"), sem("sh_added"))
        xg_loaded = [sem(f"xg_loaded{i}") for i in range(UNROLL)]
        xg_turned, xg_copied = sem("xg_turned"), sem("xg_copied")
        gu_ready, e_silu, e_act = sem("gu_ready"), sem("e_silu"), sem("e_act")
        ea_turned, ea_copied, e_down, ey_ready = sem("ea_turned"), sem("ea_copied"), sem("e_down"), sem("ey_ready")
        ey_sent = [sem(f"ey_sent{i}") for i in range(4)]
        yc_loaded = [sem(f"yc_loaded{i}") for i in range(2)]
        f_step, f_root, f_done = sem("f_step"), sem("f_root"), sem("f_done")
        out_stored = [sem(f"out_stored{i}") for i in range(2)]

        block = ctx.enter_context(nc.Block())

        def attention_loop(eng, body):
            body(0, 0, 0, post=False, nxt=True)
            with eng.Fori(0, (BATCH - 2) // 2) as i:
                body(2 * i + 1, 1, i, post=True, nxt=True)
                body(2 * i + 2, 0, i + 1, post=True, nxt=True)
            body(BATCH - 1, 1, (BATCH - 1) // 2, post=True, nxt=False)

        def slot_loop(eng, step):
            for s in range(UNROLL):
                step(s, s, 0)
            with eng.Fori(1, SLOTS // UNROLL - 1) as i:
                for k in range(UNROLL):
                    step(UNROLL * i + k, k, i)
            for s in range(SLOTS - UNROLL, SLOTS + 2):
                step(s, s % UNROLL, s // UNROLL)

        @block.sync
        def _(sp):
            sp.dma_start(wq_sb[:], wq).then_inc(w_loaded, 16)
            sp.dma_start(wk_sb[:], wk).then_inc(w_loaded, 16)
            sp.dma_start(wv_sb[:], wv).then_inc(w_loaded, 16)

            def load_xt(b, par):
                need(sp, kv_projected, b - 1)
                sp.dma_start(xt[par][:], xT[:, bass.ds(b * SEQ, SEQ)].rearrange("(c p) t -> p c t", p=P)
                             ).then_inc(xt_loaded[par], 16)

            def load_xn(b, par):
                need(sp, ln_step, LN_STEPS * (b - 2) + 1)
                sp.dma_start(xn[par][:], x[bass.ds(b * SEQ, SEQ), :].rearrange("(t p) d -> p t d", p=P)
                             ).then_inc(xn_loaded[par], 16)

            def pack(b, par, h):
                need_apart(sp, qk_packed[1 - par], 96 * (h + par), sp_passed)
                sp.wait_ge(q_hi_ready, b + 1)
                for m in range(2):
                    sp.dma_start(q_scratch[8 * m:8 * m + 8, 0], q_hi[:, m, :].bitcast(F32)).then_inc(qk_stored, 16)
                sp.wait_ge(q_lo_ready, b + 1)
                for m in range(2):
                    sp.dma_start(q_scratch[8 * m:8 * m + 8, 1], q_lo[:, m, :].bitcast(F32)).then_inc(qk_stored, 16)
                sp.wait_ge(k_hi_ready, b + 1)
                for c in (0, 1):
                    sp.dma_start(k_scratch[:, c], k_hi[:].bitcast(F32)).then_inc(qk_stored, 16)
                sp.wait_ge(k_lo_ready, b + 1)
                for c in (2, 3):
                    sp.dma_start(k_scratch[:, c], k_lo[:].bitcast(F32)).then_inc(qk_stored, 16)
                need_apart(sp, qk_stored, 128 * (b + 1), sp_passed)
                need(sp, scores_ready, 16 * (b - 1))
                src = q_scratch.rearrange("(i a) c d t -> a (c d) i t", a=2)
                for a in range(2):
                    for c1 in range(2):
                        r = 64 * a + 32 * c1
                        sp.dma_start(q_pack[par][r:r + 32].bitcast(F32), src[a]).then_inc(qk_packed[par], 16)
                ksrc = k_scratch.rearrange("g c d t -> (c d) g t")
                sp.wait_ge(set_up, SET_UP)
                for a in range(2):
                    sp.dma_start(k_pack[par][64 * a:64 * a + 64, :, a, :].bitcast(F32), ksrc
                                 ).then_inc(qk_packed[par], 16)

            load_xt(0, 0)
            load_xn(0, 0)
            load_xt(1, 1)
            load_xn(1, 1)
            sp.dma_start(bias_sb[:], bias).then_inc(w_loaded, 16)
            sp.dma_start(cst[:], consts).then_inc(w_loaded, 16)
            sp.dma_start(wo_sb[:], wo).then_inc(w_loaded, 16)
            sp.dma_start(gw_sb[:], gate_w).then_inc(w_loaded, 16)
            sp.dma_start(sw1_sb[:], sw1).then_inc(w_loaded, 16)
            sp.dma_start(sw3_sb[:], sw3).then_inc(w_loaded, 16)
            sp.dma_start(sw2_sb[:], sw2).then_inc(w_loaded, 16)
            pack(0, 0, 0)

            def keep_x1t(b, par):
                sp.wait_ge(x1t_copied, b + 1)
                sp.dma_start(x1T_all[:, :, bass.ds(b * SEQ, SEQ)], x1T[par][:]).then_inc(x1t_kept, 16)

            def body(b, par, h, post, nxt):
                if nxt:
                    if post:
                        load_xt(b + 1, 1 - par)
                    pack(b + 1, 1 - par, h + par)
                if post:
                    keep_x1t(b - 1, 1 - par)
                    if nxt:
                        load_xn(b + 1, 1 - par)

            attention_loop(sp, body)
            sp.wait_ge(ln_step, LN_STEPS * (BATCH - 1) + 1)
            sp.wait_ge(pv_done, 4 * BATCH)
            for c in range(4):
                e = slice(8 * c, 8 * c + 8)
                sp.dma_start(w13_sb[:, e], w13[:, e]).then_inc(late_loaded, 16)
            sp.dma_start(w2_sb[:], w2).then_inc(late_loaded, 16)
            keep_x1t(BATCH - 1, 1)
            sp.wait_ge(fin_step, 2)
            sp.wait_ge(pool_set_up, 4)
            with sp.Fori(0, EXPERTS) as e:
                at = sp.value_load(tail_at[0:1, bass.ds(e, 1)], min_val=0, max_val=EXPERTS * REGION)
                sp.dma_start(routed[bass.ds(at, P), :], empty[:]).then_inc(tails_written, 16)
            sp.dma_start(routed[EXPERTS * REGION:EXPERTS * REGION + P, :], empty[:]).then_inc(tails_written, 16)
            sp.wait_ge(tails_written, 16 * (EXPERTS + 1))
            sp.wait_ge(scattered, 16 * 2 * TOPK * BATCH)
            sp.wait_ge(fin_step, 15)

            def load_slot(s, k, turn):
                at = sp.value_load(slot_tab[0:1, 0, bass.ds(s, 1)], min_val=0, max_val=EXPERTS * REGION)
                if turn is not None:
                    sp.wait_ge(ey_sent[k % 4], 16 * (turn * (UNROLL // 4) + k // 4 - 1))
                sp.dma_start(xg[k][:], routed[bass.ds(at, P), :]).then_inc(xg_loaded[k], 16)

            sp.wait_ge(sh_added, 16)
            for k in range(UNROLL):
                load_slot(k, k, None)
            with sp.Fori(1, SLOTS // UNROLL) as i:
                for k in range(UNROLL):
                    load_slot(UNROLL * i + k, k, i)

            for k in range(4):
                sp.wait_ge(ey_sent[k], 16 * SLOTS // 4)
            y_view = expert_out.rearrange("(t p j) d -> t p (j d)", p=P, j=TOPK)

            def load_y(t, k, again):
                if again:
                    sp.wait_ge(f_step, F_STEPS * (t - 2) + 1)
                sp.dma_start(rows_y[k], y_view[bass.ds(t, 1)].rearrange("a p n -> (a p) n")
                             ).then_inc(yc_loaded[k], 16)

            def store(t, k):
                sp.wait_ge(f_done, t + 1)
                sp.dma_start(out_t[bass.ds(t, 1)].rearrange("a p d -> (a p) d"), f_out[k]
                             ).then_inc(out_stored[k], 16)

            load_y(0, 0, False)
            load_y(1, 1, False)
            with sp.Fori(0, TILES // 2 - 1) as i:
                for k in range(2):
                    store(2 * i + k, k)
                    load_y(2 * i + k + 2, k, True)
            for k in range(2):
                store(TILES - 2 + k, k)
            for k in range(2):
                sp.wait_ge(out_stored[k], 16 * TILES // 2)

        @block.tensor
        def _(pe):
            pe.wait_ge(w_loaded, W_LOADED)

            def project_q(b, par, h):
                pe.wait_ge(xt_loaded[par], 16 * (h + 1))
                need(pe, q_lo_ready, b)
                need(pe, x1t_copied, b - 2)
                for m in range(2):
                    for c in range(KC):
                        last = pe.matmul(Q_BANK[:, SEQ * m:SEQ * m + SEQ], wq_sb[:, c, P * m:P * m + P],
                                         xt[par][:, c, :], start=(c == 0), stop=(c == KC - 1))
                last.then_inc(q_projected, 1)

            def project_kv(b, par):
                need(pe, picks, 2 * (b - 2))
                for c in range(KC):
                    pe.matmul(KV_BANK[0:GROUPS * HD, 0:SEQ], wk_sb[:, c, :], xt[par][:, c, :],
                              start=(c == 0), stop=(c == KC - 1))
                for t in range(2):
                    for c in range(KC):
                        last = pe.matmul(KV_BANK[:, SEQ + P * t:SEQ + P * t + P], xt[par][:, c, P * t:P * t + P],
                                         wv_sb[:, c, :], start=(c == 0), stop=(c == KC - 1))
                last.then_inc(kv_projected, 1)

            def scores(b, par, h, g, u):
                pair, qb = u // 2, u % 2
                unit = 16 * b + 4 * g + u
                if g == 0 and u == 0:
                    pe.wait_ge(qk_packed[par], 96 * (h + 1))
                need(pe, biased, 2 * (unit - 2) + 2)
                n = (qb + 1) * P
                pe.matmul(S_BANK[qb][:, 0:2 * n], q_pack[par][:, 2 * g + pair, P * qb:P * qb + P],
                          k_pack[par][:, g, :, 0:n], start=True, stop=True).then_inc(scores_ready, 1)

            def turn_probs(b, g, j):
                n = 12 * b + 3 * g + j
                pb = T_BANK[(3 * g + j) % 2]
                if j < 2:
                    pe.wait_ge(probs_ready, 32 * b + 8 * g + 4 * j + 4)
                need(pe, pt_copied, n - 1)
                if j < 2:
                    for r in (2 * j, 2 * j + 1):
                        for qb in range(2):
                            at = SEQ * (r % 2) + P * qb
                            last = pe.transpose(pb[:, at:at + P], probs[g % 2][qb][:, r, 0:P], ident)
                else:
                    for r in range(REP):
                        last = pe.transpose(pb[:, P * r:P * r + P], probs[g % 2][1][:, r, P:2 * P], ident)
                last.then_inc(pt_ready, 1)

            def values(b, par, g):
                pe.wait_ge(pt_copied, 12 * b + 3 * g + 3)
                if g == 0:
                    pe.wait_ge(v_copied, b + 1)
                need(pe, normed, 4 * b + g)
                for bank_, lhs in ((O_BANK, v_sb[par]), (L_BANK, None)):
                    for kb, pT in ((0, pT0[g % 2]), (1, pT1[g % 2])):
                        for r in range(REP):
                            w = ones32[:] if lhs is None else lhs[:, kb, 32 * g:32 * g + 32]
                            last = pe.matmul(bank_[32 * r:32 * r + 32, P * kb:SEQ], w, pT[:, r, :],
                                             start=(kb == 0), stop=(kb == 1), skip_group_check=True)
                last.then_inc(pv_done, 1)

            def project_out(b, par):
                pe.wait_ge(normed, 4 * b + 4)
                pe.wait_ge(k_lo_ready, min(b + 3, BATCH) if isinstance(b, int) else b + 3)
                pe.wait_ge(v_copied, min(b + 3, BATCH) if isinstance(b, int) else b + 3)
                for t in range(2):
                    for g in range(GROUPS):
                        last = pe.matmul(KV_BANK[:, DIM * t:DIM * t + DIM], attn_T[par][:, g, P * t:P * t + P],
                                         wo_sb[:, g, :], start=(g == 0), stop=(g == GROUPS - 1))
                last.then_inc(wo_done, 1)

            def turn_x1(b, par):
                pe.wait_ge(x1_ready, 2 * b + 2)
                pe.wait_ge(q_lo_ready, min(b + 3, BATCH) if isinstance(b, int) else b + 3)
                for c in range(KC):
                    for t in range(2):
                        last = pe.transpose(Q_BANK[:, SEQ * c + P * t:SEQ * c + P * t + P],
                                            x1[par][:, t, P * c:P * c + P], ident)
                last.then_inc(x1t_ready, 1)

            def gate(b, par):
                pe.wait_ge(x1t_copied, b + 1)
                pe.wait_ge(ln_step, LN_STEPS * b + 1)
                for t in range(2):
                    for c in range(KC):
                        last = pe.matmul(KV_BANK[:, P * t:P * t + P], x1T[par][:, c, P * t:P * t + P],
                                         gw_sb[:, c, :], start=(c == 0), stop=(c == KC - 1))
                last.then_inc(logits_ready, 1)

            def ranks(b, par):
                pe.wait_ge(gate_step, GATE_STEPS * b + 22)
                for t in range(2):
                    at = KV_BANK[:, SEQ + EXPERTS * t:SEQ + EXPERTS * t + EXPERTS]
                    pe.matmul(at, tri[:], chosen[:, t, :], start=True, stop=False)
                    last = pe.matmul(at, ones_b[:], seen[par][t][:], start=False, stop=True)
                last.then_inc(ranks_ready, 1)

            def body(b, par, h, post, nxt):
                o = 1 - par
                for g in range(GROUPS):
                    for u in range(4):
                        if g < GROUPS - 1:
                            scores(b, par, h, g + 1, u)
                        elif nxt:
                            scores(b + 1, o, h + par, 0, u)
                        if u < 3:
                            turn_probs(b, g, u)
                        if g == 2 and u == 1 and post:
                            turn_x1(b - 1, o)
                    if g == 0:
                        if post:
                            values(b - 1, o, GROUPS - 1)
                        if nxt:
                            project_q(b + 1, o, h + par)
                            project_kv(b + 1, o)
                    if g == 1 and post:
                        project_out(b - 1, o)
                    if g == 2 and post:
                        gate(b - 1, o)
                    if g == 3 and post:
                        ranks(b - 1, o)
                    if g > 0:
                        values(b, par, g - 1)

            project_q(0, 0, 0)
            project_kv(0, 0)
            for u in range(4):
                scores(0, 0, 0, 0, u)
            attention_loop(pe, body)
            last_b = BATCH - 1
            values(last_b, 1, GROUPS - 1)
            project_out(last_b, 1)
            turn_x1(last_b, 1)
            gate(last_b, 1)
            ranks(last_b, 1)

            pe.wait_ge(picks, 2 * BATCH)
            pe.matmul(KV_BANK[:, 0:EXPERTS], ones_b[:], seen[0][0][:], start=True, stop=True).then_inc(counts_ready, 1)

            def shared(tb):
                n = 512
                for m in range(2):
                    need(pe, sh_act, 2 * tb - 1 + m)
                    for w, bk in ((sw1_sb, S_BANK[m]), (sw3_sb, T_BANK[m])):
                        for c in range(KC):
                            last = pe.matmul(bk[:], w[:, c, P * m:P * m + P], x1T_all[:, c, bass.ds(n * tb, n)],
                                             start=(c == 0), stop=(c == KC - 1))
                    last.then_inc(sh_up, 1)
                pe.wait_ge(sh_act, 2 * tb + 2)
                for t in range(4):
                    need(pe, sh_added, 4 * tb + t - 1)
                    for m in range(2):
                        last = pe.matmul((O_BANK, L_BANK)[t % 2][:, 0:DIM], sh_a[m][:, P * t:P * t + P],
                                         sw2_sb[:, m, :], start=(m == 0), stop=(m == 1))
                    last.then_inc(sh_down, 1)

            pe.wait_ge(x1t_kept, 16 * BATCH)
            shared(0)
            with pe.Fori(1, TOKENS // 512) as tb:
                shared(tb)

            pe.wait_ge(fin_step, 14)
            for k in range(2):
                last = pe.transpose(KV_BANK[0:1, P * k:P * k + P], fin[:, 6 + k:7 + k], ident)
            last.then_inc(slots_turned, 1)
            pe.wait_ge(fin_step, 15)
            pe.wait_ge(late_loaded, 16 * 5)
            pe.wait_ge(sh_added, TILES)

            def turn_rows(s, k, turn):
                pe.wait_ge(xg_loaded[k], 16 * (turn + 1))
                need(pe, xg_copied, s - 1)
                bk = (KV_BANK, Q_BANK)[k % 2]
                for c in range(KC):
                    last = pe.transpose(bk[:, P * c:P * c + P], xg[k][:, P * c:P * c + P], ident)
                last.then_inc(xg_turned, 1)

            def gate_up(s, k):
                e = pe.value_load(slot_tab[0:1, 1, bass.ds(s, 1)], min_val=0, max_val=EXPERTS - 1)
                pe.wait_ge(xg_copied, s + 1)
                need(pe, e_act, s - 1)
                for c in range(KC):
                    last = pe.matmul(S_BANK[k % 2][:, 0:2 * INTER], xgT[k % 2][:, c, :],
                                     w13_sb[:, bass.ds(e, 1), c, :].rearrange("p a n -> p (a n)"),
                                     start=(c == 0), stop=(c == KC - 1))
                last.then_inc(gu_ready, 1)
                return e

            def turn_act(s, k):
                pe.wait_ge(e_act, s + 1)
                need(pe, ea_copied, s - 1)
                pe.transpose(T_BANK[k % 2][:, 0:P], ea[k % 2][:], ident).then_inc(ea_turned, 1)

            def down(s, k, e=None):
                e = pe.value_load(slot_tab[0:1, 1, bass.ds(s, 1)], min_val=0, max_val=EXPERTS - 1)
                pe.wait_ge(ea_copied, s + 1)
                need(pe, ey_ready, s - 1)
                pe.matmul((O_BANK, L_BANK)[k % 2][:, 0:DIM], eaT[k % 2][:],
                          w2_sb[:, bass.ds(e, 1), :].rearrange("p a n -> p (a n)"),
                          start=True, stop=True).then_inc(e_down, 1)

            def step(s, k, turn):
                if not isinstance(s, int) or s < SLOTS:
                    gate_up(s, k)
                if not isinstance(s, int) or s + 1 < SLOTS:
                    turn_rows(s + 1, (k + 1) % UNROLL, turn + (k + 1) // UNROLL)
                if not isinstance(s, int) or s >= 2:
                    down(s - 2, (k - 2) % UNROLL)
                if not isinstance(s, int) or 1 <= s <= SLOTS:
                    turn_act(s - 1, (k - 1) % UNROLL)

            turn_rows(0, 0, 0)
            slot_loop(pe, step)

        @block.scalar
        def _(act):
            act.preload_act_table_set("natural_log_exp_and_others")

            def split_q(b):
                act.wait_ge(q_projected, b + 1)
                need(act, qk_stored, 128 * b)
                act.activation(q_hi[:].rearrange("p m t -> p (m t)"), Q_BANK[:], ACT.Copy, scale=QSCALE
                               ).then_inc(q_hi_ready, 1)

            def split_kv(b, par):
                act.wait_ge(kv_projected, b + 1)
                act.activation(k_hi[:], KV_BANK[0:GROUPS * HD, 0:SEQ], ACT.Copy).then_inc(k_hi_ready, 1)
                need(act, pv_done, 4 * (b - 1))
                act.activation(v_sb[par][:].rearrange("p t n -> p (t n)"), KV_BANK[:, SEQ:2 * SEQ], ACT.Copy
                               ).then_inc(v_copied, 1)

            def exps(b, g, u):
                pair, qb = u // 2, u % 2
                unit = 16 * b + 4 * g + u
                n = (qb + 1) * P
                if u == 0:
                    need(act, pt_ready, 3 * (4 * b + g - 1))
                for r in range(2):
                    act.wait_ge(biased, 2 * unit + r + 1)
                    act.activation(probs[g % 2][qb][:, 2 * pair + r, :], s_neg[u][:, r, 0:n], ACT.Exp,
                                   bias=m_neg[:, u, r:r + 1], scale=-1.0).then_inc(probs_ready, 1)

            def copy_pt(b, g, j):
                act.wait_ge(pt_ready, 12 * b + 3 * g + j + 1)
                if j == 0:
                    need(act, pv_done, 4 * b + g - 1)
                if j < 2:
                    dst = pT0[g % 2][:, 2 * j:2 * j + 2, :]
                else:
                    dst = pT1[g % 2][:]
                act.activation(dst.rearrange("p r t -> p (r t)"), T_BANK[(3 * g + j) % 2][:], ACT.Copy
                               ).then_inc(pt_copied, 1)

            def ln_first_root(b):
                act.wait_ge(ln_step, LN_STEPS * b + 6)
                act.activation(small[:, 1, :], small[:, 0, :], ACT.Ln).then_inc(ln_root, 1)
                act.wait_ge(ln_root, 2 * b + 1)
                act.activation(small[:, 2, :], small[:, 1, :], ACT.Exp, scale=-0.5).then_inc(ln_root, 1)

            def copy_x1t(b, par):
                act.wait_ge(x1t_ready, b + 1)
                need(act, x1t_kept, 16 * b)
                act.activation(x1T[par][:].rearrange("p c t -> p (c t)"), Q_BANK[:], ACT.Copy
                               ).then_inc(x1t_copied, 1)

            def gate_exps(b):
                act.wait_ge(logits_ready, b + 1)
                act.activation(e_neg[:], KV_BANK[:, 0:SEQ].rearrange("p (t e) -> p t e", e=P)[:, :, 0:EXPERTS],
                               ACT.Exp, scale=-1.0).then_inc(gate_exp, 1)

            def body(b, par, h, post, nxt):
                o = 1 - par
                for g in range(GROUPS):
                    if g == 2 and post:
                        ln_first_root(b - 1)
                    for u in range(4):
                        if g < GROUPS - 1:
                            exps(b, g + 1, u)
                        elif nxt:
                            exps(b + 1, 0, u)
                        if u < 3:
                            copy_pt(b, g, u)
                        if g == 2 and u == 1 and post:
                            copy_x1t(b - 1, o)
                    if g == 0 and nxt:
                        split_q(b + 1)
                        split_kv(b + 1, o)
                    if g == 2 and post:
                        gate_exps(b - 1)

            split_q(0)
            split_kv(0, 0)
            for u in range(4):
                exps(0, 0, u)
            attention_loop(act, body)
            ln_first_root(BATCH - 1)
            copy_x1t(BATCH - 1, 1)
            gate_exps(BATCH - 1)

            def shared(tb):
                for m in range(2):
                    act.wait_ge(sh_up, 2 * tb + m + 1)
                    need(act, sh_act, 2 * tb + m - 1)
                    act.activation(sh_g[m][:], S_BANK[m][:], ACT.Silu).then_inc(sh_silu, 1)

            shared(0)
            with act.Fori(1, TOKENS // 512) as tb:
                shared(tb)

            def step(s, k, turn):
                loop = not isinstance(s, int)
                if loop or s < SLOTS:
                    act.wait_ge(gu_ready, s + 1)
                    need(act, e_act, s - 1)
                    act.activation(eg[k % 2][:], S_BANK[k % 2][:, 0:INTER], ACT.Silu).then_inc(e_silu, 1)
                if loop or s + 1 < SLOTS:
                    act.wait_ge(xg_turned, s + 2)
                    need(act, gu_ready, s)
                    act.activation(xgT[(k + 1) % 2][:].rearrange("p c t -> p (c t)"),
                                   (KV_BANK, Q_BANK)[(k + 1) % 2][:, 0:DIM], ACT.Copy).then_inc(xg_copied, 1)
                if loop or s >= 2:
                    k2 = (k - 2) % UNROLL
                    act.wait_ge(e_down, s - 1)
                    turn2 = turn if k >= 2 else turn - 1
                    need(act, ey_sent[k2 % 4], 16 * (2 * turn2 + k2 // 4))
                    act.activation(ey[k2 % 4][:], (O_BANK, L_BANK)[k2 % 2][:, 0:DIM], ACT.Copy,
                                   scale=xg[k2][:, DIM + 1:DIM + 2]).then_inc(ey_ready, 1)

            act.wait_ge(xg_turned, 1)
            act.activation(xgT[0][:].rearrange("p c t -> p (c t)"), KV_BANK[:, 0:DIM], ACT.Copy
                           ).then_inc(xg_copied, 1)
            slot_loop(act, step)

            def final_root(t):
                act.wait_ge(f_step, F_STEPS * t + 5)
                act.activation(small[:, 1, 0:1], small[:, 0, 0:1], ACT.Ln).then_inc(f_root, 1)
                act.wait_ge(f_root, 2 * t + 1)
                act.activation(small[:, 2, 0:1], small[:, 1, 0:1], ACT.Exp, scale=-0.5).then_inc(f_root, 1)

            act.preload_act_table_set("natural_log_exp_and_others")
            with act.Fori(0, TILES) as t:
                final_root(t)

        @block.vector
        def _(dve):
            dve.memset(ones32[:], 1.0).then_inc(set_up, 1)
            dve.memset(ones_b[:], 1.0).then_inc(set_up, 1)
            dve.memset(seen[0][0][:], 0.0).then_inc(set_up, 1)
            dve.memset(one_row[:], 1.0).then_inc(set_up, 1)
            for i in range(2):
                dve.memset(k_pack[i][P // 2:P, :, 0, :].bitcast(F32), 0.0).then_inc(set_up, 1)
                dve.memset(k_pack[i][0:P // 2, :, 1, :].bitcast(F32), 0.0).then_inc(set_up, 1)
            dve.wait_ge(w_loaded, W_LOADED)
            dve.tensor_copy(tri[:], cst[:, C_TRI:C_TRI + P]).then_inc(set_up, 1)

            def split_q(b):
                dve.wait_ge(q_hi_ready, b + 1)
                need(dve, qk_stored, 128 * b)
                dve.scalar_tensor_tensor(q_lo[:].rearrange("p m t -> p (m t)"), Q_BANK[:], QSCALE,
                                         q_hi[:].rearrange("p m t -> p (m t)").bitcast(F32),
                                         ALU.mult, ALU.subtract).then_inc(q_lo_ready, 1)

            def split_k(b):
                dve.wait_ge(v_copied, b + 1)
                need(dve, qk_stored, 128 * b)
                dve.tensor_tensor(k_lo[:], KV_BANK[0:GROUPS * HD, 0:SEQ], k_hi[:].bitcast(F32), ALU.subtract
                                  ).then_inc(k_lo_ready, 1)

            def bias_max(b, g, u):
                pair, qb = u // 2, u % 2
                unit = 16 * b + 4 * g + u
                n = (qb + 1) * P
                dve.wait_ge(scores_ready, unit + 1)
                need_apart(dve, probs_ready, 2 * (unit - 4) + 2, dve_passed)
                for r in range(2):
                    dve.tensor_tensor_reduce(
                        out=s_neg[u][:, r, 0:n], in0=S_BANK[qb][:, n * r:n * r + n],
                        in1=bias_sb[:, REP * g + 2 * pair + r, SEQ - n:SEQ], scale=-1.0, scalar=BIG,
                        op0=ALU.add, op1=ALU.min, accum_out=m_neg[:, u, r:r + 1]).then_inc(biased, 1)

            def norm(b, par, g):
                dve.wait_ge(pv_done, 4 * b + g + 1)
                need(dve, normed, 4 * b + g)
                if g == 0:
                    need(dve, wo_done, b - 1)
                dve.reciprocal(l_inv[:], L_BANK[:, 0:SEQ]).then_inc(l_inv_ready, 1)
                dve.wait_ge(l_inv_ready, 4 * b + g + 1)
                dve.tensor_tensor(attn_T[par][:, g, :], O_BANK[:, 0:SEQ], l_inv[:], ALU.mult).then_inc(normed, 1)

            def ln_stats(b, par, h):
                n = LN_STEPS * b
                dve.wait_ge(wo_done, b + 1)
                dve.wait_ge(xn_loaded[par], 16 * (h + 1))
                need(dve, x1_ready, 2 * b)
                dve.tensor_tensor(resid[:].rearrange("p t d -> p (t d)"), KV_BANK[:],
                                  xn[par][:].rearrange("p t d -> p (t d)"), ALU.add).then_inc(ln_step, 1)
                dve.wait_ge(ln_step, n + 1)
                for t in range(2):
                    dve.bn_stats(bn[:, t, :], resid[:, t, :]).then_inc(ln_step, 1)
                need_apart(dve, ln_step, n + 3, dve_passed)
                for t in range(2):
                    dve.bn_aggr(mv[:, t, :], bn[:, t, :]).then_inc(ln_step, 1)
                dve.wait_ge(ln_step, n + 5)
                dve.tensor_scalar(small[:, 0, :], mv[:, :, 1], EPS, None, ALU.add).then_inc(ln_step, 1)

            def polish(semaphore, n, w):
                v, y, a, c, d, r = (small[:, k, 0:w] for k in (0, 2, 3, 4, 5, 6))
                dve.tensor_tensor(a, y, y, ALU.mult).then_inc(semaphore, 1)
                dve.wait_ge(semaphore, n + 1)
                dve.tensor_tensor(c, a, v, ALU.mult).then_inc(semaphore, 1)
                dve.wait_ge(semaphore, n + 2)
                dve.tensor_scalar(d, c, -0.5, 1.5, ALU.mult, ALU.add).then_inc(semaphore, 1)
                dve.wait_ge(semaphore, n + 3)
                dve.tensor_tensor(r, y, d, ALU.mult).then_inc(semaphore, 1)
                dve.wait_ge(semaphore, n + 4)

            def ln_apply(b, par):
                dve.wait_ge(ln_root, 2 * b + 2)
                polish(ln_step, LN_STEPS * b + 6, 2)
                need(dve, x1t_ready, b)
                need(dve, rows_copied, 4 * b)
                for t in range(2):
                    dve.tensor_scalar(x1[par][:, t, :], resid[:, t, :], mv[:, t, 0:1], small[:, 6, t:t + 1],
                                      ALU.subtract, ALU.mult).then_inc(x1_ready, 1)

            def router(b, par, part):
                n = GATE_STEPS * b
                done = [0]

                def op(k, ins):
                    ins.then_inc(gate_step, 1)
                    done[0] = k

                def after(k):
                    need_apart(dve, gate_step, n + k, dve_passed)

                iota8 = iota[:, 0:RGROUPS]
                if part == 0:
                    dve.wait_ge(gate_exp, b + 1)
                    need(dve, gate_step, n)
                    op(1, dve.tensor_scalar(e_one[:], e_neg[:], 1.0, None, ALU.add))
                    after(1)
                    op(2, dve.reciprocal(score[:], e_one[:]))
                    after(2)
                    op(3, dve.tensor_reduce(g_score[:], score[:].rearrange("p t (g e) -> p t g e", g=RGROUPS),
                                            AX.X, ALU.max))
                    after(3)
                    for t in range(2):
                        op(4 + t, dve.max(g_top[:, t, :], g_score[:, t, :]))
                    after(5)
                    for t in range(2):
                        op(6 + t, dve.max_index(g_idx[:, t, :], g_top[:, t, :], g_score[:, t, :]))
                elif part == 1:
                    after(7)
                    shape = [P, 2, RGROUPS, TOPG]
                    op(8, dve.tensor_tensor(g_eq[:], g_idx[:, :, 0:TOPG].unsqueeze(2).to_broadcast(shape),
                                            iota8.unsqueeze(1).unsqueeze(3).to_broadcast(shape), ALU.is_equal))
                    after(8)
                    op(9, dve.tensor_reduce(g_mask[:], g_eq[:], AX.X, ALU.add))
                    after(9)
                    op(10, dve.tensor_scalar(g_pen[:], g_mask[:], 4.0, -4.0, ALU.mult, ALU.add))
                    after(10)
                    shape = [P, 2, RGROUPS, EXPERTS // RGROUPS]
                    op(11, dve.tensor_tensor(masked[:].rearrange("p t (g e) -> p t g e", g=RGROUPS),
                                             score[:].rearrange("p t (g e) -> p t g e", g=RGROUPS),
                                             g_pen[:].unsqueeze(3).to_broadcast(shape), ALU.add))
                    after(11)
                    for t in range(2):
                        op(12 + t, dve.max(top[:, t, :], masked[:, t, :]))
                    after(13)
                    for t in range(2):
                        op(14 + t, dve.max_index(top_idx[:, t, :], top[:, t, :], masked[:, t, :]))
                elif part == 2:
                    after(15)
                    op(16, dve.tensor_reduce(top_sum[:], top[:, :, 0:TOPK], AX.X, ALU.add))
                    after(16)
                    op(17, dve.reciprocal(top_inv[:], top_sum[:]))
                    after(17)
                    need(dve, rows_copied, 4 * b)
                    op(18, dve.scalar_tensor_tensor(weight[:], top[:, :, 0:TOPK], ROUTE_SCALE,
                                                    top_inv[:].unsqueeze(2).to_broadcast([P, 2, TOPK]),
                                                    ALU.mult, ALU.mult))
                    shape = [P, 2, TOPK, EXPERTS]
                    op(19, dve.tensor_tensor(onehot[:], top_idx[:, :, 0:TOPK].unsqueeze(3).to_broadcast(shape),
                                             iota.unsqueeze(1).unsqueeze(1).to_broadcast(shape), ALU.is_equal))
                    after(19)
                    with nc.allow_low_precision(reason="zeros and ones, exact in bfloat16"):
                        op(20, dve.tensor_reduce(chosen[:], onehot[:].rearrange("p t j e -> p t e j"), AX.X, ALU.add))
                    after(20)
                    op(21, dve.tensor_tensor(seen[par][1][:], seen[par][0][:], chosen[:, 0, :], ALU.add))
                    after(21)
                    op(22, dve.tensor_tensor(seen[1 - par][0][:], seen[par][1][:], chosen[:, 1, :], ALU.add))
                else:
                    dve.wait_ge(ranks_ready, b + 1)
                    for t in range(2):
                        ins = dve.tensor_tensor(
                            picked[:, t], onehot[:, t],
                            KV_BANK[:, SEQ + EXPERTS * t:SEQ + EXPERTS * t + EXPERTS].unsqueeze(1)
                            .to_broadcast([P, TOPK, EXPERTS]), ALU.mult)
                        ins.then_inc(picks, 1)
                    dve.wait_ge(picks, 2 * b + 2)
                    op(23, dve.tensor_reduce(rank[:], picked[:], AX.X, ALU.add))
                    after(23)
                    need(dve, scattered, 16 * 2 * TOPK * b)
                    op(24, dve.scalar_tensor_tensor(position[:], top_idx[:, :, 0:TOPK], float(REGION), rank[:],
                                                    ALU.mult, ALU.add))

            def body(b, par, h, post, nxt):
                o = 1 - par
                for g in range(GROUPS):
                    if g == 2 and post:
                        ln_stats(b - 1, o, h - 1 + par)
                    for u in range(4):
                        if g < GROUPS - 1:
                            bias_max(b, g + 1, u)
                        elif nxt:
                            bias_max(b + 1, 0, u)
                        if g == 2 and u == 0 and post:
                            ln_apply(b - 1, o)
                        if g == 3 and u < 3 and post:
                            router(b - 1, o, u)
                    if g == 0:
                        if post:
                            norm(b - 1, o, GROUPS - 1)
                        if nxt:
                            split_q(b + 1)
                            split_k(b + 1)
                    if g > 0:
                        norm(b, par, g - 1)
                    if g == 3 and post:
                        router(b - 1, o, 3)

            split_q(0)
            split_k(0)
            for u in range(4):
                bias_max(0, 0, u)
            attention_loop(dve, body)
            b = BATCH - 1
            norm(b, 1, GROUPS - 1)
            ln_stats(b, 1, b // 2)
            ln_apply(b, 1)
            for part in range(4):
                router(b, 1, part)

            cnt = KV_BANK[:, 0:EXPERTS]
            col = [fin[:, k:k + 1] for k in range(8)]
            slot = cst[:, C_SLOT:C_SLOT + 1]
            dve.wait_ge(counts_ready, 1)
            steps = [
                lambda: dve.tensor_scalar(cnt_i[:], cnt, float(P - 1), None, ALU.add),
                lambda: dve.tensor_tensor(tail_at[:], KV_BANK[0:1, 0:EXPERTS], cst[0:1, C_REG:C_REG + EXPERTS], ALU.add),
                lambda: dve.tensor_scalar(cnt_s[:], cnt_i[:], 7, None, ALU.arith_shift_right),
                lambda: dve.tensor_copy(per_e[:], cnt_s[:]),
                lambda: dve.tensor_tensor_scan(upto[:], one_row[:], per_e[:], 0.0, ALU.mult, ALU.add),
                lambda: dve.tensor_scalar(used[:], upto[:], slot, None, ALU.is_le),
                lambda: dve.tensor_reduce(col[0], used[:], AX.X, ALU.add),
                lambda: dve.tensor_tensor(before[:], used[:], per_e[:], ALU.mult),
                lambda: dve.tensor_reduce(col[1], before[:], AX.X, ALU.add),
                lambda: dve.tensor_tensor(col[2], slot, col[1], ALU.subtract),
                lambda: dve.tensor_scalar(col[3], col[2], float(P), None, ALU.mult),
                lambda: dve.scalar_tensor_tensor(col[4], col[0], float(REGION), col[3], ALU.mult, ALU.add),
                lambda: dve.tensor_scalar(col[6], col[4], float(EXPERTS * REGION), None, ALU.min),
                lambda: dve.tensor_scalar(col[7], col[0], float(EXPERTS - 1), None, ALU.min),
            ]
            for k, f in enumerate(steps):
                need(dve, fin_step, k)
                f().then_inc(fin_step, 1)

            def shared(tb):
                for m in range(2):
                    dve.wait_ge(sh_silu, 2 * tb + m + 1)
                    need(dve, sh_down, 4 * tb)
                    dve.tensor_tensor(sh_a[m][:], T_BANK[m][:], sh_g[m][:], ALU.mult).then_inc(sh_act, 1)
                for t in range(4):
                    tile = x_sum[:, bass.ds(4 * tb + t, 1), :].rearrange("p a d -> p (a d)")
                    dve.wait_ge(sh_down, 4 * tb + t + 1)
                    dve.tensor_tensor(tile, (O_BANK, L_BANK)[t % 2][:, 0:DIM], tile, ALU.add).then_inc(sh_added, 1)

            dve.wait_ge(rows_copied, 4 * BATCH)
            shared(0)
            with dve.Fori(1, TOKENS // 512) as tb:
                shared(tb)
            dve.wait_ge(slots_turned, 1)
            dve.tensor_copy(slot_tab[0:1].rearrange("a k s -> a (k s)"), KV_BANK[0:1, 0:2 * P]).then_inc(fin_step, 1)

            def step(s, k, turn):
                loop = not isinstance(s, int)
                if loop or s < SLOTS:
                    dve.wait_ge(e_silu, s + 1)
                    need(dve, ea_turned, s - 1)
                    dve.tensor_tensor(ea[k % 2][:], S_BANK[k % 2][:, INTER:2 * INTER], eg[k % 2][:], ALU.mult
                                      ).then_inc(e_act, 1)
                if loop or 1 <= s <= SLOTS:
                    k1 = (k - 1) % 2
                    dve.wait_ge(ea_turned, s)
                    need(dve, e_down, s - 2)
                    dve.tensor_copy(eaT[k1][:], T_BANK[k1][:, 0:P]).then_inc(ea_copied, 1)

            slot_loop(dve, step)

            def final(t, k, h):
                n = F_STEPS * t
                dve.wait_ge(yc_loaded[k], 16 * (h + 1))
                need(dve, f_done, t)
                need(dve, f_step, n)
                dve.tensor_reduce(y_sum, rows_y[k].rearrange("p (j d) -> p d j", j=TOPK), AX.X, ALU.add
                                  ).then_inc(f_step, 1)
                dve.wait_ge(f_step, n + 1)
                dve.tensor_tensor(resid[:, 0, :], y_sum, x_sum[:, bass.ds(t, 1), :].rearrange("p a d -> p (a d)"),
                                  ALU.add).then_inc(f_step, 1)
                dve.wait_ge(f_step, n + 2)
                dve.bn_stats(bn[:, 0, :], resid[:, 0, :]).then_inc(f_step, 1)
                need_apart(dve, f_step, n + 3, dve_passed)
                dve.bn_aggr(mv[:, 0, :], bn[:, 0, :]).then_inc(f_step, 1)
                dve.wait_ge(f_step, n + 4)
                dve.tensor_scalar(small[:, 0, 0:1], mv[:, 0, 1:2], EPS, None, ALU.add).then_inc(f_step, 1)
                dve.wait_ge(f_root, 2 * t + 2)
                polish(f_step, n + 5, 1)
                need(dve, out_stored[k], 16 * h)
                dve.tensor_scalar(f_out[k], resid[:, 0, :], mv[:, 0, 0:1], small[:, 6, 0:1],
                                  ALU.subtract, ALU.mult).then_inc(f_done, 1)

            final(0, 0, 0)
            final(1, 1, 0)
            with dve.Fori(1, TILES // 2) as h:
                for k in range(2):
                    final(2 * h + k, k, h)

        @block.gpsimd
        def _(pool):
            pool.memset(empty[:, 0:DIM], 0.0).then_inc(pool_set_up, 1)
            pool.memset(empty[:, DIM:DIM + 1].bitcast(I32), NO_ROW).then_inc(pool_set_up, 1)
            pool.memset(empty[:, DIM + 1:ROW], 0.0).then_inc(pool_set_up, 1)
            pool.iota(codes[:], [[P * TOPK, TILES], [1, TOPK]], base=0, channel_multiplier=TOPK
                      ).then_inc(pool_set_up, 1)

            def dispatch(b, par):
                need_apart(pool, x1_ready, 2 * b + 2, pool_passed)
                need_apart(pool, scattered, 16 * 2 * TOPK * b, pool_passed)
                pool.tensor_copy(x_sum[:, bass.ds(2 * b, 2), :], x1[par][:]).then_inc(rows_copied, 1)
                for t in range(2):
                    ins = pool.tensor_copy(rows[:, t, :, 0:DIM],
                                           x1[par][:, t, :].unsqueeze(1).to_broadcast([P, TOPK, DIM]))
                    if t == 1:
                        ins.then_inc(rows_copied, 1)
                    else:
                        ins.then_inc(first_copied, 1)
                pool.tensor_copy(rows[:, :, :, DIM:DIM + 1].bitcast(I32),
                                 codes[:, bass.ds(2 * b, 2), :].unsqueeze(3)).then_inc(rows_copied, 1)
                need_apart(pool, gate_step, GATE_STEPS * b + 18, pool_passed)
                pool.tensor_copy(rows[:, :, :, DIM + 1:ROW], weight[:].unsqueeze(3)).then_inc(rows_copied, 1)
                need_apart(pool, gate_step, GATE_STEPS * b + GATE_STEPS, pool_passed)
                need_apart(pool, rows_copied, 4 * b + 4, pool_passed)
                need_apart(pool, first_copied, b + 1, pool_passed)
                for t in range(2):
                    for j in range(TOPK):
                        pool.indirect_dma_start(
                            routed, bass.IndirectOffsetOnAxis(ap=position[:, t, j:j + 1], axis=0),
                            rows[:, t, j, :], None).then_inc(scattered, 16)

            pool.wait_ge(pool_set_up, 4)
            dispatch(0, 0)
            with pool.Fori(0, (BATCH - 2) // 2) as i:
                dispatch(2 * i + 1, 1)
                dispatch(2 * i + 2, 0)
            dispatch(BATCH - 1, 1)

            def send(s, k):
                need_apart(pool, ey_ready, s + 1, pool_passed)
                pool.indirect_dma_start(
                    expert_out, bass.IndirectOffsetOnAxis(ap=xg[k][:, DIM:DIM + 1].bitcast(I32), axis=0),
                    ey[k % 4][:], None, bounds_check=TOKENS * TOPK - 1, oob_is_err=False
                ).then_inc(ey_sent[k % 4], 16)

            with pool.Fori(0, SLOTS // UNROLL) as i:
                for k in range(UNROLL):
                    send(UNROLL * i + k, k)


_OUT = (BATCH, SEQ, DIM)


def _constants():
    import numpy as np

    c = np.zeros((P, C_END), np.float32)
    c[:, C_ID:C_ID + P] = np.eye(P)
    c[:, C_TRI:C_TRI + P] = np.triu(np.ones((P, P)), 1)
    c[:, C_IOTA:C_IOTA + EXPERTS] = np.arange(EXPERTS)
    c[:, C_REG:C_REG + EXPERTS] = np.arange(EXPERTS) * REGION
    c[:, C_SLOT] = np.arange(P)
    slopes = ((2.0 ** (-8.0 / HEADS)) ** np.arange(1, HEADS + 1)).astype(np.float32)
    dist = (P + np.arange(P))[:, None] - np.arange(SEQ)[None, :]
    root = np.sqrt(np.maximum(dist, 0).astype(np.float32))
    bias = -slopes[None, :, None] * root[:, None, :]
    return c, np.where(dist[:, None, :] >= 0, bias, np.float32(-1e30)).astype(np.float32)


def kernel(L0_attn_x, L0_attn_Wq, L0_attn_Wk, L0_attn_Wv, L0_attn_Wo, L0_ffn_gate_w,
           L0_ffn_w11, L0_ffn_w33, L0_ffn_w22, L0_ffn_sw1, L0_ffn_sw2, L0_ffn_sw3):
    import numpy as np
    import concourse.bacc as bacc
    from concourse.bass_utils import run_bass_kernel_spmd

    def chunks(w, pad=0):
        t = np.asarray(w).T
        t = np.concatenate([t, np.zeros((t.shape[0], pad), t.dtype)], 1) if pad else t
        return np.ascontiguousarray(t.reshape(-1, P, t.shape[1]).transpose(1, 0, 2))

    x = np.asarray(L0_attn_x).reshape(TOKENS, DIM)
    wv = np.zeros((GROUPS, 32, DIM), x.dtype)
    wv[:, :HD] = np.asarray(L0_attn_Wv).reshape(GROUPS, HD, DIM)
    wo = np.zeros((GROUPS, REP, 32, DIM), x.dtype)
    wo[:, :, :HD] = np.asarray(L0_attn_Wo).T.reshape(GROUPS, REP, HD, DIM)
    w13 = np.stack([np.asarray(L0_ffn_w11), np.asarray(L0_ffn_w33)], 1).reshape(EXPERTS, 2 * INTER, KC, P)
    consts, bias = _constants()
    arrays = {
        "xT": np.ascontiguousarray(x.T), "x": x,
        "wq": chunks(L0_attn_Wq), "wk": chunks(L0_attn_Wk), "wv": chunks(wv.reshape(P, DIM)),
        "wo": np.ascontiguousarray(wo.reshape(GROUPS, P, DIM).transpose(1, 0, 2)),
        "bias": bias, "consts": consts, "gate_w": chunks(L0_ffn_gate_w, P - EXPERTS),
        "w13": np.ascontiguousarray(w13.transpose(3, 0, 2, 1)),
        "w2": np.ascontiguousarray(np.asarray(L0_ffn_w22).transpose(2, 0, 1)),
        "sw1": chunks(L0_ffn_sw1), "sw3": chunks(L0_ffn_sw3), "sw2": chunks(L0_ffn_sw2),
    }
    nc = bacc.Bacc("TRN2", target_bir_lowering=False, num_devices=1)
    args = {n: nc.dram_tensor(n, a.shape, mybir.dt.from_np(a.dtype), kind="ExternalInput").ap()
            for n, a in arrays.items()}
    out = nc.dram_tensor("out", _OUT, F32, kind="ExternalOutput").ap()
    build(nc, out=out, **args)
    r = run_bass_kernel_spmd(nc, [arrays], core_ids=[0])
    return r.results[0]["out"]
```

```python
from contextlib import ExitStack

import concourse.bass as bass
from concourse import mybir

F32 = mybir.dt.float32
F32R = mybir.dt.float32r
BF16 = mybir.dt.bfloat16
I32 = mybir.dt.int32
U32 = mybir.dt.uint32
ALU = mybir.AluOpType
ACT = mybir.ActivationFunctionType
AX = mybir.AxisListType

P = 128
BATCH, SEQ, DIM = 8, 256, 256
TOKENS = BATCH * SEQ
TILES = TOKENS // P
KC = DIM // P
HEADS, GROUPS, HD = 16, 4, 16
REP = HEADS // GROUPS
PAIRS = HEADS // 2
QSCALE = 0.25
EXPERTS, INTER = 32, 128
RGROUPS, TOPG, TOPK = 8, 4, 6
ROUTE_SCALE = 2.5
EPS = 1e-5
ROW = DIM + 2
REGION = P + TOKENS
SLOTS = TOKENS * TOPK // P + EXPERTS
PAD_WRITES = 8
W_CHUNKS = 24
W_CHUNK = EXPERTS * 3 * INTER * KC // W_CHUNKS
FIN_STEPS = 17
NO_ROW = 1 << 20
LN_STEPS = 10
GATE_STEPS = 24
F_STATS = 7
V_BLANK = 2
PACKS_BLANK = V_BLANK + 4
SET_UP = PACKS_BLANK + 4
BIG = 3.0e38
UNROLL = 8

C_ID, C_TRI, C_IOTA, C_SLOT, C_END = 0, 128, 256, 288, 289


def need(eng, semaphore, value):
    if not isinstance(value, int) or value > 0:
        eng.wait_ge(semaphore, value)


def need_apart(eng, semaphore, value, passed):
    need(eng, semaphore, value)
    if not isinstance(value, int):
        eng.sem_inc(passed, 1)


class Turn:

    def __init__(self, eng, turn, slot=None):
        keep = (lambda v: v) if isinstance(turn, int) else eng.snap
        self.turn, self.slot = turn, slot
        self.first = isinstance(turn, int) and turn == 0
        self.counts = {-1: turn, 0: keep(turn + 1), 1: keep(turn + 2)}
        self.counts16 = {d: keep(16 * self.counts[d]) for d in (-1, 0, 1)}

    def exists(self, k, ahead):
        at = self.slot if self.slot is not None else (k if self.first else UNROLL + k)
        return 0 <= at + ahead < SLOTS

    def wait(self, eng, semaphores, k, ahead, by=1, again=0):
        at = k + ahead
        d = at // UNROLL + again
        if d < -1:
            raise ValueError("not held in a register")
        need(eng, semaphores[at % UNROLL], (self.counts16 if by == 16 else self.counts)[d])


def build(nc, xT, x, wq, wk, wv, wo, bias, consts, gate_w, expert_weights, sw1, sw3, sw2, out):
    ctx, early = ExitStack(), ExitStack()
    with ctx:
        def sb(name, shape, dt=F32, where=ctx):
            return where.enter_context(nc.sbuf_tensor(name, shape, dt))

        def sem(name):
            return ctx.enter_context(nc.semaphore(name))

        def sems(name):
            return [sem(f"{name}{k}") for k in range(UNROLL)]

        def dram(name, shape, dt=F32):
            return nc.dram_tensor(name, shape, dt, kind="Internal").ap()

        q_scratch = dram("q_scratch", [HEADS, 2, HD, SEQ])
        k_scratch = dram("k_scratch", [GROUPS, 4, HD, SEQ])
        routed = dram("routed", [EXPERTS * REGION + P, ROW])
        expert_out = dram("expert_out", [TOKENS * TOPK, DIM])

        x_sum = sb("x_sum", [P, TILES, DIM])
        x1T_all = sb("x1T_all", [P, KC, TOKENS])
        cst = sb("cst", [P, C_END])
        ident = cst[:, C_ID:C_ID + P]
        iota = cst[:, C_IOTA:C_IOTA + EXPERTS]
        tri = sb("tri", [P, P], BF16)
        ones_b = sb("ones_b", [P, P], BF16)
        wo_sb = sb("wo_sb", [P, KC, DIM])
        gw_sb = sb("gw_sb", [P, KC, EXPERTS])
        sw1_sb = sb("sw1_sb", [P, KC, DIM])
        sw3_sb = sb("sw3_sb", [P, KC, DIM])
        sw2_sb = sb("sw2_sb", [P, KC, DIM])
        attn_T = [sb(f"attn_T{i}", [P, KC, SEQ]) for i in range(2)]
        xn = [sb(f"xn{i}", [P, 2, DIM]) for i in range(2)]
        resid = sb("resid", [P, 2, DIM])
        x1 = [sb(f"x1_{i}", [P, 2, DIM]) for i in range(2)]
        x1T = [sb(f"x1T_{i}", [P, KC, SEQ]) for i in range(2)]
        rows = sb("rows", [P, 2, TOPK, ROW])
        codes = sb("codes", [P, TILES, TOPK], I32)
        empty = sb("empty", [P, ROW])
        sh_g = [sb(f"sh_g{m}", [P, 512]) for m in range(2)]
        sh_a = [sb(f"sh_a{m}", [P, 512]) for m in range(2)]
        bn = sb("bn", [P, 2, 6])
        mv = sb("mv", [P, 2, 2])
        small = sb("small", [P, 8, 2])
        e_neg = sb("e_neg", [P, 2, EXPERTS])
        e_one = sb("e_one", [P, 2, EXPERTS])
        score = sb("score", [P, 2, EXPERTS])
        g_score = sb("g_score", [P, 2, RGROUPS])
        g_top = sb("g_top", [P, 2, 8])
        g_idx = sb("g_idx", [P, 2, 8], U32)
        g_eq = sb("g_eq", [P, 2, RGROUPS, TOPG])
        g_mask = sb("g_mask", [P, 2, RGROUPS])
        g_pen = sb("g_pen", [P, 2, RGROUPS])
        masked = sb("masked", [P, 2, EXPERTS])
        top = sb("top", [P, 2, 8])
        top_idx = sb("top_idx", [P, 2, 8], U32)
        top_sum = sb("top_sum", [P, 2])
        top_inv = sb("top_inv", [P, 2])
        weight = sb("weight", [P, 2, TOPK])
        onehot = sb("onehot", [P, 2, TOPK, EXPERTS])
        picked = sb("picked", [P, 2, TOPK, EXPERTS])
        chosen = sb("chosen", [P, 2, EXPERTS], BF16)
        seen = [[sb(f"seen{i}{j}", [P, EXPERTS], BF16) for j in range(2)] for i in range(2)]
        rank = sb("rank", [P, 2, TOPK])
        position = sb("position", [P, 2, TOPK], I32)
        cnt_i = sb("cnt_i", [P, EXPERTS], I32)
        cnt_s = sb("cnt_s", [P, EXPERTS], I32)
        per_e = sb("per_e", [P, EXPERTS])
        upto = sb("upto", [P, EXPERTS])
        one_row = sb("one_row", [P, EXPERTS])
        before = sb("before", [P, EXPERTS])
        used = sb("used", [P, EXPERTS])
        fin = sb("fin", [P, 8])
        shift = sb("shift", [P, P])
        again = sb("again", [P, SLOTS])
        out_row = sb("out_row", [P, UNROLL], I32)
        rows_of = sb("rows_of", [P, EXPERTS])
        rows_here = sb("rows_here", [P, EXPERTS])
        slot_tab = sb("slot_tab", [1, 2, P], I32)

        bias_sb = sb("bias_sb", [P, HEADS, SEQ], F32, early)
        wq_sb = sb("wq_sb", [P, KC, DIM], F32, early)
        wk_sb = sb("wk_sb", [P, KC, GROUPS * HD], F32, early)
        wv_sb = sb("wv_sb", [P, KC, GROUPS * HD], F32, early)
        xt = [sb(f"xt{i}", [P, KC, SEQ], F32, early) for i in range(2)]
        q_hi = sb("q_hi", [P, 2, SEQ], F32R, early)
        q_lo = sb("q_lo", [P, 2, SEQ], F32R, early)
        k_hi = sb("k_hi", [GROUPS * HD, SEQ], F32R, early)
        k_lo = sb("k_lo", [GROUPS * HD, SEQ], F32R, early)
        q_pack = [sb(f"q_pack{i}", [P, PAIRS, SEQ], F32R, early) for i in range(2)]
        k_pack = [sb(f"k_pack{i}", [P, GROUPS, 2, SEQ], F32R, early) for i in range(2)]
        v_sb = [sb(f"v_sb{i}", [P, 2, GROUPS, 3 * HD], F32, early) for i in range(2)]
        s_neg = [sb(f"s_neg{i}", [P, 2, SEQ], F32, early) for i in range(4)]
        m_neg = sb("m_neg", [P, 4, 2], F32, early)
        probs = [[sb(f"probs{i}{q}", [P, REP, (q + 1) * P], F32, early) for q in range(2)] for i in range(2)]
        pT0 = [sb(f"pT0_{i}", [P, REP, SEQ], F32, early) for i in range(2)]
        pT1 = [sb(f"pT1_{i}", [P, REP, P], F32, early) for i in range(2)]
        row_sum = [sb(f"row_sum{i}", [P, 2, 2, 2 * REP], F32, early) for i in range(2)]
        l_inv = sb("l_inv", [P, 2 * 2 * REP], F32, early)
        l_wide = sb("l_wide", [P, 2, P], F32, early)
        l_rows = sb("l_rows", [P, SEQ], F32, early)
        early.close()

        late = ctx
        out_t = out.rearrange("b s d -> (b s) d").rearrange("(t p) d -> t p d", p=P)
        expert_w = sb("expert_w", [P, TILES * TOPK * DIM], F32, late)
        w13_sb = expert_w[:, 0:EXPERTS * KC * 2 * INTER].rearrange("p (e c n) -> p e c n", e=EXPERTS, c=KC)
        w2_sb = expert_w[:, EXPERTS * KC * 2 * INTER:].rearrange("p (e n) -> p e n", e=EXPERTS)
        xg = [sb(f"xg{i}", [P, ROW], F32, late) for i in range(UNROLL)]
        xgT = [sb(f"xgT{i}", [P, KC, P], F32, late) for i in range(4)]
        eg = [sb(f"eg{i}", [P, INTER], F32, late) for i in range(4)]
        ea = [sb(f"ea{i}", [P, INTER], F32, late) for i in range(2)]
        eaT = [sb(f"eaT{i}", [P, INTER], F32, late) for i in range(2)]
        rows_y = expert_w[:].rearrange("p (t n) -> p t n", t=TILES)
        f_out = [resid, x1[0]]
        f_resid = x1[1][:]
        y_sum = x1T[0][:, 0, :]
        f_bn = sb("f_bn", [P, 2, 2, 6])
        f_mv = sb("f_mv", [P, 2, 2, 2])
        f_small = sb("f_small", [P, 2, 8, 2])
        ey = [rows[:, k // 4, k % 4, 0:DIM] for k in range(UNROLL)]

        bank = [ctx.enter_context(nc.psum_tensor(f"bank{i}", [P, 512], F32)) for i in range(8)]
        S_BANK, T_BANK, O_BANK, G_BANK, KV_BANK, Q_BANK = bank[0:2], bank[2:4], bank[4], bank[5], bank[6], bank[7]

        w_loaded, tables_loaded, late_w_loaded = sem("w_loaded"), sem("tables_loaded"), sem("late_w_loaded")
        late_loaded = [sem(f"late_loaded{i}") for i in range(2)]
        xt_loaded = [sem(f"xt_loaded{i}") for i in range(2)]
        xn_loaded = [sem(f"xn_loaded{i}") for i in range(2)]
        set_up = sem("set_up")
        pool_set_up = sem("pool_set_up")
        passed = sem("passed")
        q_projected, q_hi_ready, q_lo_ready = sem("q_projected"), sem("q_hi_ready"), sem("q_lo_ready")
        kv_projected, k_hi_ready, k_lo_ready = sem("kv_projected"), sem("k_hi_ready"), sem("k_lo_ready")
        v_copied = sem("v_copied")
        qk_stored = sem("qk_stored")
        qk_packed = [sem(f"qk_packed{i}") for i in range(2)]
        l_turned, l_step = sem("l_turned"), sem("l_step")
        scores_ready, biased, probs_ready = sem("scores_ready"), sem("biased"), sem("probs_ready")
        pt_ready, pt_copied, pv_done = sem("pt_ready"), sem("pt_copied"), sem("pv_done")
        l_wide_ready, normed, wo_done = sem("l_wide_ready"), sem("normed"), sem("wo_done")
        ln_step, ln_root, x1_ready = sem("ln_step"), sem("ln_root"), sem("x1_ready")
        x1t_ready, x1t_copied = sem("x1t_ready"), sem("x1t_copied")
        x1t_kept, x1_kept = [sem(f"x1t_kept{i}") for i in range(2)], [sem(f"x1_kept{i}") for i in range(2)]
        logits_ready, gate_exp, gate_step, ranks_ready = (
            sem("logits_ready"), sem("gate_exp"), sem("gate_step"), sem("ranks_ready"))
        picks, rows_copied, codes_copied, scattered = (
            sem("picks"), sem("rows_copied"), sem("codes_copied"), sem("scattered"))
        counts_ready, fin_step, pads_written = sem("counts_ready"), sem("fin_step"), sem("pads_written")
        sh_up, sh_silu, sh_act, sh_down, sh_added = (
            sem("sh_up"), sem("sh_silu"), sem("sh_act"), sem("sh_down"), sem("sh_added"))
        xg_loaded, xg_turned, xg_copied = sems("xg_loaded"), sems("xg_turned"), sems("xg_copied")
        gu_ready, e_silu, e_act = sems("gu_ready"), sems("e_silu"), sems("e_act")
        ea_turned, ea_copied, e_down = sems("ea_turned"), sems("ea_copied"), sems("e_down")
        ey_ready, ey_sent = sems("ey_ready"), sems("ey_sent")
        y_loaded = [sem(f"y_loaded{i}") for i in range(4)]
        f_summed, f_stat, f_root, f_fin, f_done = (
            sem("f_summed"), sem("f_stat"), sem("f_root"), sem("f_fin"), sem("f_done"))
        out_stored = [sem(f"out_stored{i}") for i in range(2)]

        block = ctx.enter_context(nc.Block())

        def attention_loop(eng, body):
            body(0, 0, 0, False, False, True)
            body(1, 1, 0, True, False, True)
            with eng.Fori(1, BATCH // 2 - 1) as h:
                body(2 * h, 0, h, True, True, True)
                body(2 * h + 1, 1, h, True, True, True)
            body(BATCH - 2, 0, BATCH // 2 - 1, True, True, True)
            body(BATCH - 1, 1, BATCH // 2 - 1, True, True, False)

        def slot_loop(eng, step):
            for k in range(UNROLL):
                step(k, Turn(eng, 0))
            with eng.Fori(1, SLOTS // UNROLL - 1) as i:
                turn = Turn(eng, i)
                for k in range(UNROLL):
                    step(k, turn)
            for s in range(SLOTS - UNROLL, SLOTS + 2):
                step(s % UNROLL, Turn(eng, s // UNROLL, s))

        def pair_loop(eng, body):
            body(0, 0, 0)
            with eng.Fori(0, (TILES // 2 - 2) // 2) as i:
                body(2 * i + 1, 1, i)
                body(2 * i + 2, 0, i + 1)
            body(TILES // 2 - 1, 1, TILES // 4 - 1)

        @block.sync
        def _(sp):
            def load_xt(b, par):
                need(sp, kv_projected, b - 1)
                sp.dma_start(xt[par][:], xT[:, bass.ds(b * SEQ, SEQ)].rearrange("(c p) t -> p c t", p=P)
                             ).then_inc(xt_loaded[par], 16)

            def load_xn(b, par):
                need(sp, ln_step, LN_STEPS * (b - 2) + 1)
                sp.dma_start(xn[par][:], x[bass.ds(b * SEQ, SEQ), :].rearrange("(t p) d -> p t d", p=P)
                             ).then_inc(xn_loaded[par], 16)

            def pack(b, par, h):
                need_apart(sp, qk_packed[1 - par], 96 * (h + par), passed)
                sp.wait_ge(q_hi_ready, b + 1)
                for m in range(2):
                    sp.dma_start(q_scratch[8 * m:8 * m + 8, 0], q_hi[:, m, :].bitcast(F32)).then_inc(qk_stored, 16)
                sp.wait_ge(q_lo_ready, b + 1)
                for m in range(2):
                    sp.dma_start(q_scratch[8 * m:8 * m + 8, 1], q_lo[:, m, :].bitcast(F32)).then_inc(qk_stored, 16)
                sp.wait_ge(k_hi_ready, b + 1)
                for c in (0, 1):
                    sp.dma_start(k_scratch[:, c], k_hi[:].bitcast(F32)).then_inc(qk_stored, 16)
                sp.wait_ge(k_lo_ready, b + 1)
                for c in (2, 3):
                    sp.dma_start(k_scratch[:, c], k_lo[:].bitcast(F32)).then_inc(qk_stored, 16)
                need_apart(sp, qk_stored, 128 * (b + 1), passed)
                need(sp, scores_ready, 16 * (b - 1))
                src = q_scratch.rearrange("(i a) c d t -> a (c d) i t", a=2)
                for a in range(2):
                    for c1 in range(2):
                        r = 64 * a + 32 * c1
                        sp.dma_start(q_pack[par][r:r + 32].bitcast(F32), src[a]).then_inc(qk_packed[par], 16)
                ksrc = k_scratch.rearrange("g c d t -> (c d) g t")
                if isinstance(b, int) and b < 2:
                    sp.wait_ge(set_up, PACKS_BLANK)
                for a in range(2):
                    sp.dma_start(k_pack[par][64 * a:64 * a + 64, :, a, :].bitcast(F32), ksrc
                                 ).then_inc(qk_packed[par], 16)

            load_xt(0, 0)
            sp.dma_start(wq_sb[:], wq).then_inc(w_loaded, 16)
            sp.dma_start(wk_sb[:], wk).then_inc(w_loaded, 16)
            sp.dma_start(wv_sb[:], wv).then_inc(w_loaded, 16)
            pack(0, 0, 0)
            load_xt(1, 1)
            load_xn(0, 0)
            load_xn(1, 1)
            sp.dma_start(wo_sb[:], wo).then_inc(late_w_loaded, 16)
            sp.dma_start(gw_sb[:], gate_w).then_inc(late_w_loaded, 16)
            sp.dma_start(sw1_sb[:], sw1).then_inc(late_w_loaded, 16)
            sp.dma_start(sw3_sb[:], sw3).then_inc(late_w_loaded, 16)
            sp.dma_start(sw2_sb[:], sw2).then_inc(late_w_loaded, 16)

            sp.wait_ge(pool_set_up, 4)
            for w in range(PAD_WRITES):
                n = EXPERTS // PAD_WRITES
                pads = routed[REGION * n * w:REGION * n * (w + 1), :].rearrange("(e r) n -> r e n", r=REGION)[0:P]
                sp.dma_start(pads, empty[:].unsqueeze(1).to_broadcast([P, n, ROW])).then_inc(pads_written, 16)
            sp.dma_start(routed[EXPERTS * REGION:EXPERTS * REGION + P, :], empty[:]).then_inc(pads_written, 16)

            def keep_x1(b, par):
                sp.wait_ge(x1_ready, 2 * b + 2)
                sp.dma_start(x_sum[:, bass.ds(2 * b, 2), :], x1[par][:]).then_inc(x1_kept[par], 16)
                sp.wait_ge(x1t_copied, b + 1)
                sp.dma_start(x1T_all[:, :, bass.ds(b * SEQ, SEQ)], x1T[par][:]).then_inc(x1t_kept[par], 16)

            def body(b, par, h, one_behind, two_behind, ahead):
                if ahead:
                    if one_behind:
                        load_xt(b + 1, 1 - par)
                    pack(b + 1, 1 - par, h + par)
                if one_behind:
                    if ahead:
                        load_xn(b + 1, 1 - par)
                    keep_x1(b - 1, 1 - par)

            attention_loop(sp, body)
            sp.wait_ge(normed, 2 * BATCH)
            def load_weights(i, k):
                need(sp, late_loaded[k], 16 * i)
                at = bass.ds(W_CHUNK * (2 * i + k), W_CHUNK)
                sp.dma_start(expert_w[:, at], expert_weights[:, at]).then_inc(late_loaded[k], 16)

            for k in range(2):
                load_weights(0, k)
            with sp.Fori(1, W_CHUNKS // 2) as i:
                for k in range(2):
                    load_weights(i, k)
            keep_x1(BATCH - 1, 1)
            sp.wait_ge(pads_written, 16 * (PAD_WRITES + 1))
            sp.wait_ge(scattered, 16 * 2 * TOPK * BATCH)
            sp.wait_ge(fin_step, FIN_STEPS + 2)

            def load_slot(s, k, turn):
                at = sp.value_load(slot_tab[0:1, 0, bass.ds(s, 1)], min_val=0, max_val=EXPERTS * REGION)
                if turn is not None:
                    sp.wait_ge(ey_sent[k], turn)
                sp.dma_start(xg[k][:], routed[bass.ds(at, P), :]).then_inc(xg_loaded[k], 16)

            sp.wait_ge(sh_added, 16)
            for k in range(UNROLL):
                load_slot(k, k, None)
            with sp.Fori(1, SLOTS // UNROLL) as i:
                sent = sp.snap(16 * i)
                for k in range(UNROLL):
                    load_slot(UNROLL * i + k, k, sent)

            for k in range(UNROLL):
                sp.wait_ge(ey_sent[k], 16 * SLOTS // UNROLL)
            y_view = expert_out.rearrange("(t p j) d -> t p (j d)", p=P, j=TOPK)

            def load_y(p, par, h):
                for t in range(2):
                    need(sp, y_loaded[2 * par + t], 16 * h)
                    sp.dma_start(rows_y[:, bass.ds(2 * p + t, 1), :].rearrange("p a n -> p (a n)"),
                                 y_view[bass.ds(2 * p + t, 1)].rearrange("a p n -> (a p) n")
                                 ).then_inc(y_loaded[2 * par + t], 16)

            for p in range(2):
                load_y(p, p, 0)
            with sp.Fori(1, TILES // 4) as h:
                load_y(2 * h, 0, h)
                load_y(2 * h + 1, 1, h)
            for k in range(2):
                sp.wait_ge(out_stored[k], 16 * TILES // 4)

        @block.tensor
        def _(pe):
            def project_q(b, par, h):
                pe.wait_ge(xt_loaded[par], 16 * (h + 1))
                need(pe, q_lo_ready, b)
                need(pe, x1t_copied, b - 2)
                for m in range(2):
                    for c in range(KC):
                        last = pe.matmul(Q_BANK[:, SEQ * m:SEQ * m + SEQ], wq_sb[:, c, P * m:P * m + P],
                                         xt[par][:, c, :], start=(c == 0), stop=(c == KC - 1))
                last.then_inc(q_projected, 1)

            def project_kv(b, par):
                need(pe, ln_step, LN_STEPS * (b - 3) + 1)
                for c in range(KC):
                    pe.matmul(KV_BANK[0:GROUPS * HD, 0:SEQ], wk_sb[:, c, :], xt[par][:, c, :],
                              start=(c == 0), stop=(c == KC - 1))
                for t in range(2):
                    at = SEQ + GROUPS * HD * t
                    for c in range(KC):
                        last = pe.matmul(KV_BANK[:, at:at + GROUPS * HD], xt[par][:, c, P * t:P * t + P],
                                         wv_sb[:, c, :], start=(c == 0), stop=(c == KC - 1))
                last.then_inc(kv_projected, 1)

            def scores(b, par, h, g, u):
                pair, qb = u // 2, u % 2
                unit = 16 * b + 4 * g + u
                if g == 0 and u == 0:
                    pe.wait_ge(qk_packed[par], 96 * (h + 1))
                need(pe, biased, 2 * (unit - 2) + 2)
                n = (qb + 1) * P
                pe.matmul(S_BANK[qb][:, 0:2 * n], q_pack[par][:, 2 * g + pair, P * qb:P * qb + P],
                          k_pack[par][:, g, :, 0:n], start=True, stop=True).then_inc(scores_ready, 1)

            def turn_probs(b, g, j):
                n = 12 * b + 3 * g + j
                pb = T_BANK[(3 * g + j) % 2]
                if j < 2:
                    pe.wait_ge(probs_ready, 32 * b + 8 * g + 4 * j + 4)
                need(pe, pt_copied, n - 1)
                if j < 2:
                    for r in (2 * j, 2 * j + 1):
                        for qb in range(2):
                            at = SEQ * (r % 2) + P * qb
                            last = pe.transpose(pb[:, at:at + P], probs[g % 2][qb][:, r, 0:P], ident)
                else:
                    for r in range(REP):
                        last = pe.transpose(pb[:, P * r:P * r + P], probs[g % 2][1][:, r, P:2 * P], ident)
                last.then_inc(pt_ready, 1)

            def values(b, par, g):
                pe.wait_ge(pt_copied, 12 * b + 3 * g + 3)
                if g == 0:
                    pe.wait_ge(v_copied, b + 1)
                need(pe, normed, 2 * b + g // 2)
                for kb, pT in ((0, pT0[g % 2]), (1, pT1[g % 2])):
                    for r in (0, 2, 1, 3):
                        at, col = 64 * (g % 2) + 32 * (r // 2), HD * (1 - r % 2)
                        last = pe.matmul(O_BANK[at:at + 32, P * kb:SEQ], v_sb[par][:, kb, g, col:col + 32], pT[:, r, :],
                                         start=(kb == 0 and r % 2 == 0), stop=(kb == 1 and r % 2 == 1),
                                         skip_group_check=True)
                if g % 2 == 0:
                    last.then_inc(pv_done, 1)
                    return
                last.then_inc(pv_done, 1)
                pe.wait_ge(l_wide_ready, 2 * b + g // 2 + 1)
                for qb in range(2):
                    last = pe.transpose(O_BANK[:, SEQ + P * qb:SEQ + P * qb + P], l_wide[:, qb, :], ident)
                last.then_inc(l_turned, 1)

            def project_out(b, par):
                pe.wait_ge(normed, 2 * b + 2)
                if isinstance(b, int) and b == 0:
                    pe.wait_ge(late_w_loaded, 16 * 5)
                pe.wait_ge(k_lo_ready, min(b + 3, BATCH) if isinstance(b, int) else b + 3)
                pe.wait_ge(v_copied, min(b + 3, BATCH) if isinstance(b, int) else b + 3)
                for t in range(2):
                    for c in range(KC):
                        last = pe.matmul(KV_BANK[:, DIM * t:DIM * t + DIM], attn_T[par][:, c, P * t:P * t + P],
                                         wo_sb[:, c, :], start=(c == 0), stop=(c == KC - 1))
                last.then_inc(wo_done, 1)

            def turn_x1(b, par):
                pe.wait_ge(x1_ready, 2 * b + 2)
                pe.wait_ge(q_lo_ready, min(b + 3, BATCH) if isinstance(b, int) else b + 3)
                for c in range(KC):
                    for t in range(2):
                        last = pe.transpose(Q_BANK[:, SEQ * c + P * t:SEQ * c + P * t + P],
                                            x1[par][:, t, P * c:P * c + P], ident)
                last.then_inc(x1t_ready, 1)

            def gate(b, par):
                pe.wait_ge(x1t_copied, b + 1)
                need(pe, picks, 2 * b)
                for t in range(2):
                    for c in range(KC):
                        last = pe.matmul(G_BANK[:, EXPERTS * t:EXPERTS * t + EXPERTS], x1T[par][:, c, P * t:P * t + P],
                                         gw_sb[:, c, :], start=(c == 0), stop=(c == KC - 1))
                last.then_inc(logits_ready, 1)

            def ranks(b, par):
                pe.wait_ge(gate_step, GATE_STEPS * b + 22)
                for t in range(2):
                    at = G_BANK[:, P + EXPERTS * t:P + EXPERTS * t + EXPERTS]
                    pe.matmul(at, tri[:], chosen[:, t, :], start=True, stop=False)
                    last = pe.matmul(at, ones_b[:], seen[par][t][:], start=False, stop=True)
                last.then_inc(ranks_ready, 1)

            def body(b, par, h, one_behind, two_behind, ahead):
                o = 1 - par
                for g in range(GROUPS):
                    for u in range(4):
                        if g < GROUPS - 1:
                            scores(b, par, h, g + 1, u)
                        elif ahead:
                            scores(b + 1, o, h + par, 0, u)
                        if u < 3:
                            turn_probs(b, g, u)
                        if g == 3 and u == 1 and one_behind:
                            turn_x1(b - 1, o)
                    if g > 0:
                        values(b, par, g - 1)
                    if g == 0:
                        if one_behind:
                            values(b - 1, o, GROUPS - 1)
                        if ahead:
                            project_q(b + 1, o, h + par)
                            project_kv(b + 1, o)
                    if g == 1 and one_behind:
                        project_out(b - 1, o)
                    if g == 2 and two_behind:
                        ranks(b - 2, par)
                    if g == 3 and one_behind:
                        gate(b - 1, o)

            pe.wait_ge(w_loaded, 16 * 3)
            project_q(0, 0, 0)
            project_kv(0, 0)
            for u in range(4):
                scores(0, 0, 0, 0, u)
            pe.wait_ge(tables_loaded, 16 * (GROUPS + 1))
            attention_loop(pe, body)

            def shared(tb):
                n = 512
                for i in range(2):
                    pe.wait_ge(x1t_kept[i], 16 * (tb + 1))
                for m in range(2):
                    need(pe, sh_act, 2 * tb - 1 + m)
                    for w, bk in ((sw1_sb, S_BANK[m]), (sw3_sb, T_BANK[m])):
                        for c in range(KC):
                            last = pe.matmul(bk[:], w[:, c, P * m:P * m + P], x1T_all[:, c, n * tb:n * tb + n],
                                             start=(c == 0), stop=(c == KC - 1))
                    last.then_inc(sh_up, 1)
                pe.wait_ge(sh_act, 2 * tb + 2)
                pe.wait_ge(ln_step, LN_STEPS * (BATCH - 1) + 1)
                for t in range(4):
                    need(pe, sh_added, 4 * tb + t - 1)
                    for m in range(2):
                        last = pe.matmul((O_BANK, KV_BANK)[t % 2][:, 0:DIM], sh_a[m][:, P * t:P * t + P],
                                         sw2_sb[:, m, :], start=(m == 0), stop=(m == 1))
                    last.then_inc(sh_down, 1)

            last_b = BATCH - 1
            values(last_b, 1, GROUPS - 1)
            project_out(last_b, 1)
            ranks(last_b - 1, 0)
            shared(0)
            turn_x1(last_b, 1)
            gate(last_b, 1)
            shared(1)
            ranks(last_b, 1)
            pe.wait_ge(picks, 2 * BATCH)
            pe.matmul(G_BANK[:, 0:EXPERTS], ones_b[:], seen[0][0][:], start=True, stop=True).then_inc(counts_ready, 1)
            shared(2)

            pe.wait_ge(fin_step, FIN_STEPS)
            for k in range(2):
                pe.transpose(G_BANK[0:1, SEQ + P * k:SEQ + P * k + P], fin[:, 6 + k:7 + k], ident)
            last = pe.transpose(G_BANK[:, P:2 * P], shift[:], ident)
            last.then_inc(counts_ready, 1)
            shared(3)
            pe.wait_ge(fin_step, FIN_STEPS + 2)
            for k in range(2):
                pe.wait_ge(late_loaded[k], 16 * W_CHUNKS // 2)
            pe.wait_ge(sh_added, TILES)

            def turn_rows(k, turn, ahead):
                at = (k + ahead) % UNROLL
                turn.wait(pe, xg_loaded, k, ahead, 16)
                for c in range(KC):
                    last = pe.transpose((KV_BANK, Q_BANK)[at % 2][:, P * c:P * c + P],
                                        xg[at][:, P * c:P * c + P], ident)
                last.then_inc(xg_turned[at], 1)

            def gate_up(k, turn, e):
                turn.wait(pe, xg_copied, k, 0)
                for c in range(KC):
                    last = pe.matmul(S_BANK[k % 2][:, 0:2 * INTER], xgT[k % 4][:, c, :],
                                     w13_sb[:, bass.ds(e, 1), c, :].rearrange("p a n -> p (a n)"),
                                     start=(c == 0), stop=(c == KC - 1))
                last.then_inc(gu_ready[k], 1)

            def turn_act(k, turn):
                at = (k - 1) % UNROLL
                turn.wait(pe, e_act, k, -1)
                pe.transpose(T_BANK[at % 2][:, 0:P], ea[at % 2][:], ident).then_inc(ea_turned[at], 1)

            def down(k, turn, e):
                at = (k - 2) % UNROLL
                turn.wait(pe, ea_copied, k, -2)
                if not turn.exists(k, 0):
                    turn.wait(pe, ey_ready, k, -4)
                pe.matmul((O_BANK, G_BANK)[at % 2][:, 0:DIM], eaT[at % 2][:],
                          w2_sb[:, bass.ds(e, 1), :].rearrange("p a n -> p (a n)"),
                          start=True, stop=True).then_inc(e_down[at], 1)

            def expert_of(slot):
                return pe.value_load(slot_tab[0:1, 1, bass.ds(slot, 1)], min_val=0, max_val=EXPERTS - 1)

            experts = {}

            def step(k, turn):
                slot = UNROLL * turn.turn + k
                if k == 0 and turn.exists(k, 0):
                    experts.clear()
                if turn.exists(k, 0):
                    experts[k] = expert_of(slot)
                    gate_up(k, turn, experts[k])
                if turn.exists(k, 2):
                    turn_rows(k, turn, 2)
                if turn.exists(k, -2):
                    if k < 2:
                        e = expert_of(slot - 2)
                    else:
                        e = experts[k - 2]
                    down(k, turn, e)
                if turn.exists(k, -1):
                    turn_act(k, turn)

            for k in range(2):
                turn_rows(k, Turn(pe, 0), 0)
            slot_loop(pe, step)

            def final(p, par, h):
                pe.wait_ge(y_loaded[2 * par + 1], 16 * (h + 1))
                need(pe, f_done, 2 * (p - 1))
                tile = x_sum[:, bass.ds(2 * p + 1, 1), :].rearrange("p a d -> p (a d)")
                for j in range(TOPK + 1):
                    src = tile if j == TOPK else rows_y[:, bass.ds(2 * p + 1, 1), DIM * j:DIM * j + DIM
                                                        ].rearrange("p a d -> p (a d)")
                    last = pe.matmul(S_BANK[par][:, 0:DIM], ident, src, start=(j == 0), stop=(j == TOPK))
                last.then_inc(f_summed, 1)

            pair_loop(pe, final)

        @block.scalar
        def _(act):
            act.dma_start(cst[:], consts).then_inc(tables_loaded, 16)
            for g in range(GROUPS):
                heads = slice(REP * g, REP * g + REP)
                act.dma_start(bias_sb[:, heads], bias[:, heads]).then_inc(tables_loaded, 16)
            act.preload_act_table_set("natural_log_exp_and_others")

            def split_q(b):
                act.wait_ge(q_projected, b + 1)
                need(act, qk_stored, 128 * b)
                act.activation(q_hi[:].rearrange("p m t -> p (m t)"), Q_BANK[:], ACT.Copy, scale=QSCALE
                               ).then_inc(q_hi_ready, 1)

            def split_kv(b, par):
                act.wait_ge(kv_projected, b + 1)
                act.activation(k_hi[:], KV_BANK[0:GROUPS * HD, 0:SEQ], ACT.Copy).then_inc(k_hi_ready, 1)
                need(act, pv_done, 4 * (b - 1))
                if isinstance(b, int) and b < 2:
                    act.wait_ge(set_up, V_BLANK)
                act.activation(v_sb[par][:, :, :, HD:2 * HD],
                               KV_BANK[:, SEQ:SEQ + P].rearrange("p (t g d) -> p t g d", t=2, g=GROUPS), ACT.Copy
                               ).then_inc(v_copied, 1)

            def exps(b, b_par, g, u):
                pair, qb = u // 2, u % 2
                unit = 16 * b + 4 * g + u
                n = (qb + 1) * P
                if u == 0:
                    need(act, pt_ready, 3 * (4 * b + g - 1))
                for r in range(2):
                    head = REP * (g % 2) + 2 * pair + r
                    act.wait_ge(biased, 2 * unit + r + 1)
                    act.activation(probs[g % 2][qb][:, 2 * pair + r, :], s_neg[u][:, r, 0:n], ACT.Exp,
                                   bias=m_neg[:, u, r:r + 1], scale=-1.0,
                                   accum_out=row_sum[b_par][:, g // 2, qb, head:head + 1]).then_inc(probs_ready, 1)

            def copy_pt(b, g, j):
                act.wait_ge(pt_ready, 12 * b + 3 * g + j + 1)
                if j == 0:
                    need(act, pv_done, 4 * b + g - 1)
                if j < 2:
                    dst = pT0[g % 2][:, 2 * j:2 * j + 2, :]
                else:
                    dst = pT1[g % 2][:]
                act.activation(dst.rearrange("p r t -> p (r t)"), T_BANK[(3 * g + j) % 2][:], ACT.Copy
                               ).then_inc(pt_copied, 1)

            def ln_first_root(b):
                act.wait_ge(ln_step, LN_STEPS * b + 6)
                act.activation(small[:, 1, :], small[:, 0, :], ACT.Ln).then_inc(ln_root, 1)
                act.wait_ge(ln_root, 2 * b + 1)
                act.activation(small[:, 2, :], small[:, 1, :], ACT.Exp, scale=-0.5).then_inc(ln_root, 1)

            def copy_x1t(b, par, h):
                act.wait_ge(x1t_ready, b + 1)
                need(act, x1t_kept[par], 16 * h)
                act.activation(x1T[par][:].rearrange("p c t -> p (c t)"), Q_BANK[:], ACT.Copy
                               ).then_inc(x1t_copied, 1)

            def gate_exps(b):
                act.wait_ge(logits_ready, b + 1)
                act.activation(e_neg[:].rearrange("p t e -> p (t e)"), G_BANK[:, 0:2 * EXPERTS],
                               ACT.Exp, scale=-1.0).then_inc(gate_exp, 1)

            def copy_x1_rows(b, par, t):
                act.wait_ge(x1_ready, 2 * b + 2)
                need(act, scattered, 16 * 2 * TOPK * b)
                act.activation(rows[:, t, :, 0:DIM], x1[par][:, t, :].unsqueeze(1).to_broadcast([P, TOPK, DIM]),
                               ACT.Copy).then_inc(rows_copied, 1)

            def body(b, par, h, one_behind, two_behind, ahead):
                o = 1 - par
                for g in range(GROUPS):
                    if g == 0 and two_behind:
                        gate_exps(b - 2)
                    for u in range(4):
                        if g < GROUPS - 1:
                            exps(b, par, g + 1, u)
                        elif ahead:
                            exps(b + 1, o, 0, u)
                        if u < 3:
                            copy_pt(b, g, u)
                        if g == 1 and u == 0 and ahead:
                            split_q(b + 1)
                            split_kv(b + 1, o)
                        if g == 2 and u == 2 and one_behind:
                            ln_first_root(b - 1)
                        if g == 3 and u == 1 and one_behind:
                            copy_x1t(b - 1, o, h - 1 + par)
                        if two_behind and (g, u) in ((2, 3), (3, 2)):
                            copy_x1_rows(b - 2, par, g - 2)

            split_q(0)
            split_kv(0, 0)
            for u in range(4):
                exps(0, 0, 0, u)
            attention_loop(act, body)

            def shared(tb):
                for m in range(2):
                    act.wait_ge(sh_up, 2 * tb + m + 1)
                    need(act, sh_act, 2 * tb + m - 1)
                    act.activation(sh_g[m][:], S_BANK[m][:], ACT.Silu).then_inc(sh_silu, 1)

            last_b = BATCH - 1
            gate_exps(last_b - 1)
            ln_first_root(last_b)
            shared(0)
            for t in range(2):
                copy_x1_rows(last_b - 1, 0, t)
            copy_x1t(last_b, 1, last_b // 2)
            gate_exps(last_b)
            shared(1)
            shared(2)
            for t in range(2):
                copy_x1_rows(last_b, 1, t)
            shared(3)

            def copy_rows(k, turn, ahead):
                at = (k + ahead) % UNROLL
                turn.wait(act, xg_turned, k, ahead)
                act.activation(xgT[at % 4][:].rearrange("p c t -> p (c t)"),
                               (KV_BANK, Q_BANK)[at % 2][:, 0:DIM], ACT.Copy).then_inc(xg_copied[at], 1)

            def step(k, turn):
                if k >= UNROLL - 2 and turn.exists(k, 0):
                    turn.wait(act, ey_sent, k, 0, 16, again=-1)
                if turn.exists(k, 0):
                    turn.wait(act, gu_ready, k, 0)
                    act.activation(eg[k % 4][:], S_BANK[k % 2][:, 0:INTER], ACT.Silu).then_inc(e_silu[k], 1)
                if turn.exists(k, -2):
                    at = (k - 2) % UNROLL
                    turn.wait(act, e_down, k, -2)
                    if k >= 2:
                        turn.wait(act, ey_sent, k, -2, 16, again=-1)
                    act.activation(ey[at], (O_BANK, G_BANK)[at % 2][:, 0:DIM], ACT.Copy,
                                   scale=xg[at][:, DIM + 1:DIM + 2]).then_inc(ey_ready[at], 1)
                if turn.exists(k, 2):
                    copy_rows(k, turn, 2)

            for k in range(2):
                copy_rows(k, Turn(act, 0), 0)
            slot_loop(act, step)

            def final_apply(p, par, h):
                act.wait_ge(f_fin, 5 * p + 5)
                need(act, out_stored[par], 16 * h)
                for t, src in enumerate((f_resid[:, par, :], S_BANK[par][:, 0:DIM])):
                    last = act.activation(f_out[par][:, t, :], src, ACT.Identity, scale=f_small[:, par, 6, t:t + 1],
                                          bias=f_small[:, par, 7, t:t + 1])
                    last.then_inc(f_done, 1)
                act.wait_ge(f_done, 2 * p + 2)
                act.dma_start(out_t[bass.ds(2 * p, 2)].rearrange("t p d -> p t d"), f_out[par][:]
                              ).then_inc(out_stored[par], 16)

            def final(p, par, h):
                if not isinstance(p, int) or p > 0:
                    final_apply(p - 1, 1 - par, h - 1 + par)
                act.wait_ge(f_stat, F_STATS * p + F_STATS)
                act.activation(f_small[:, par, 1, :], f_small[:, par, 0, :], ACT.Ln).then_inc(f_root, 1)
                act.wait_ge(f_root, 2 * p + 1)
                act.activation(f_small[:, par, 2, :], f_small[:, par, 1, :], ACT.Exp, scale=-0.5).then_inc(f_root, 1)

            act.preload_act_table_set("natural_log_exp_and_others")
            pair_loop(act, final)
            final_apply(TILES // 2 - 1, 1, TILES // 4 - 1)

        @block.vector
        def _(dve):
            for i in range(2):
                dve.memset(v_sb[i][:], 0.0).then_inc(set_up, 1)
            for i in range(2):
                dve.memset(k_pack[i][P // 2:P, :, 0, :].bitcast(F32), 0.0).then_inc(set_up, 1)
                dve.memset(k_pack[i][0:P // 2, :, 1, :].bitcast(F32), 0.0).then_inc(set_up, 1)
            dve.memset(ones_b[:], 1.0).then_inc(set_up, 1)
            dve.memset(seen[0][0][:], 1.0).then_inc(set_up, 1)
            dve.memset(one_row[:], 1.0).then_inc(set_up, 1)
            dve.wait_ge(tables_loaded, 16 * (GROUPS + 1))
            dve.tensor_copy(tri[:], cst[:, C_TRI:C_TRI + P]).then_inc(set_up, 1)

            def split_q(b):
                dve.wait_ge(q_hi_ready, b + 1)
                need(dve, qk_stored, 128 * b)
                dve.scalar_tensor_tensor(q_lo[:].rearrange("p m t -> p (m t)"), Q_BANK[:], QSCALE,
                                         q_hi[:].rearrange("p m t -> p (m t)").bitcast(F32),
                                         ALU.mult, ALU.subtract).then_inc(q_lo_ready, 1)

            def split_k(b):
                dve.wait_ge(v_copied, b + 1)
                need(dve, qk_stored, 128 * b)
                dve.tensor_tensor(k_lo[:], KV_BANK[0:GROUPS * HD, 0:SEQ], k_hi[:].bitcast(F32), ALU.subtract
                                  ).then_inc(k_lo_ready, 1)

            def bias_max(b, g, u):
                pair, qb = u // 2, u % 2
                unit = 16 * b + 4 * g + u
                n = (qb + 1) * P
                dve.wait_ge(scores_ready, unit + 1)
                need_apart(dve, probs_ready, 2 * (unit - 4) + 2, passed)
                for r in range(2):
                    dve.tensor_tensor_reduce(
                        out=s_neg[u][:, r, 0:n], in0=S_BANK[qb][:, n * r:n * r + n],
                        in1=bias_sb[:, REP * g + 2 * pair + r, SEQ - n:SEQ], scale=-1.0, scalar=BIG,
                        op0=ALU.add, op1=ALU.min, accum_out=m_neg[:, u, r:r + 1]).then_inc(biased, 1)

            def invert(b, par, pp):
                n = 2 * b + pp
                dve.wait_ge(probs_ready, 32 * b + 16 * pp + 16)
                need(dve, l_wide_ready, n)
                dve.reciprocal(l_inv[:], row_sum[par][:, pp].rearrange("p q h -> p (q h)")).then_inc(l_step, 1)
                dve.wait_ge(l_step, 2 * n + 1)
                need(dve, l_turned, n)
                dve.tensor_copy(l_wide[:].rearrange("p q (h d) -> p (q h) d", d=HD),
                                l_inv[:].unsqueeze(2).to_broadcast([P, 4 * REP, HD])).then_inc(l_wide_ready, 1)

            def norm(b, par, pp):
                n = 2 * b + pp
                dve.wait_ge(l_turned, n + 1)
                if pp == 0:
                    need(dve, wo_done, b - 1)
                need(dve, normed, n)
                dve.tensor_copy(l_rows[:], O_BANK[:, SEQ:2 * SEQ]).then_inc(l_step, 1)
                dve.wait_ge(l_step, 2 * n + 2)
                dve.tensor_tensor(attn_T[par][:, pp, :], O_BANK[:, 0:SEQ], l_rows[:], ALU.mult).then_inc(normed, 1)

            def ln_stats(b, par, h):
                n = LN_STEPS * b
                dve.wait_ge(wo_done, b + 1)
                dve.wait_ge(xn_loaded[par], 16 * (h + 1))
                need(dve, x1_ready, 2 * b)
                dve.tensor_tensor(resid[:].rearrange("p t d -> p (t d)"), KV_BANK[:],
                                  xn[par][:].rearrange("p t d -> p (t d)"), ALU.add).then_inc(ln_step, 1)
                dve.wait_ge(ln_step, n + 1)
                for t in range(2):
                    dve.bn_stats(bn[:, t, :], resid[:, t, :]).then_inc(ln_step, 1)
                need_apart(dve, ln_step, n + 3, passed)
                for t in range(2):
                    dve.bn_aggr(mv[:, t, :], bn[:, t, :]).then_inc(ln_step, 1)
                dve.wait_ge(ln_step, n + 5)
                dve.tensor_scalar(small[:, 0, :], mv[:, :, 1], EPS, None, ALU.add).then_inc(ln_step, 1)

            def polish(semaphore, n, cols, w):
                v, y, a, c, d, r = (cols[:, k, 0:w] for k in (0, 2, 3, 4, 5, 6))
                dve.tensor_tensor(a, y, y, ALU.mult).then_inc(semaphore, 1)
                dve.wait_ge(semaphore, n + 1)
                dve.tensor_tensor(c, a, v, ALU.mult).then_inc(semaphore, 1)
                dve.wait_ge(semaphore, n + 2)
                dve.tensor_scalar(d, c, -0.5, 1.5, ALU.mult, ALU.add).then_inc(semaphore, 1)
                dve.wait_ge(semaphore, n + 3)
                dve.tensor_tensor(r, y, d, ALU.mult).then_inc(semaphore, 1)
                dve.wait_ge(semaphore, n + 4)

            def ln_apply(b, par, h):
                dve.wait_ge(ln_root, 2 * b + 2)
                polish(ln_step, LN_STEPS * b + 6, small, 2)
                need(dve, x1t_ready, b - 1)
                need(dve, rows_copied, 2 * (b - 1))
                need(dve, x1_kept[par], 16 * h)
                for t in range(2):
                    dve.tensor_scalar(x1[par][:, t, :], resid[:, t, :], mv[:, t, 0:1], small[:, 6, t:t + 1],
                                      ALU.subtract, ALU.mult).then_inc(x1_ready, 1)

            def router(b, par, part):
                n = GATE_STEPS * b
                done = [0]

                def op(k, ins):
                    ins.then_inc(gate_step, 1)
                    done[0] = k

                def after(k):
                    need_apart(dve, gate_step, n + k, passed)

                iota8 = iota[:, 0:RGROUPS]
                if part == 0:
                    dve.wait_ge(gate_exp, b + 1)
                    need(dve, gate_step, n)
                    op(1, dve.tensor_scalar(e_one[:], e_neg[:], 1.0, None, ALU.add))
                    after(1)
                    op(2, dve.reciprocal(score[:], e_one[:]))
                    after(2)
                    op(3, dve.tensor_reduce(g_score[:], score[:].rearrange("p t (g e) -> p t g e", g=RGROUPS),
                                            AX.X, ALU.max))
                    after(3)
                    for t in range(2):
                        op(4 + t, dve.max(g_top[:, t, :], g_score[:, t, :]))
                    after(5)
                    for t in range(2):
                        op(6 + t, dve.max_index(g_idx[:, t, :], g_top[:, t, :], g_score[:, t, :]))
                elif part == 1:
                    after(7)
                    shape = [P, 2, RGROUPS, TOPG]
                    op(8, dve.tensor_tensor(g_eq[:], g_idx[:, :, 0:TOPG].unsqueeze(2).to_broadcast(shape),
                                            iota8.unsqueeze(1).unsqueeze(3).to_broadcast(shape), ALU.is_equal))
                    after(8)
                    op(9, dve.tensor_reduce(g_mask[:], g_eq[:], AX.X, ALU.add))
                    after(9)
                    op(10, dve.tensor_scalar(g_pen[:], g_mask[:], 4.0, -4.0, ALU.mult, ALU.add))
                    after(10)
                    shape = [P, 2, RGROUPS, EXPERTS // RGROUPS]
                    op(11, dve.tensor_tensor(masked[:].rearrange("p t (g e) -> p t g e", g=RGROUPS),
                                             score[:].rearrange("p t (g e) -> p t g e", g=RGROUPS),
                                             g_pen[:].unsqueeze(3).to_broadcast(shape), ALU.add))
                    after(11)
                    for t in range(2):
                        op(12 + t, dve.max(top[:, t, :], masked[:, t, :]))
                    after(13)
                    for t in range(2):
                        op(14 + t, dve.max_index(top_idx[:, t, :], top[:, t, :], masked[:, t, :]))
                elif part == 2:
                    after(15)
                    op(16, dve.tensor_reduce(top_sum[:], top[:, :, 0:TOPK], AX.X, ALU.add))
                    after(16)
                    op(17, dve.reciprocal(top_inv[:], top_sum[:]))
                    after(17)
                    need(dve, codes_copied, 2 * b)
                    op(18, dve.scalar_tensor_tensor(weight[:], top[:, :, 0:TOPK], ROUTE_SCALE,
                                                    top_inv[:].unsqueeze(2).to_broadcast([P, 2, TOPK]),
                                                    ALU.mult, ALU.mult))
                    shape = [P, 2, TOPK, EXPERTS]
                    op(19, dve.tensor_tensor(onehot[:], top_idx[:, :, 0:TOPK].unsqueeze(3).to_broadcast(shape),
                                             iota.unsqueeze(1).unsqueeze(1).to_broadcast(shape), ALU.is_equal))
                    after(19)
                    with nc.allow_low_precision(reason="zeros and ones, exact in bfloat16"):
                        op(20, dve.tensor_reduce(chosen[:], onehot[:].rearrange("p t j e -> p t e j"), AX.X, ALU.add))
                    after(20)
                    op(21, dve.tensor_tensor(seen[par][1][:], seen[par][0][:], chosen[:, 0, :], ALU.add))
                    after(21)
                    op(22, dve.tensor_tensor(seen[1 - par][0][:], seen[par][1][:], chosen[:, 1, :], ALU.add))
                else:
                    dve.wait_ge(ranks_ready, b + 1)
                    for t in range(2):
                        ins = dve.tensor_tensor(
                            picked[:, t], onehot[:, t],
                            G_BANK[:, P + EXPERTS * t:P + EXPERTS * t + EXPERTS].unsqueeze(1)
                            .to_broadcast([P, TOPK, EXPERTS]), ALU.mult)
                        ins.then_inc(picks, 1)
                    dve.wait_ge(picks, 2 * b + 2)
                    op(23, dve.tensor_reduce(rank[:], picked[:], AX.X, ALU.add))
                    after(23)
                    need(dve, scattered, 16 * 2 * TOPK * b)
                    op(24, dve.scalar_tensor_tensor(position[:], top_idx[:, :, 0:TOPK], float(REGION), rank[:],
                                                    ALU.mult, ALU.add))

            def body(b, par, h, one_behind, two_behind, ahead):
                o = 1 - par
                for g in range(GROUPS):
                    for u in range(4):
                        if g < GROUPS - 1:
                            bias_max(b, g + 1, u)
                        elif ahead:
                            bias_max(b + 1, 0, u)
                        if two_behind:
                            part = {(0, 1): 0, (0, 3): 1, (1, 2): 2, (3, 1): 3}.get((g, u))
                            if part is not None:
                                router(b - 2, par, part)
                        if (g, u) == (1, 0) and one_behind:
                            norm(b - 1, o, 1)
                        if (g, u) == (1, 1) and ahead:
                            split_q(b + 1)
                            split_k(b + 1)
                        if (g, u) == (1, 3):
                            invert(b, par, 0)
                        if one_behind:
                            if (g, u) == (2, 1):
                                ln_stats(b - 1, o, h - 1 + par)
                            if (g, u) == (2, 3):
                                ln_apply(b - 1, o, h - 1 + par)
                        if (g, u) == (3, 0):
                            norm(b, par, 0)
                        if (g, u) == (3, 3):
                            invert(b, par, 1)

            split_q(0)
            split_k(0)
            for u in range(4):
                bias_max(0, 0, u)
            attention_loop(dve, body)

            def shared(tb):
                for m in range(2):
                    dve.wait_ge(sh_silu, 2 * tb + m + 1)
                    need(dve, sh_down, 4 * tb)
                    dve.tensor_tensor(sh_a[m][:], T_BANK[m][:], sh_g[m][:], ALU.mult).then_inc(sh_act, 1)
                for i in range(2):
                    dve.wait_ge(x1_kept[i], 16 * (tb + 1))
                for t in range(4):
                    tile = x_sum[:, 4 * tb + t, :]
                    dve.wait_ge(sh_down, 4 * tb + t + 1)
                    dve.tensor_tensor(tile, (O_BANK, KV_BANK)[t % 2][:, 0:DIM], tile, ALU.add).then_inc(sh_added, 1)

            b = BATCH - 1
            norm(b, 1, 1)
            for part in range(3):
                router(b - 1, 0, part)
            ln_stats(b, 1, b // 2)
            router(b - 1, 0, 3)
            ln_apply(b, 1, b // 2)
            shared(0)
            for part in range(3):
                router(b, 1, part)
            shared(1)
            router(b, 1, 3)

            cnt = G_BANK[:, 0:EXPERTS]
            col = [fin[:, k:k + 1] for k in range(8)]
            slot = cst[:, C_SLOT:C_SLOT + 1]
            dve.wait_ge(counts_ready, 1)
            steps = [
                lambda: dve.tensor_scalar(cnt_i[:], cnt, -1.0, None, ALU.add),
                lambda: dve.tensor_scalar(rows_of[:], cnt, -float(P), None, ALU.add),
                lambda: dve.tensor_scalar(cnt_s[:], cnt_i[:], 7, None, ALU.arith_shift_right),
                lambda: dve.tensor_copy(per_e[:], cnt_s[:]),
                lambda: dve.tensor_tensor_scan(upto[:], one_row[:], per_e[:], 0.0, ALU.mult, ALU.add),
                lambda: dve.tensor_scalar(used[:], upto[:], slot, None, ALU.is_le),
                lambda: dve.tensor_reduce(col[0], used[:], AX.X, ALU.add),
                lambda: dve.tensor_tensor(before[:], used[:], per_e[:], ALU.mult),
                lambda: dve.tensor_reduce(col[1], before[:], AX.X, ALU.add),
                lambda: dve.tensor_tensor(col[2], slot, col[1], ALU.subtract),
                lambda: dve.tensor_scalar(col[3], col[2], float(P), float(P), ALU.mult, ALU.add),
                lambda: dve.scalar_tensor_tensor(rows_here[:], iota, col[0], rows_of[:], ALU.is_equal, ALU.mult),
                lambda: dve.tensor_reduce(col[4], rows_here[:], AX.X, ALU.add),
                lambda: dve.tensor_tensor(col[5], col[3], col[4], ALU.min),
                lambda: dve.scalar_tensor_tensor(col[6], col[0], float(REGION), col[5], ALU.mult, ALU.add),
                lambda: dve.tensor_scalar(col[7], col[0], float(EXPERTS - 1), None, ALU.min),
                lambda: dve.tensor_tensor(shift[:], col[3].to_broadcast([P, P]), col[4].to_broadcast([P, P]),
                                          ALU.subtract),
            ]
            for k, f in enumerate(steps):
                need(dve, fin_step, k)
                f().then_inc(fin_step, 1)

            shared(2)
            dve.wait_ge(counts_ready, 2)
            dve.tensor_copy(slot_tab[0:1].rearrange("a k s -> a (k s)"), G_BANK[0:1, SEQ:2 * SEQ]).then_inc(fin_step, 1)
            dve.tensor_scalar(again[:], G_BANK[:, P:2 * P], slot, float(NO_ROW), ALU.is_gt, ALU.mult
                              ).then_inc(fin_step, 1)
            shared(3)

            def step(k, turn):
                if turn.exists(k, 0):
                    turn.wait(dve, e_silu, k, 0)
                    dve.tensor_tensor(out_row[:, k:k + 1], xg[k][:, DIM:DIM + 1],
                                      again[:, bass.ds(UNROLL * turn.turn + k, 1)], ALU.add)
                    dve.tensor_tensor(ea[k % 2][:], S_BANK[k % 2][:, INTER:2 * INTER], eg[k % 4][:], ALU.mult
                                      ).then_inc(e_act[k], 1)
                if turn.exists(k, -1):
                    at = (k - 1) % UNROLL
                    turn.wait(dve, ea_turned, k, -1)
                    dve.tensor_copy(eaT[at % 2][:], T_BANK[at % 2][:, 0:P]).then_inc(ea_copied[at], 1)

            dve.wait_ge(fin_step, FIN_STEPS + 2)
            slot_loop(dve, step)

            def final_stage2(p, par):
                dve.wait_ge(f_root, 2 * p + 2)
                polish(f_fin, 5 * p, f_small[:, par], 2)
                dve.scalar_tensor_tensor(f_small[:, par, 7, :], f_mv[:, par, :, 0], -1.0, f_small[:, par, 6, :],
                                         ALU.mult, ALU.mult).then_inc(f_fin, 1)

            def final(p, par, h):
                n = F_STATS * p
                tile = x_sum[:, bass.ds(2 * p, 1), :].rearrange("p a d -> p (a d)")
                dve.wait_ge(y_loaded[2 * par], 16 * (h + 1))
                need(dve, f_stat, n)
                dve.tensor_reduce(y_sum, rows_y[:, bass.ds(2 * p, 1), :].rearrange("p a (j d) -> p (a d) j", j=TOPK), AX.X, ALU.add
                                  ).then_inc(f_stat, 1)
                dve.wait_ge(f_stat, n + 1)
                need(dve, f_done, 2 * (p - 1))
                dve.tensor_tensor(f_resid[:, par, :], y_sum, tile, ALU.add).then_inc(f_stat, 1)
                dve.wait_ge(f_stat, n + 2)
                dve.bn_stats(f_bn[:, par, 0, :], f_resid[:, par, :]).then_inc(f_stat, 1)
                if not isinstance(p, int) or p > 0:
                    final_stage2(p - 1, 1 - par)
                dve.wait_ge(f_summed, p + 1)
                dve.bn_stats(f_bn[:, par, 1, :], S_BANK[par][:, 0:DIM]).then_inc(f_stat, 1)
                need_apart(dve, f_stat, n + 4, passed)
                for t in range(2):
                    dve.bn_aggr(f_mv[:, par, t, :], f_bn[:, par, t, :]).then_inc(f_stat, 1)
                dve.wait_ge(f_stat, n + 6)
                dve.tensor_scalar(f_small[:, par, 0, :], f_mv[:, par, :, 1], EPS, None, ALU.add).then_inc(f_stat, 1)

            pair_loop(dve, final)
            final_stage2(TILES // 2 - 1, 1)

        @block.gpsimd
        def _(pool):
            pool.memset(empty[:, 0:DIM], 0.0).then_inc(pool_set_up, 1)
            pool.memset(empty[:, DIM:DIM + 1], float(NO_ROW)).then_inc(pool_set_up, 1)
            pool.memset(empty[:, DIM + 1:ROW], 0.0).then_inc(pool_set_up, 1)
            pool.iota(codes[:], [[P * TOPK, TILES], [1, TOPK]], base=0, channel_multiplier=TOPK
                      ).then_inc(pool_set_up, 1)

            def dispatch(b, par):
                need_apart(pool, scattered, 16 * 2 * TOPK * b, passed)
                pool.tensor_copy(rows[:, :, :, DIM:DIM + 1],
                                 codes[:, bass.ds(2 * b, 2), :].unsqueeze(3)).then_inc(codes_copied, 1)
                need_apart(pool, gate_step, GATE_STEPS * b + 18, passed)
                pool.tensor_copy(rows[:, :, :, DIM + 1:ROW], weight[:].unsqueeze(3)).then_inc(codes_copied, 1)
                need_apart(pool, gate_step, GATE_STEPS * b + GATE_STEPS, passed)
                need_apart(pool, codes_copied, 2 * b + 2, passed)
                need_apart(pool, rows_copied, 2 * b + 2, passed)
                for t in range(2):
                    for j in range(TOPK):
                        pool.indirect_dma_start(
                            routed, bass.IndirectOffsetOnAxis(ap=position[:, t, j:j + 1], axis=0),
                            rows[:, t, j, :], None).then_inc(scattered, 16)

            pool.wait_ge(pool_set_up, 4)
            dispatch(0, 0)
            with pool.Fori(0, (BATCH - 2) // 2) as i:
                dispatch(2 * i + 1, 1)
                dispatch(2 * i + 2, 0)
            dispatch(BATCH - 1, 1)

            def send(k, count):
                need_apart(pool, ey_ready[k], count, passed)
                pool.indirect_dma_start(
                    expert_out, bass.IndirectOffsetOnAxis(ap=out_row[:, k:k + 1], axis=0),
                    ey[k], None, bounds_check=TOKENS * TOPK - 1, oob_is_err=False
                ).then_inc(ey_sent[k], 16)

            with pool.Fori(0, SLOTS // UNROLL) as i:
                count = pool.snap(i + 1)
                for k in range(UNROLL):
                    send(k, count)


_OUT = (BATCH, SEQ, DIM)


def _constants():
    import numpy as np

    c = np.zeros((P, C_END), np.float32)
    c[:, C_ID:C_ID + P] = np.eye(P)
    c[:, C_TRI:C_TRI + P] = np.triu(np.ones((P, P)), 1)
    c[:, C_IOTA:C_IOTA + EXPERTS] = np.arange(EXPERTS)
    c[:, C_SLOT] = np.arange(P)
    slopes = ((2.0 ** (-8.0 / HEADS)) ** np.arange(1, HEADS + 1)).astype(np.float32)
    dist = (P + np.arange(P))[:, None] - np.arange(SEQ)[None, :]
    root = np.sqrt(np.maximum(dist, 0).astype(np.float32))
    bias = -slopes[None, :, None] * root[:, None, :]
    return c, np.where(dist[:, None, :] >= 0, bias, np.float32(-1e30)).astype(np.float32)


def kernel(L0_attn_x, L0_attn_Wq, L0_attn_Wk, L0_attn_Wv, L0_attn_Wo, L0_ffn_gate_w,
           L0_ffn_w11, L0_ffn_w33, L0_ffn_w22, L0_ffn_sw1, L0_ffn_sw2, L0_ffn_sw3):
    import numpy as np
    import concourse.bacc as bacc
    from concourse.bass_utils import run_bass_kernel_spmd

    def chunks(w):
        t = np.asarray(w).T
        return np.ascontiguousarray(t.reshape(-1, P, t.shape[1]).transpose(1, 0, 2))

    x = np.asarray(L0_attn_x).reshape(TOKENS, DIM)
    w13 = np.stack([np.asarray(L0_ffn_w11), np.asarray(L0_ffn_w33)], 1).reshape(EXPERTS, 2 * INTER, KC, P)
    w2 = np.asarray(L0_ffn_w22).transpose(2, 0, 1).reshape(P, -1)
    consts, bias = _constants()
    arrays = {
        "xT": np.ascontiguousarray(x.T), "x": x,
        "wq": chunks(L0_attn_Wq), "wk": chunks(L0_attn_Wk), "wv": chunks(L0_attn_Wv),
        "wo": chunks(L0_attn_Wo),
        "bias": bias, "consts": consts, "gate_w": chunks(L0_ffn_gate_w),
        "expert_weights": np.concatenate([w13.transpose(3, 0, 2, 1).reshape(P, -1), w2], 1),
        "sw1": chunks(L0_ffn_sw1), "sw3": chunks(L0_ffn_sw3), "sw2": chunks(L0_ffn_sw2),
    }
    nc = bacc.Bacc("TRN2", target_bir_lowering=False, num_devices=1)
    args = {n: nc.dram_tensor(n, a.shape, mybir.dt.from_np(a.dtype), kind="ExternalInput").ap()
            for n, a in arrays.items()}
    out = nc.dram_tensor("out", _OUT, F32, kind="ExternalOutput").ap()
    build(nc, out=out, **args)
    r = run_bass_kernel_spmd(nc, [arrays], core_ids=[0])
    return r.results[0]["out"]
```

```python
from contextlib import ExitStack

import concourse.bass as bass
from concourse import mybir

F32 = mybir.dt.float32
F32R = mybir.dt.float32r
BF16 = mybir.dt.bfloat16
I32 = mybir.dt.int32
U32 = mybir.dt.uint32
ALU = mybir.AluOpType
ACT = mybir.ActivationFunctionType
AX = mybir.AxisListType

P = 128
BATCH, SEQ, DIM = 8, 256, 256
TOKENS = BATCH * SEQ
TILES = TOKENS // P
KC = DIM // P
HEADS, GROUPS, HD = 16, 4, 16
REP = HEADS // GROUPS
PAIRS = HEADS // 2
QSCALE = 0.25
EXPERTS, INTER = 32, 128
RGROUPS, TOPG, TOPK = 8, 4, 6
ROUTE_SCALE = 2.5
EPS = 1e-5
ROW = DIM + 2
REGION = P + TOKENS
SLOTS = TOKENS * TOPK // P + EXPERTS
W_CHUNKS = 24
W_CHUNK = EXPERTS * 3 * INTER * KC // W_CHUNKS
FIN_STEPS = 17
NO_ROW = 1 << 20
LN_STEPS = 10
GATE_STEPS = 24
F_STATS = 7
V_BLANK = 2
PACKS_BLANK = V_BLANK + 4
BIG = 3.0e38
VECTOR_COPIES = (0, 2, 3)
UNROLL = 8
PACKED = 4

C_ID, C_TRI, C_IOTA, C_SLOT, C_PACK, C_END = 0, 128, 256, 288, 289, 321


def need(eng, semaphore, value):
    if not isinstance(value, int) or value > 0:
        eng.wait_ge(semaphore, value)


def need_apart(eng, semaphore, value, passed):
    need(eng, semaphore, value)
    if not isinstance(value, int):
        eng.sem_inc(passed, 1)


class Turn:

    def __init__(self, eng, turn, slot=None):
        self.eng, self.turn, self.slot = eng, turn, slot
        self.first = isinstance(turn, int) and turn == 0
        self.counts = {}

    def count(self, ahead, by):
        if (ahead, by) not in self.counts:
            value = by * (self.turn + 1 + ahead)
            self.counts[ahead, by] = value if isinstance(value, int) else self.eng.snap(value)
        return self.counts[ahead, by]

    def exists(self, k, ahead):
        at = self.slot if self.slot is not None else (k if self.first else UNROLL + k)
        return 0 <= at + ahead < SLOTS

    def wait(self, eng, semaphores, k, ahead, by=1, again=0):
        at = k + ahead
        d = at // UNROLL + again
        if d < -1:
            raise ValueError("not held in a register")
        need(eng, semaphores[at % UNROLL], self.count(d, by))


def build(nc, xT, x, wq, wk, wv, wo, bias, consts, gate_w, expert_weights, sw1, sw3, sw2, out):
    ctx, early = ExitStack(), ExitStack()
    with ctx:
        def sb(name, shape, dt=F32, where=ctx):
            return where.enter_context(nc.sbuf_tensor(name, shape, dt))

        def sem(name):
            return ctx.enter_context(nc.semaphore(name))

        def sems(name):
            return [sem(f"{name}{k}") for k in range(UNROLL)]

        def dram(name, shape, dt=F32):
            return nc.dram_tensor(name, shape, dt, kind="Internal").ap()

        q_scratch = dram("q_scratch", [PAIRS, 2, HD, 2 * SEQ])
        k_scratch = dram("k_scratch", [GROUPS, 2, 2 * HD, SEQ])
        routed = dram("routed", [EXPERTS * REGION + P, ROW])
        expert_out = dram("expert_out", [TOKENS * TOPK, DIM])

        x_sum = sb("x_sum", [P, TILES, DIM])
        x1T_all = sb("x1T_all", [P, KC, TOKENS])
        cst = sb("cst", [P, C_END])
        ident = cst[:, C_ID:C_ID + P]
        iota = cst[:, C_IOTA:C_IOTA + EXPERTS]
        tri = sb("tri", [P, P], BF16)
        ones_b = sb("ones_b", [P, P], BF16)
        wo_sb = sb("wo_sb", [P, KC, DIM])
        gw_sb = sb("gw_sb", [P, KC, EXPERTS])
        sw1_sb = sb("sw1_sb", [P, KC, DIM])
        sw3_sb = sb("sw3_sb", [P, KC, DIM])
        sw2_sb = sb("sw2_sb", [P, KC, DIM])
        attn_T = [sb(f"attn_T{i}", [P, KC, SEQ]) for i in range(2)]
        xn = [sb(f"xn{i}", [P, 2, DIM]) for i in range(2)]
        resid = sb("resid", [P, 2, DIM])
        x1 = [sb(f"x1_{i}", [P, 2, DIM]) for i in range(2)]
        x1T = [sb(f"x1T_{i}", [P, KC, SEQ]) for i in range(2)]
        rows = sb("rows", [P, 2, TOPK, ROW])
        codes = sb("codes", [P, TILES, TOPK], I32)
        empty = sb("empty", [P, ROW])
        sh_g = [sb(f"sh_g{m}", [P, 512]) for m in range(2)]
        sh_a = [sb(f"sh_a{m}", [P, 512]) for m in range(2)]
        bn = sb("bn", [P, 2, 6])
        mv = sb("mv", [P, 2, 2])
        small = sb("small", [P, 8, 2])
        e_neg = sb("e_neg", [P, 2, EXPERTS])
        e_one = sb("e_one", [P, 2, EXPERTS])
        score = sb("score", [P, 2, EXPERTS])
        g_score = sb("g_score", [P, 2, RGROUPS])
        g_top = sb("g_top", [P, 2, 8])
        g_idx = sb("g_idx", [P, 2, 8], U32)
        g_eq = sb("g_eq", [P, 2, RGROUPS, TOPG])
        g_mask = sb("g_mask", [P, 2, RGROUPS])
        g_pen = sb("g_pen", [P, 2, RGROUPS])
        masked = sb("masked", [P, 2, EXPERTS])
        top = sb("top", [P, 2, 8])
        top_idx = sb("top_idx", [P, 2, 8], U32)
        top_sum = sb("top_sum", [P, 2])
        top_inv = sb("top_inv", [P, 2])
        weight = sb("weight", [P, 2, TOPK])
        onehot = sb("onehot", [P, 2, TOPK, EXPERTS])
        picked = sb("picked", [P, 2, TOPK, EXPERTS])
        chosen = sb("chosen", [P, 2, EXPERTS], BF16)
        seen = [[sb(f"seen{i}{j}", [P, EXPERTS], BF16) for j in range(2)] for i in range(2)]
        rank = sb("rank", [P, 2, TOPK])
        position = sb("position", [P, 2, TOPK], I32)
        cnt_i = sb("cnt_i", [P, EXPERTS], I32)
        cnt_s = sb("cnt_s", [P, EXPERTS], I32)
        per_e = sb("per_e", [P, EXPERTS])
        upto = sb("upto", [P, EXPERTS])
        one_row = sb("one_row", [P, EXPERTS])
        before = sb("before", [P, EXPERTS])
        used = sb("used", [P, EXPERTS])
        fin = sb("fin", [P, 8])
        shift = sb("shift", [P, P])
        again = sb("again", [P, SLOTS])
        out_row = sb("out_row", [P, UNROLL], I32)
        rows_of = sb("rows_of", [P, EXPERTS])
        rows_here = sb("rows_here", [P, EXPERTS])
        slot_tab = sb("slot_tab", [1, SLOTS], I32)
        packed_tab = sb("packed_tab", [1, SLOTS // PACKED], I32)

        bias_sb = sb("bias_sb", [P, HEADS, SEQ], F32, early)
        wq_sb = sb("wq_sb", [P, KC, DIM], F32, early)
        wk_sb = sb("wk_sb", [P, KC, P], F32, early)
        wv_sb = sb("wv_sb", [P, KC, GROUPS * HD], F32, early)
        xt = [sb(f"xt{i}", [P, KC, SEQ], F32, early) for i in range(2)]
        q_hi = sb("q_hi", [P, 2, SEQ], F32R, early)
        q_lo = sb("q_lo", [P, 2, SEQ], F32R, early)
        k_hi = sb("k_hi", [P, SEQ], F32R, early)
        k_lo = sb("k_lo", [P, SEQ], F32R, early)
        q_pack = [sb(f"q_pack{i}", [P, PAIRS, SEQ], F32R, early) for i in range(2)]
        k_pack = [sb(f"k_pack{i}", [P, GROUPS, 2, SEQ], F32R, early) for i in range(2)]
        v_sb = [sb(f"v_sb{i}", [P, 2, GROUPS, 3 * HD], F32, early) for i in range(2)]
        s_neg = [sb(f"s_neg{i}", [P, 2, SEQ], F32, early) for i in range(4)]
        m_neg = sb("m_neg", [P, 4, 2], F32, early)
        probs = [[sb(f"probs{i}{q}", [P, REP, (q + 1) * P], F32, early) for q in range(2)] for i in range(2)]
        pT0 = [sb(f"pT0_{i}", [P, REP, SEQ], F32, early) for i in range(2)]
        pT1 = [sb(f"pT1_{i}", [P, REP, P], F32, early) for i in range(2)]
        row_sum = [sb(f"row_sum{i}", [P, 2, 2, 2 * REP], F32, early) for i in range(2)]
        l_inv = sb("l_inv", [P, 2 * 2 * REP], F32, early)
        l_wide = sb("l_wide", [P, 2, P], F32, early)
        l_rows = sb("l_rows", [P, SEQ], F32, early)
        early.close()

        late = ctx
        out_t = out.rearrange("b s d -> (b s) d").rearrange("(t p) d -> t p d", p=P)
        expert_w = sb("expert_w", [P, TILES * TOPK * DIM], F32, late)
        w13_sb = expert_w[:, 0:EXPERTS * KC * 2 * INTER].rearrange("p (e c n) -> p e c n", e=EXPERTS, c=KC)
        w2_sb = expert_w[:, EXPERTS * KC * 2 * INTER:].rearrange("p (e n) -> p e n", e=EXPERTS)
        xg = [sb(f"xg{i}", [P, ROW], F32, late) for i in range(UNROLL)]
        xgT = [sb(f"xgT{i}", [P, KC, P], F32, late) for i in range(4)]
        eg = [sb(f"eg{i}", [P, INTER], F32, late) for i in range(4)]
        ea = [sb(f"ea{i}", [P, INTER], F32, late) for i in range(2)]
        eaT = [sb(f"eaT{i}", [P, INTER], F32, late) for i in range(2)]
        rows_y = expert_w[:].rearrange("p (t n) -> p t n", t=TILES)
        f_out = [resid, x1[0]]
        f_resid = x1[1][:]
        y_sum = x1T[0][:, 0, :]
        y_half = [attn_T[i] for i in range(2)]
        f_bn = sb("f_bn", [P, 2, 2, 6])
        f_mv = sb("f_mv", [P, 2, 2, 2])
        f_small = sb("f_small", [P, 2, 8, 2])
        ey = [rows[:, k // 4, k % 4, 0:DIM] for k in range(UNROLL)]

        bank = [ctx.enter_context(nc.psum_tensor(f"bank{i}", [P, 512], F32)) for i in range(8)]
        S_BANK, T_BANK, O_BANK, KV_BANK, Q_BANK = bank[0:3], bank[3:5], bank[5], bank[6], bank[7]

        w_loaded, tables_loaded, late_w_loaded = sem("w_loaded"), sem("tables_loaded"), sem("late_w_loaded")
        late_loaded = [sem(f"late_loaded{i}") for i in range(2)]
        xt_loaded = [sem(f"xt_loaded{i}") for i in range(2)]
        xn_loaded = [sem(f"xn_loaded{i}") for i in range(2)]
        set_up = sem("set_up")
        pool_set_up = sem("pool_set_up")
        passed = sem("passed")
        q_projected, q_hi_ready, q_lo_ready = sem("q_projected"), sem("q_hi_ready"), sem("q_lo_ready")
        kv_projected, k_hi_ready, k_lo_ready = sem("kv_projected"), sem("k_hi_ready"), sem("k_lo_ready")
        v_copied = sem("v_copied")
        qk_stored = sem("qk_stored")
        qk_packed = [sem(f"qk_packed{i}") for i in range(2)]
        l_turned, l_step = sem("l_turned"), sem("l_step")
        scores_ready, biased, probs_ready = sem("scores_ready"), sem("biased"), sem("probs_ready")
        pt_ready, pt_copied, pv_done = sem("pt_ready"), sem("pt_copied"), sem("pv_done")
        l_wide_ready, normed, wo_done = sem("l_wide_ready"), sem("normed"), sem("wo_done")
        ln_step, ln_root, x1_ready = sem("ln_step"), sem("ln_root"), sem("x1_ready")
        x1t_ready, x1t_copied = sem("x1t_ready"), sem("x1t_copied")
        x1_kept = [sem(f"x1_kept{i}") for i in range(2)]
        logits_ready, gate_exp, gate_step, ranks_ready = (
            sem("logits_ready"), sem("gate_exp"), sem("gate_step"), sem("ranks_ready"))
        picks, rows_copied, codes_copied, scattered = (
            sem("picks"), sem("rows_copied"), sem("codes_copied"), sem("scattered"))
        counts_ready, fin_step, pads_written = sem("counts_ready"), sem("fin_step"), sem("pads_written")
        sh_up, sh_silu, sh_act, sh_down, sh_added = (
            sem("sh_up"), sem("sh_silu"), sem("sh_act"), sem("sh_down"), sem("sh_added"))
        xg_loaded, xg_turned, xg_copied = sems("xg_loaded"), sems("xg_turned"), sems("xg_copied")
        gu_ready, e_silu, e_act = sems("gu_ready"), sems("e_silu"), sems("e_act")
        ea_turned, ea_copied, e_down = sems("ea_turned"), sems("ea_copied"), sems("e_down")
        ey_ready, ey_sent = sems("ey_ready"), sems("ey_sent")
        y_loaded = [sem(f"y_loaded{i}") for i in range(4)]
        f_paired = sem("f_paired")
        f_summed, f_stat, f_root, f_fin, f_done = (
            sem("f_summed"), sem("f_stat"), sem("f_root"), sem("f_fin"), sem("f_done"))
        out_stored = [sem(f"out_stored{i}") for i in range(2)]

        block = ctx.enter_context(nc.Block())

        LOGITS = KV_BANK[:, SEQ + P:SEQ + P + 2 * EXPERTS]
        RANKS = [KV_BANK[:, SEQ + P + EXPERTS * (2 + t):SEQ + P + EXPERTS * (3 + t)] for t in range(2)]
        SCORES = [S_BANK[0], S_BANK[1], S_BANK[2], S_BANK[1]]
        DOWN = [O_BANK, S_BANK[2]]

        def attention_loop(eng, body):
            body(0, 0, 0, False, False, True)
            body(1, 1, 0, True, False, True)
            with eng.Fori(1, BATCH // 2 - 1) as h:
                body(2 * h, 0, h, True, True, True)
                body(2 * h + 1, 1, h, True, True, True)
            body(BATCH - 2, 0, BATCH // 2 - 1, True, True, True)
            body(BATCH - 1, 1, BATCH // 2 - 1, True, True, False)

        def slot_loop(eng, step):
            for k in range(UNROLL):
                step(k, Turn(eng, 0))
            with eng.Fori(0, (SLOTS // UNROLL - 2) // 2) as i:
                for j in (1, 2):
                    turn = Turn(eng, 2 * i + j)
                    for k in range(UNROLL):
                        step(k, turn)
            for s in range(SLOTS - UNROLL, SLOTS + 2):
                step(s % UNROLL, Turn(eng, s // UNROLL, s))

        def pair_loop(eng, body):
            body(0, 0, 0)
            with eng.Fori(0, (TILES // 2 - 2) // 2) as i:
                body(2 * i + 1, 1, i)
                body(2 * i + 2, 0, i + 1)
            body(TILES // 2 - 1, 1, TILES // 4 - 1)

        @block.sync
        def _(sp):
            def load_xt(b, par):
                need(sp, kv_projected, b - 1)
                sp.dma_start(xt[par][:], xT[:, bass.ds(b * SEQ, SEQ)].rearrange("(c p) t -> p c t", p=P)
                             ).then_inc(xt_loaded[par], 16)

            def load_xn(b, par):
                need(sp, ln_step, LN_STEPS * (b - 2) + 1)
                sp.dma_start(xn[par][:], x[bass.ds(b * SEQ, SEQ), :].rearrange("(t p) d -> p t d", p=P)
                             ).then_inc(xn_loaded[par], 16)

            def pack(b, par, h):
                need_apart(sp, qk_packed[1 - par], 96 * (h + par), passed)
                for c, (q_part, q_ready, k_part, k_ready) in enumerate((
                        (q_hi, q_hi_ready, k_hi, k_hi_ready), (q_lo, q_lo_ready, k_lo, k_lo_ready))):
                    sp.wait_ge(q_ready, b + 1)
                    sp.dma_start(q_scratch[:, c],
                                 q_part[:].rearrange("p m t -> p (m t)").bitcast(F32)).then_inc(qk_stored, 16)
                    sp.wait_ge(k_ready, b + 1)
                    sp.dma_start(k_scratch[:, c], k_part[:].bitcast(F32)).then_inc(qk_stored, 16)
                need_apart(sp, qk_stored, 64 * (b + 1), passed)
                need(sp, scores_ready, 16 * (b - 1))
                for a in range(2):
                    src = q_scratch[:, :, :, SEQ * a:SEQ * a + SEQ].rearrange("i c d t -> (c d) i t")
                    for c1 in range(2):
                        r = 64 * a + 32 * c1
                        sp.dma_start(q_pack[par][r:r + 32].bitcast(F32), src).then_inc(qk_packed[par], 16)
                ksrc = k_scratch.rearrange("g c n t -> (c n) g t")
                if isinstance(b, int) and b < 2:
                    sp.wait_ge(set_up, PACKS_BLANK)
                for a in range(2):
                    sp.dma_start(k_pack[par][64 * a:64 * a + 64, :, a, :].bitcast(F32), ksrc
                                 ).then_inc(qk_packed[par], 16)

            load_xt(0, 0)
            sp.dma_start(wq_sb[:], wq).then_inc(w_loaded, 16)
            pack(0, 0, 0)
            load_xt(1, 1)
            load_xn(0, 0)
            load_xn(1, 1)
            sp.dma_start(wo_sb[:], wo).then_inc(late_w_loaded, 16)
            sp.dma_start(gw_sb[:], gate_w).then_inc(late_w_loaded, 16)
            sp.dma_start(sw1_sb[:], sw1).then_inc(late_w_loaded, 16)
            sp.dma_start(sw3_sb[:], sw3).then_inc(late_w_loaded, 16)
            sp.dma_start(sw2_sb[:], sw2).then_inc(late_w_loaded, 16)

            sp.wait_ge(pool_set_up, 4)
            sp.dma_start(routed[EXPERTS * REGION:EXPERTS * REGION + P, :], empty[:]).then_inc(pads_written, 16)

            def write_pads(b):
                n = EXPERTS // BATCH
                pads = routed[bass.ds(REGION * n * b, REGION * n), :].rearrange("(e r) n -> r e n", r=REGION)[0:P]
                sp.dma_start(pads, empty[:].unsqueeze(1).to_broadcast([P, n, ROW])).then_inc(pads_written, 16)

            def keep_x1(b, par):
                sp.wait_ge(x1t_copied, b + 1)
                sp.dma_start(x_sum[:, bass.ds(2 * b, 2), :], x1[par][:]).then_inc(x1_kept[par], 16)
                sp.dma_start(x1T_all[:, :, bass.ds(b * SEQ, SEQ)], x1T[par][:]).then_inc(x1_kept[par], 16)

            def body(b, par, h, one_behind, two_behind, ahead):
                if ahead:
                    pack(b + 1, 1 - par, h + par)
                if not isinstance(b, int) or b + 2 < BATCH:
                    load_xt(b + 2, par)
                if one_behind:
                    if ahead:
                        load_xn(b + 1, 1 - par)
                    keep_x1(b - 1, 1 - par)
                if isinstance(b, int) and b == 1:
                    for i in range(BATCH):
                        write_pads(i)

            attention_loop(sp, body)
            sp.wait_ge(normed, 2 * BATCH)

            def load_weights(i, k):
                need(sp, late_loaded[k], 16 * i)
                at = bass.ds(W_CHUNK * (2 * i + k), W_CHUNK)
                sp.dma_start(expert_w[:, at], expert_weights[:, at]).then_inc(late_loaded[k], 16)

            for k in range(2):
                load_weights(0, k)
            with sp.Fori(1, W_CHUNKS // 4) as i:
                for k in range(2):
                    load_weights(i, k)
            keep_x1(BATCH - 1, 1)
            with sp.Fori(W_CHUNKS // 4, W_CHUNKS // 2) as i:
                for k in range(2):
                    load_weights(i, k)
            sp.wait_ge(pads_written, 16 * (BATCH + 1))
            sp.wait_ge(scattered, 16 * 2 * TOPK * BATCH)
            sp.wait_ge(fin_step, FIN_STEPS + 3)

            def load_slot(s, k, turn):
                at = sp.value_load(slot_tab[0:1, bass.ds(s, 1)], min_val=0, max_val=EXPERTS * REGION)
                if turn is not None:
                    sp.wait_ge(ey_ready[k], turn)
                sp.dma_start(xg[k][:], routed[bass.ds(at, P), :]).then_inc(xg_loaded[k], 16)

            for k in range(UNROLL):
                load_slot(k, k, None)
            with sp.Fori(1, SLOTS // UNROLL) as i:
                for k in range(UNROLL):
                    load_slot(UNROLL * i + k, k, i)

            for k in range(UNROLL):
                sp.wait_ge(ey_sent[k], 16 * SLOTS // UNROLL)
            y_view = expert_out.rearrange("(t p j) d -> t p (j d)", p=P, j=TOPK)

            def load_y(p, par, h):
                for t in range(2):
                    need(sp, y_loaded[2 * par + t], 16 * h)
                    sp.dma_start(rows_y[:, bass.ds(2 * p + t, 1), :].rearrange("p a n -> p (a n)"),
                                 y_view[bass.ds(2 * p + t, 1)].rearrange("a p n -> (a p) n")
                                 ).then_inc(y_loaded[2 * par + t], 16)

            for p in range(2):
                load_y(p, p, 0)
            with sp.Fori(1, TILES // 4) as h:
                load_y(2 * h, 0, h)
                load_y(2 * h + 1, 1, h)
            for k in range(2):
                sp.wait_ge(out_stored[k], 16 * TILES // 4)

        @block.tensor
        def _(pe):
            def project_q(b, par, h):
                pe.wait_ge(xt_loaded[par], 16 * (h + 1))
                need(pe, q_lo_ready, b)
                need(pe, x1t_copied, b - 2)
                for m in range(2):
                    for c in range(KC):
                        last = pe.matmul(Q_BANK[:, SEQ * m:SEQ * m + SEQ], wq_sb[:, c, P * m:P * m + P],
                                         xt[par][:, c, :], start=(c == 0), stop=(c == KC - 1))
                last.then_inc(q_projected, 1)

            def project_kv(b, par):
                need(pe, k_lo_ready, b)
                need(pe, gate_exp, b - 2)
                for c in range(KC):
                    pe.matmul(KV_BANK[:, 0:SEQ], wk_sb[:, c, :], xt[par][:, c, :],
                              start=(c == 0), stop=(c == KC - 1))
                for t in range(2):
                    at = SEQ + GROUPS * HD * t
                    for c in range(KC):
                        last = pe.matmul(KV_BANK[:, at:at + GROUPS * HD], xt[par][:, c, P * t:P * t + P],
                                         wv_sb[:, c, :], start=(c == 0), stop=(c == KC - 1))
                last.then_inc(kv_projected, 1)

            def scores(b, par, h, g, u):
                pair, qb = u // 2, u % 2
                unit = 16 * b + 4 * g + u
                if g == 0 and u == 0:
                    pe.wait_ge(qk_packed[par], 96 * (h + 1))
                need(pe, biased, 2 * (unit - (4 if u % 2 == 0 else 2)) + 2)
                n = (qb + 1) * P
                pe.matmul(SCORES[u][:, 0:2 * n], q_pack[par][:, 2 * g + pair, P * qb:P * qb + P],
                          k_pack[par][:, g, :, 0:n], start=True, stop=True).then_inc(scores_ready, 1)

            def turn_probs(b, g, j):
                n = 12 * b + 3 * g + j
                pb = T_BANK[(3 * g + j) % 2]
                if j < 2:
                    pe.wait_ge(probs_ready, 32 * b + 8 * g + 4 * j + 4)
                need(pe, pt_copied, n - 1)
                if j < 2:
                    for r in (2 * j, 2 * j + 1):
                        for qb in range(2):
                            at = SEQ * (r % 2) + P * qb
                            last = pe.transpose(pb[:, at:at + P], probs[g % 2][qb][:, r, 0:P], ident)
                else:
                    for r in range(REP):
                        last = pe.transpose(pb[:, P * r:P * r + P], probs[g % 2][1][:, r, P:2 * P], ident)
                last.then_inc(pt_ready, 1)

            def values(b, par, g):
                pe.wait_ge(pt_copied, 12 * b + 3 * g + 3)
                if g == 0:
                    pe.wait_ge(v_copied, b + 1)
                need(pe, normed, 2 * b + g // 2)
                for kb, pT in ((0, pT0[g % 2]), (1, pT1[g % 2])):
                    for r in (0, 2, 1, 3):
                        at, col = 64 * (g % 2) + 32 * (r // 2), HD * (1 - r % 2)
                        last = pe.matmul(O_BANK[at:at + 32, P * kb:SEQ], v_sb[par][:, kb, g, col:col + 32], pT[:, r, :],
                                         start=(kb == 0 and r % 2 == 0), stop=(kb == 1 and r % 2 == 1),
                                         skip_group_check=True)
                if g % 2 == 0:
                    last.then_inc(pv_done, 1)
                    return
                last.then_inc(pv_done, 1)
                pe.wait_ge(l_wide_ready, 2 * b + g // 2 + 1)
                for qb in range(2):
                    last = pe.transpose(O_BANK[:, SEQ + P * qb:SEQ + P * qb + P], l_wide[:, qb, :], ident)
                last.then_inc(l_turned, 1)

            def project_out(b, par):
                pe.wait_ge(normed, 2 * b + 2)
                if isinstance(b, int) and b == 0:
                    pe.wait_ge(late_w_loaded, 16 * 5)
                pe.wait_ge(q_lo_ready, min(b + 3, BATCH) if isinstance(b, int) else b + 3)
                need(pe, x1t_copied, b)
                for t in range(2):
                    for c in range(KC):
                        last = pe.matmul(Q_BANK[:, DIM * t:DIM * t + DIM], attn_T[par][:, c, P * t:P * t + P],
                                         wo_sb[:, c, :], start=(c == 0), stop=(c == KC - 1))
                last.then_inc(wo_done, 1)

            def turn_x1(b, par):
                pe.wait_ge(x1_ready, 2 * b + 2)
                for c in range(KC):
                    for t in range(2):
                        last = pe.transpose(Q_BANK[:, SEQ * c + P * t:SEQ * c + P * t + P],
                                            x1[par][:, t, P * c:P * c + P], ident)
                last.then_inc(x1t_ready, 1)

            def gate(b, par):
                pe.wait_ge(x1t_copied, b + 1)
                need(pe, picks, 2 * b)
                for t in range(2):
                    for c in range(KC):
                        last = pe.matmul(LOGITS[:, EXPERTS * t:EXPERTS * t + EXPERTS], x1T[par][:, c, P * t:P * t + P],
                                         gw_sb[:, c, :], start=(c == 0), stop=(c == KC - 1))
                last.then_inc(logits_ready, 1)

            def ranks(b, par):
                pe.wait_ge(gate_step, GATE_STEPS * b + 22)
                for t in range(2):
                    at = RANKS[t]
                    pe.matmul(at, tri[:], chosen[:, t, :], start=True, stop=False)
                    last = pe.matmul(at, ones_b[:], seen[par][t][:], start=False, stop=True)
                last.then_inc(ranks_ready, 1)

            def body(b, par, h, one_behind, two_behind, ahead):
                o = 1 - par
                for g in range(GROUPS):
                    for u in range(4):
                        if g < GROUPS - 1:
                            scores(b, par, h, g + 1, u)
                        elif ahead:
                            scores(b + 1, o, h + par, 0, u)
                        if u < 3:
                            turn_probs(b, g, u)
                        if (g, u) == (0, 1) and ahead:
                            project_q(b + 1, o, h + par)
                            project_kv(b + 1, o)
                        if g == 3 and u == 1 and one_behind:
                            turn_x1(b - 1, o)
                    if g > 0:
                        values(b, par, g - 1)
                    if g == 0:
                        if one_behind:
                            values(b - 1, o, GROUPS - 1)
                    if g == 1 and one_behind:
                        project_out(b - 1, o)
                    if g == 2 and two_behind:
                        ranks(b - 2, par)
                    if g == 3 and one_behind:
                        gate(b - 1, o)

            pe.wait_ge(w_loaded, 16 * 3)
            project_q(0, 0, 0)
            project_kv(0, 0)
            for u in range(4):
                scores(0, 0, 0, 0, u)
            pe.wait_ge(tables_loaded, 16 * (GROUPS + 1))
            attention_loop(pe, body)

            def shared_up(tb, m):
                n = 512
                if m == 0:
                    for i in range(2):
                        pe.wait_ge(x1_kept[i], 32 * (tb + 1))
                need(pe, sh_act, 2 * tb - 1 + m)
                for w, bk in ((sw1_sb, S_BANK[m]), (sw3_sb, T_BANK[m])):
                    for c in range(KC):
                        last = pe.matmul(bk[:], w[:, c, P * m:P * m + P], x1T_all[:, c, n * tb:n * tb + n],
                                         start=(c == 0), stop=(c == KC - 1))
                last.then_inc(sh_up, 1)

            def shared_down(tb):
                pe.wait_ge(sh_act, 2 * tb + 2)
                for t in range(4):
                    need(pe, sh_added, 4 * tb + t - 1)
                    for m in range(2):
                        last = pe.matmul(DOWN[t % 2][:, 0:DIM], sh_a[m][:, P * t:P * t + P],
                                         sw2_sb[:, m, :], start=(m == 0), stop=(m == 1))
                    last.then_inc(sh_down, 1)

            last_b = BATCH - 1
            values(last_b, 1, GROUPS - 1)
            project_out(last_b, 1)
            ranks(last_b - 1, 0)
            shared_up(0, 0)
            shared_up(0, 1)
            shared_up(1, 0)
            shared_down(0)
            turn_x1(last_b, 1)
            shared_up(1, 1)
            gate(last_b, 1)
            shared_up(2, 0)
            shared_down(1)
            ranks(last_b, 1)
            shared_up(2, 1)
            pe.wait_ge(picks, 2 * BATCH)
            pe.matmul(LOGITS[:, 0:EXPERTS], ones_b[:], seen[0][0][:], start=True, stop=True).then_inc(counts_ready, 1)
            shared_up(3, 0)
            shared_down(2)
            pe.wait_ge(fin_step, FIN_STEPS)
            pe.transpose(Q_BANK[0:1, SEQ:SEQ + P], fin[:, 6:7], ident)
            pe.matmul(Q_BANK[0:1, SEQ + P:SEQ + P + SLOTS // PACKED], fin[:, 7:8],
                      cst[:, C_PACK:C_PACK + SLOTS // PACKED], start=True, stop=True)
            pe.transpose(Q_BANK[:, 0:P], shift[:], ident).then_inc(counts_ready, 1)
            shared_up(3, 1)
            shared_down(3)
            pe.wait_ge(fin_step, FIN_STEPS + 3)
            for k in range(2):
                pe.wait_ge(late_loaded[k], 16 * W_CHUNKS // 2)
            pe.wait_ge(sh_added, TILES)

            def turn_rows(k, turn, ahead):
                at = (k + ahead) % UNROLL
                turn.wait(pe, xg_loaded, k, ahead, 16)
                for c in range(KC):
                    last = pe.transpose((KV_BANK, Q_BANK)[at % 2][:, P * c:P * c + P],
                                        xg[at][:, P * c:P * c + P], ident)
                last.then_inc(xg_turned[at], 1)

            def gate_up(k, turn, e):
                turn.wait(pe, xg_copied, k, 0)
                for c in range(KC):
                    last = pe.matmul(S_BANK[k % 2][:, 0:2 * INTER], xgT[k % 4][:, c, :],
                                     w13_sb[:, bass.ds(e, 1), c, :].rearrange("p a n -> p (a n)"),
                                     start=(c == 0), stop=(c == KC - 1))
                last.then_inc(gu_ready[k], 1)

            def turn_act(k, turn):
                at = (k - 1) % UNROLL
                turn.wait(pe, e_act, k, -1)
                pe.transpose(T_BANK[at % 2][:, 0:P], ea[at % 2][:], ident).then_inc(ea_turned[at], 1)

            def down(k, turn, e):
                at = (k - 2) % UNROLL
                turn.wait(pe, ea_copied, k, -2)
                if not turn.exists(k, 0):
                    turn.wait(pe, ey_ready, k, -4)
                pe.matmul(DOWN[at % 2][:, 0:DIM], eaT[at % 2][:],
                          w2_sb[:, bass.ds(e, 1), :].rearrange("p a n -> p (a n)"),
                          start=True, stop=True).then_inc(e_down[at], 1)

            def experts_of(word):
                return pe.value_load(packed_tab[0:1, bass.ds(word, 1)], min_val=0, max_val=EXPERTS ** PACKED - 1)

            def expert_in(word, k):
                return pe.snap((word >> (5 * (k % PACKED))) & (EXPERTS - 1), min_val=0, max_val=EXPERTS - 1)

            words = {}

            def step(k, turn):
                first_word = turn.turn * (UNROLL // PACKED)
                if k % PACKED == 0 and turn.exists(k, 0):
                    words[k // PACKED] = experts_of(first_word + k // PACKED)
                if turn.exists(k, 0):
                    gate_up(k, turn, expert_in(words[k // PACKED], k))
                if turn.exists(k, 2):
                    turn_rows(k, turn, 2)
                if turn.exists(k, -2):
                    if k == 0:
                        words[-1] = experts_of(first_word - 1)
                    down(k, turn, expert_in(words[(k - 2) // PACKED], k - 2))
                if turn.exists(k, -1):
                    turn_act(k, turn)

            for k in range(2):
                turn_rows(k, Turn(pe, 0), 0)
            slot_loop(pe, step)

            def final(p, par, h):
                need(pe, f_done, 2 * (p - 1))
                tile = x_sum[:, bass.ds(2 * p + 1, 1), :].rearrange("p a d -> p (a d)")
                pe.matmul(S_BANK[par][:, 0:DIM], ident, tile, start=True, stop=False)
                pe.wait_ge(y_loaded[2 * par + 1], 16 * (h + 1))
                for j in (4, 5):
                    row = rows_y[:, bass.ds(2 * p + 1, 1), DIM * j:DIM * j + DIM].rearrange("p a d -> p (a d)")
                    pe.matmul(S_BANK[par][:, 0:DIM], ident, row, start=False, stop=False)
                pe.wait_ge(f_paired, p + 1)
                for j in range(2):
                    last = pe.matmul(S_BANK[par][:, 0:DIM], ident, y_half[par][:, j, :], start=False, stop=(j == 1))
                last.then_inc(f_summed, 1)

            pair_loop(pe, final)

        @block.scalar
        def _(act):
            act.dma_start(wk_sb[:], wk).then_inc(w_loaded, 16)
            act.dma_start(wv_sb[:], wv).then_inc(w_loaded, 16)
            act.dma_start(cst[:], consts).then_inc(tables_loaded, 16)
            for g in range(GROUPS):
                heads = slice(REP * g, REP * g + REP)
                act.dma_start(bias_sb[:, heads], bias[:, heads]).then_inc(tables_loaded, 16)
            act.preload_act_table_set("natural_log_exp_and_others")

            def split_q(b):
                act.wait_ge(q_projected, b + 1)
                need(act, qk_stored, 64 * b)
                act.activation(q_hi[:].rearrange("p m t -> p (m t)"), Q_BANK[:], ACT.Copy, scale=QSCALE
                               ).then_inc(q_hi_ready, 1)

            def split_kv(b, par):
                act.wait_ge(kv_projected, b + 1)
                act.activation(k_hi[:], KV_BANK[:, 0:SEQ], ACT.Copy).then_inc(k_hi_ready, 1)
                need(act, pv_done, 4 * (b - 1))
                if isinstance(b, int) and b < 2:
                    act.wait_ge(set_up, V_BLANK)
                act.activation(v_sb[par][:, :, :, HD:2 * HD],
                               KV_BANK[:, SEQ:SEQ + P].rearrange("p (t g d) -> p t g d", t=2, g=GROUPS), ACT.Copy
                               ).then_inc(v_copied, 1)

            def exps(b, b_par, g, u):
                pair, qb = u // 2, u % 2
                unit = 16 * b + 4 * g + u
                n = (qb + 1) * P
                if u == 0:
                    need(act, pt_ready, 3 * (4 * b + g - 1))
                for r in range(2):
                    head = REP * (g % 2) + 2 * pair + r
                    act.wait_ge(biased, 2 * unit + r + 1)
                    act.activation(probs[g % 2][qb][:, 2 * pair + r, :], s_neg[u][:, r, 0:n], ACT.Exp,
                                   bias=m_neg[:, u, r:r + 1], scale=-1.0,
                                   accum_out=row_sum[b_par][:, g // 2, qb, head:head + 1]).then_inc(probs_ready, 1)

            def copy_pt(b, g, j):
                act.wait_ge(pt_ready, 12 * b + 3 * g + j + 1)
                if j == 0:
                    if (g - 1) % GROUPS in VECTOR_COPIES:
                        need(act, pt_copied, 12 * b + 3 * g)
                    need(act, pv_done, 4 * b + g - 1)
                dst = pT0[g % 2][:, 2 * j:2 * j + 2, :] if j < 2 else pT1[g % 2][:]
                act.activation(dst.rearrange("p r t -> p (r t)"), T_BANK[(3 * g + j) % 2][:], ACT.Copy
                               ).then_inc(pt_copied, 1)

            def ln_first_root(b):
                act.wait_ge(ln_step, LN_STEPS * b + 6)
                act.activation(small[:, 1, :], small[:, 0, :], ACT.Ln).then_inc(ln_root, 1)
                act.wait_ge(ln_root, 2 * b + 1)
                act.activation(small[:, 2, :], small[:, 1, :], ACT.Exp, scale=-0.5).then_inc(ln_root, 1)

            def copy_x1t(b, par, h):
                act.wait_ge(x1t_ready, b + 1)
                need(act, x1_kept[par], 32 * h)
                act.activation(x1T[par][:].rearrange("p c t -> p (c t)"), Q_BANK[:], ACT.Copy
                               ).then_inc(x1t_copied, 1)

            def gate_exps(b):
                act.wait_ge(logits_ready, b + 1)
                act.activation(e_neg[:].rearrange("p t e -> p (t e)"), LOGITS,
                               ACT.Exp, scale=-1.0).then_inc(gate_exp, 1)

            def copy_x1_rows(b, par, t):
                act.wait_ge(x1_ready, 2 * b + 2)
                need(act, scattered, 16 * 2 * TOPK * b)
                act.activation(rows[:, t, :, 0:DIM], x1[par][:, t, :].unsqueeze(1).to_broadcast([P, TOPK, DIM]),
                               ACT.Copy).then_inc(rows_copied, 1)

            def body(b, par, h, one_behind, two_behind, ahead):
                o = 1 - par
                for g in range(GROUPS):
                    if g == 0 and two_behind:
                        gate_exps(b - 2)
                    for u in range(4):
                        if 0 < u < 3 or (u == 3 and g not in VECTOR_COPIES):
                            copy_pt(b, g, u - 1)
                        if g < GROUPS - 1:
                            exps(b, par, g + 1, u)
                        elif ahead:
                            exps(b + 1, o, 0, u)
                        if (g, u) == (0, 2) and ahead:
                            split_q(b + 1)
                            split_kv(b + 1, o)
                        if g == 2 and u == 2 and one_behind:
                            ln_first_root(b - 1)
                        if g == 3 and u == 1 and one_behind:
                            copy_x1t(b - 1, o, h - 1 + par)
                        if two_behind and (g, u) in ((2, 3), (3, 3)):
                            copy_x1_rows(b - 2, par, g - 2)

            split_q(0)
            split_kv(0, 0)
            for u in range(4):
                exps(0, 0, 0, u)
            attention_loop(act, body)

            def shared_silu(tb, m):
                act.wait_ge(sh_up, 2 * tb + m + 1)
                need(act, sh_act, 2 * tb + m - 1)
                act.activation(sh_g[m][:], S_BANK[m][:], ACT.Silu).then_inc(sh_silu, 1)

            last_b = BATCH - 1
            gate_exps(last_b - 1)
            ln_first_root(last_b)
            shared_silu(0, 0)
            shared_silu(0, 1)
            for t in range(2):
                copy_x1_rows(last_b - 1, 0, t)
            shared_silu(1, 0)
            copy_x1t(last_b, 1, last_b // 2)
            shared_silu(1, 1)
            gate_exps(last_b)
            shared_silu(2, 0)
            for t in range(2):
                copy_x1_rows(last_b, 1, t)
            shared_silu(2, 1)
            shared_silu(3, 0)
            shared_silu(3, 1)

            def copy_rows(k, turn, ahead):
                at = (k + ahead) % UNROLL
                turn.wait(act, xg_turned, k, ahead)
                act.activation(xgT[at % 4][:].rearrange("p c t -> p (c t)"),
                               (KV_BANK, Q_BANK)[at % 2][:, 0:DIM], ACT.Copy).then_inc(xg_copied[at], 1)

            def step(k, turn):
                if k >= UNROLL - 2 and turn.exists(k, 0):
                    turn.wait(act, ey_sent, k, 0, 16, again=-1)
                if turn.exists(k, 0):
                    turn.wait(act, gu_ready, k, 0)
                    act.activation(eg[k % 4][:], S_BANK[k % 2][:, 0:INTER], ACT.Silu).then_inc(e_silu[k], 1)
                if turn.exists(k, -2):
                    at = (k - 2) % UNROLL
                    turn.wait(act, e_down, k, -2)
                    if k >= 2:
                        turn.wait(act, ey_sent, k, -2, 16, again=-1)
                    act.activation(ey[at], DOWN[at % 2][:, 0:DIM], ACT.Copy,
                                   scale=xg[at][:, DIM + 1:DIM + 2]).then_inc(ey_ready[at], 1)
                if turn.exists(k, 2):
                    copy_rows(k, turn, 2)

            for k in range(2):
                copy_rows(k, Turn(act, 0), 0)
            slot_loop(act, step)

            def final_apply(p, par, h):
                act.wait_ge(f_fin, 5 * p + 5)
                need(act, out_stored[par], 16 * h)
                for t, src in enumerate((f_resid[:, par, :], S_BANK[par][:, 0:DIM])):
                    last = act.activation(f_out[par][:, t, :], src, ACT.Identity, scale=f_small[:, par, 6, t:t + 1],
                                          bias=f_small[:, par, 7, t:t + 1])
                    last.then_inc(f_done, 1)
                act.wait_ge(f_done, 2 * p + 2)
                act.dma_start(out_t[bass.ds(2 * p, 2)].rearrange("t p d -> p t d"), f_out[par][:]
                              ).then_inc(out_stored[par], 16)

            def final(p, par, h):
                if not isinstance(p, int) or p > 0:
                    final_apply(p - 1, 1 - par, h - 1 + par)
                act.wait_ge(f_stat, F_STATS * p + F_STATS)
                act.activation(f_small[:, par, 1, :], f_small[:, par, 0, :], ACT.Ln).then_inc(f_root, 1)
                act.wait_ge(f_root, 2 * p + 1)
                act.activation(f_small[:, par, 2, :], f_small[:, par, 1, :], ACT.Exp, scale=-0.5).then_inc(f_root, 1)

            act.preload_act_table_set("natural_log_exp_and_others")
            pair_loop(act, final)
            final_apply(TILES // 2 - 1, 1, TILES // 4 - 1)

        @block.vector
        def _(dve):
            for i in range(2):
                dve.memset(v_sb[i][:], 0.0).then_inc(set_up, 1)
            for i in range(2):
                dve.memset(k_pack[i][P // 2:P, :, 0, :].bitcast(F32), 0.0).then_inc(set_up, 1)
                dve.memset(k_pack[i][0:P // 2, :, 1, :].bitcast(F32), 0.0).then_inc(set_up, 1)
            dve.memset(ones_b[:], 1.0).then_inc(set_up, 1)
            dve.memset(seen[0][0][:], 1.0).then_inc(set_up, 1)
            dve.memset(one_row[:], 1.0).then_inc(set_up, 1)
            dve.wait_ge(tables_loaded, 16 * (GROUPS + 1))
            dve.tensor_copy(tri[:], cst[:, C_TRI:C_TRI + P]).then_inc(set_up, 1)

            def split_q(b):
                dve.wait_ge(q_hi_ready, b + 1)
                need(dve, qk_stored, 64 * b)
                dve.scalar_tensor_tensor(q_lo[:].rearrange("p m t -> p (m t)"), Q_BANK[:], QSCALE,
                                         q_hi[:].rearrange("p m t -> p (m t)").bitcast(F32),
                                         ALU.mult, ALU.subtract).then_inc(q_lo_ready, 1)

            def split_k(b):
                dve.wait_ge(v_copied, b + 1)
                need(dve, qk_stored, 64 * b)
                dve.tensor_tensor(k_lo[:], KV_BANK[:, 0:SEQ], k_hi[:].bitcast(F32), ALU.subtract
                                  ).then_inc(k_lo_ready, 1)

            def bias_max(b, g, u):
                pair, qb = u // 2, u % 2
                unit = 16 * b + 4 * g + u
                n = (qb + 1) * P
                if u == 0:
                    need(dve, probs_ready, 2 * (unit - 4) + 2)
                need_apart(dve, scores_ready, unit + 1, passed)
                for r in range(2):
                    dve.tensor_tensor_reduce(
                        out=s_neg[u][:, r, 0:n], in0=SCORES[u][:, n * r:n * r + n],
                        in1=bias_sb[:, REP * g + 2 * pair + r, SEQ - n:SEQ], scale=-1.0, scalar=BIG,
                        op0=ALU.add, op1=ALU.min, accum_out=m_neg[:, u, r:r + 1]).then_inc(biased, 1)

            def copy_pt1(b, g):
                dve.wait_ge(pt_ready, 12 * b + 3 * g + 3)
                dve.wait_ge(pt_copied, 12 * b + 3 * g + 2)
                dve.tensor_copy(pT1[g % 2][:].rearrange("p r t -> p (r t)"), T_BANK[3 * g % 2][:]).then_inc(pt_copied, 1)

            def invert(b, par, pp):
                n = 2 * b + pp
                dve.wait_ge(probs_ready, 32 * b + 16 * pp + 16)
                need(dve, l_wide_ready, n)
                dve.reciprocal(l_inv[:], row_sum[par][:, pp].rearrange("p q h -> p (q h)")).then_inc(l_step, 1)
                dve.wait_ge(l_step, 2 * n + 1)
                need(dve, l_turned, n)
                dve.tensor_copy(l_wide[:].rearrange("p q (h d) -> p (q h) d", d=HD),
                                l_inv[:].unsqueeze(2).to_broadcast([P, 4 * REP, HD])).then_inc(l_wide_ready, 1)

            def norm(b, par, pp):
                n = 2 * b + pp
                dve.wait_ge(l_turned, n + 1)
                if pp == 0:
                    need(dve, wo_done, b - 1)
                need(dve, normed, n)
                dve.tensor_copy(l_rows[:], O_BANK[:, SEQ:2 * SEQ]).then_inc(l_step, 1)
                dve.wait_ge(l_step, 2 * n + 2)
                dve.tensor_tensor(attn_T[par][:, pp, :], O_BANK[:, 0:SEQ], l_rows[:], ALU.mult).then_inc(normed, 1)

            def ln_stats(b, par, h):
                n = LN_STEPS * b
                dve.wait_ge(wo_done, b + 1)
                dve.wait_ge(xn_loaded[par], 16 * (h + 1))
                need(dve, x1_ready, 2 * b)
                dve.tensor_tensor(resid[:].rearrange("p t d -> p (t d)"), Q_BANK[:],
                                  xn[par][:].rearrange("p t d -> p (t d)"), ALU.add).then_inc(ln_step, 1)
                dve.wait_ge(ln_step, n + 1)
                for t in range(2):
                    dve.bn_stats(bn[:, t, :], resid[:, t, :]).then_inc(ln_step, 1)
                need_apart(dve, ln_step, n + 3, passed)
                for t in range(2):
                    dve.bn_aggr(mv[:, t, :], bn[:, t, :]).then_inc(ln_step, 1)
                dve.wait_ge(ln_step, n + 5)
                dve.tensor_scalar(small[:, 0, :], mv[:, :, 1], EPS, None, ALU.add).then_inc(ln_step, 1)

            def polish(semaphore, n, cols, w):
                v, y, a, c, d, r = (cols[:, k, 0:w] for k in (0, 2, 3, 4, 5, 6))
                dve.tensor_tensor(a, y, y, ALU.mult).then_inc(semaphore, 1)
                dve.wait_ge(semaphore, n + 1)
                dve.tensor_tensor(c, a, v, ALU.mult).then_inc(semaphore, 1)
                dve.wait_ge(semaphore, n + 2)
                dve.tensor_scalar(d, c, -0.5, 1.5, ALU.mult, ALU.add).then_inc(semaphore, 1)
                dve.wait_ge(semaphore, n + 3)
                dve.tensor_tensor(r, y, d, ALU.mult).then_inc(semaphore, 1)
                dve.wait_ge(semaphore, n + 4)

            def ln_apply(b, par, h):
                dve.wait_ge(ln_root, 2 * b + 2)
                polish(ln_step, LN_STEPS * b + 6, small, 2)
                need(dve, x1t_ready, b - 1)
                need(dve, rows_copied, 2 * (b - 1))
                need(dve, x1_kept[par], 32 * h)
                for t in range(2):
                    dve.tensor_scalar(x1[par][:, t, :], resid[:, t, :], mv[:, t, 0:1], small[:, 6, t:t + 1],
                                      ALU.subtract, ALU.mult).then_inc(x1_ready, 1)

            def router(b, par, part):
                n = GATE_STEPS * b

                def op(k, ins):
                    ins.then_inc(gate_step, 1)

                def after(k):
                    need_apart(dve, gate_step, n + k, passed)

                iota8 = iota[:, 0:RGROUPS]
                if part == 0:
                    dve.wait_ge(gate_exp, b + 1)
                    need(dve, gate_step, n)
                    op(1, dve.tensor_scalar(e_one[:], e_neg[:], 1.0, None, ALU.add))
                    after(1)
                    op(2, dve.reciprocal(score[:], e_one[:]))
                    after(2)
                    op(3, dve.tensor_reduce(g_score[:], score[:].rearrange("p t (g e) -> p t g e", g=RGROUPS),
                                            AX.X, ALU.max))
                    after(3)
                    for t in range(2):
                        op(4 + t, dve.max(g_top[:, t, :], g_score[:, t, :]))
                    after(5)
                    for t in range(2):
                        op(6 + t, dve.max_index(g_idx[:, t, :], g_top[:, t, :], g_score[:, t, :]))
                elif part == 1:
                    after(7)
                    shape = [P, 2, RGROUPS, TOPG]
                    op(8, dve.tensor_tensor(g_eq[:], g_idx[:, :, 0:TOPG].unsqueeze(2).to_broadcast(shape),
                                            iota8.unsqueeze(1).unsqueeze(3).to_broadcast(shape), ALU.is_equal))
                    after(8)
                    op(9, dve.tensor_reduce(g_mask[:], g_eq[:], AX.X, ALU.add))
                    after(9)
                    op(10, dve.tensor_scalar(g_pen[:], g_mask[:], 4.0, -4.0, ALU.mult, ALU.add))
                    after(10)
                    shape = [P, 2, RGROUPS, EXPERTS // RGROUPS]
                    op(11, dve.tensor_tensor(masked[:].rearrange("p t (g e) -> p t g e", g=RGROUPS),
                                             score[:].rearrange("p t (g e) -> p t g e", g=RGROUPS),
                                             g_pen[:].unsqueeze(3).to_broadcast(shape), ALU.add))
                    after(11)
                    for t in range(2):
                        op(12 + t, dve.max(top[:, t, :], masked[:, t, :]))
                    after(13)
                    for t in range(2):
                        op(14 + t, dve.max_index(top_idx[:, t, :], top[:, t, :], masked[:, t, :]))
                elif part == 2:
                    after(15)
                    op(16, dve.tensor_reduce(top_sum[:], top[:, :, 0:TOPK], AX.X, ALU.add))
                    after(16)
                    op(17, dve.reciprocal(top_inv[:], top_sum[:]))
                    after(17)
                    need(dve, codes_copied, 2 * b)
                    op(18, dve.scalar_tensor_tensor(weight[:], top[:, :, 0:TOPK], ROUTE_SCALE,
                                                    top_inv[:].unsqueeze(2).to_broadcast([P, 2, TOPK]),
                                                    ALU.mult, ALU.mult))
                    shape = [P, 2, TOPK, EXPERTS]
                    op(19, dve.tensor_tensor(onehot[:], top_idx[:, :, 0:TOPK].unsqueeze(3).to_broadcast(shape),
                                             iota.unsqueeze(1).unsqueeze(1).to_broadcast(shape), ALU.is_equal))
                    after(19)
                    with nc.allow_low_precision(reason="zeros and ones, exact in bfloat16"):
                        op(20, dve.tensor_reduce(chosen[:], onehot[:].rearrange("p t j e -> p t e j"), AX.X, ALU.add))
                    after(20)
                    op(21, dve.tensor_tensor(seen[par][1][:], seen[par][0][:], chosen[:, 0, :], ALU.add))
                    after(21)
                    op(22, dve.tensor_tensor(seen[1 - par][0][:], seen[par][1][:], chosen[:, 1, :], ALU.add))
                else:
                    dve.wait_ge(ranks_ready, b + 1)
                    for t in range(2):
                        ins = dve.tensor_tensor(
                            picked[:, t], onehot[:, t],
                            RANKS[t].unsqueeze(1)
                            .to_broadcast([P, TOPK, EXPERTS]), ALU.mult)
                        ins.then_inc(picks, 1)
                    dve.wait_ge(picks, 2 * b + 2)
                    op(23, dve.tensor_reduce(rank[:], picked[:], AX.X, ALU.add))
                    after(23)
                    need(dve, scattered, 16 * 2 * TOPK * b)
                    op(24, dve.scalar_tensor_tensor(position[:], top_idx[:, :, 0:TOPK], float(REGION), rank[:],
                                                    ALU.mult, ALU.add))

            def body(b, par, h, one_behind, two_behind, ahead):
                o = 1 - par
                for g in range(GROUPS):
                    for u in range(4):
                        if g < GROUPS - 1:
                            bias_max(b, g + 1, u)
                        elif ahead:
                            bias_max(b + 1, 0, u)
                        if u == 3 and g in VECTOR_COPIES:
                            copy_pt1(b, g)
                        if two_behind:
                            part = {(0, 1): 0, (1, 1): 1, (1, 3): 2, (3, 1): 3}.get((g, u))
                            if part is not None:
                                router(b - 2, par, part)
                        if (g, u) == (1, 0) and one_behind:
                            norm(b - 1, o, 1)
                        if (g, u) == (0, 3) and ahead:
                            split_q(b + 1)
                            split_k(b + 1)
                        if (g, u) == (1, 3):
                            invert(b, par, 0)
                        if one_behind:
                            if (g, u) == (2, 2):
                                ln_stats(b - 1, o, h - 1 + par)
                            if (g, u) == (2, 3):
                                ln_apply(b - 1, o, h - 1 + par)
                        if (g, u) == (3, 0):
                            norm(b, par, 0)
                        if (g, u) == (3, 3):
                            invert(b, par, 1)

            split_q(0)
            split_k(0)
            for u in range(4):
                bias_max(0, 0, u)
            attention_loop(dve, body)

            def shared_act(tb, m):
                dve.wait_ge(sh_silu, 2 * tb + m + 1)
                need(dve, sh_down, 4 * tb)
                dve.tensor_tensor(sh_a[m][:], T_BANK[m][:], sh_g[m][:], ALU.mult).then_inc(sh_act, 1)

            def shared_add(tb):
                for i in range(2):
                    dve.wait_ge(x1_kept[i], 32 * (tb + 1))
                for t in range(4):
                    tile = x_sum[:, 4 * tb + t, :]
                    dve.wait_ge(sh_down, 4 * tb + t + 1)
                    dve.tensor_tensor(tile, DOWN[t % 2][:, 0:DIM], tile, ALU.add).then_inc(sh_added, 1)

            b = BATCH - 1
            norm(b, 1, 1)
            for part in range(3):
                router(b - 1, 0, part)
            ln_stats(b, 1, b // 2)
            ln_apply(b, 1, b // 2)
            shared_act(0, 0)
            shared_act(0, 1)
            router(b - 1, 0, 3)
            shared_add(0)
            shared_act(1, 0)
            shared_act(1, 1)
            for part in range(3):
                router(b, 1, part)
            shared_add(1)
            shared_act(2, 0)
            router(b, 1, 3)
            shared_act(2, 1)

            cnt = LOGITS[:, 0:EXPERTS]
            col = [fin[:, k:k + 1] for k in range(8)]
            slot = cst[:, C_SLOT:C_SLOT + 1]
            dve.wait_ge(counts_ready, 1)
            steps = [
                lambda: dve.tensor_scalar(cnt_i[:], cnt, -1.0, None, ALU.add),
                lambda: dve.tensor_scalar(rows_of[:], cnt, -float(P), None, ALU.add),
                lambda: dve.tensor_scalar(cnt_s[:], cnt_i[:], 7, None, ALU.arith_shift_right),
                lambda: dve.tensor_copy(per_e[:], cnt_s[:]),
                lambda: dve.tensor_tensor_scan(upto[:], one_row[:], per_e[:], 0.0, ALU.mult, ALU.add),
                lambda: dve.tensor_scalar(used[:], upto[:], slot, None, ALU.is_le),
                lambda: dve.tensor_reduce(col[0], used[:], AX.X, ALU.add),
                lambda: dve.tensor_tensor(before[:], used[:], per_e[:], ALU.mult),
                lambda: dve.tensor_reduce(col[1], before[:], AX.X, ALU.add),
                lambda: dve.tensor_tensor(col[2], slot, col[1], ALU.subtract),
                lambda: dve.tensor_scalar(col[3], col[2], float(P), float(P), ALU.mult, ALU.add),
                lambda: dve.scalar_tensor_tensor(rows_here[:], iota, col[0], rows_of[:], ALU.is_equal, ALU.mult),
                lambda: dve.tensor_reduce(col[4], rows_here[:], AX.X, ALU.add),
                lambda: dve.tensor_tensor(col[5], col[3], col[4], ALU.min),
                lambda: dve.scalar_tensor_tensor(col[6], col[0], float(REGION), col[5], ALU.mult, ALU.add),
                lambda: dve.tensor_scalar(col[7], col[0], float(EXPERTS - 1), None, ALU.min),
                lambda: dve.tensor_tensor(shift[:], col[3].to_broadcast([P, P]), col[4].to_broadcast([P, P]),
                                          ALU.subtract),
            ]
            for k, f in enumerate(steps):
                need(dve, fin_step, k)
                f().then_inc(fin_step, 1)

            shared_add(2)
            dve.wait_ge(counts_ready, 2)
            dve.tensor_copy(slot_tab[:], Q_BANK[0:1, SEQ:SEQ + P]).then_inc(fin_step, 1)
            dve.tensor_copy(packed_tab[:], Q_BANK[0:1, SEQ + P:SEQ + P + SLOTS // PACKED]).then_inc(fin_step, 1)
            dve.tensor_scalar(again[:], Q_BANK[:, 0:P], slot, float(NO_ROW), ALU.is_gt, ALU.mult
                              ).then_inc(fin_step, 1)
            shared_act(3, 0)
            shared_act(3, 1)
            shared_add(3)

            def step(k, turn):
                if turn.exists(k, 0):
                    turn.wait(dve, e_silu, k, 0)
                    turn.wait(dve, ey_sent, k, 0, 16, again=-1)
                    dve.tensor_tensor(out_row[:, k:k + 1], xg[k][:, DIM:DIM + 1],
                                      again[:, bass.ds(UNROLL * turn.turn + k, 1)], ALU.add)
                    dve.tensor_tensor(ea[k % 2][:], S_BANK[k % 2][:, INTER:2 * INTER], eg[k % 4][:], ALU.mult
                                      ).then_inc(e_act[k], 1)
                if turn.exists(k, -1):
                    at = (k - 1) % UNROLL
                    turn.wait(dve, ea_turned, k, -1)
                    dve.tensor_copy(eaT[at % 2][:], T_BANK[at % 2][:, 0:P]).then_inc(ea_copied[at], 1)

            dve.wait_ge(fin_step, FIN_STEPS + 3)
            slot_loop(dve, step)

            def final_stage2(p, par):
                dve.wait_ge(f_root, 2 * p + 2)
                polish(f_fin, 5 * p, f_small[:, par], 2)
                dve.scalar_tensor_tensor(f_small[:, par, 7, :], f_mv[:, par, :, 0], -1.0, f_small[:, par, 6, :],
                                         ALU.mult, ALU.mult).then_inc(f_fin, 1)

            def final(p, par, h):
                n = F_STATS * p
                tile = x_sum[:, bass.ds(2 * p, 1), :].rearrange("p a d -> p (a d)")
                dve.wait_ge(y_loaded[2 * par], 16 * (h + 1))
                need(dve, f_stat, n)
                dve.tensor_reduce(y_sum, rows_y[:, bass.ds(2 * p, 1), :].rearrange("p a (j d) -> p (a d) j", j=TOPK),
                                  AX.X, ALU.add
                                  ).then_inc(f_stat, 1)
                dve.wait_ge(f_stat, n + 1)
                need(dve, f_done, 2 * (p - 1))
                dve.tensor_tensor(f_resid[:, par, :], y_sum, tile, ALU.add).then_inc(f_stat, 1)
                dve.wait_ge(f_stat, n + 2)
                dve.bn_stats(f_bn[:, par, 0, :], f_resid[:, par, :]).then_inc(f_stat, 1)
                if not isinstance(p, int) or p > 0:
                    final_stage2(p - 1, 1 - par)
                dve.wait_ge(f_summed, p + 1)
                dve.bn_stats(f_bn[:, par, 1, :], S_BANK[par][:, 0:DIM]).then_inc(f_stat, 1)
                need_apart(dve, f_stat, n + 4, passed)
                for t in range(2):
                    dve.bn_aggr(f_mv[:, par, t, :], f_bn[:, par, t, :]).then_inc(f_stat, 1)
                dve.wait_ge(f_stat, n + 6)
                dve.tensor_scalar(f_small[:, par, 0, :], f_mv[:, par, :, 1], EPS, None, ALU.add).then_inc(f_stat, 1)

            pair_loop(dve, final)
            final_stage2(TILES // 2 - 1, 1)

        @block.gpsimd
        def _(pool):
            pool.memset(empty[:, 0:DIM], 0.0).then_inc(pool_set_up, 1)
            pool.memset(empty[:, DIM:DIM + 1], float(NO_ROW)).then_inc(pool_set_up, 1)
            pool.memset(empty[:, DIM + 1:ROW], 0.0).then_inc(pool_set_up, 1)
            pool.iota(codes[:], [[P * TOPK, TILES], [1, TOPK]], base=0, channel_multiplier=TOPK
                      ).then_inc(pool_set_up, 1)

            def dispatch(b, par):
                need_apart(pool, scattered, 16 * 2 * TOPK * b, passed)
                pool.tensor_copy(rows[:, :, :, DIM:DIM + 1],
                                 codes[:, bass.ds(2 * b, 2), :].unsqueeze(3)).then_inc(codes_copied, 1)
                need_apart(pool, gate_step, GATE_STEPS * b + 18, passed)
                pool.tensor_copy(rows[:, :, :, DIM + 1:ROW], weight[:].unsqueeze(3)).then_inc(codes_copied, 1)
                need_apart(pool, gate_step, GATE_STEPS * b + GATE_STEPS, passed)
                need_apart(pool, codes_copied, 2 * b + 2, passed)
                need_apart(pool, rows_copied, 2 * b + 2, passed)
                for t in range(2):
                    for j in range(TOPK):
                        pool.indirect_dma_start(
                            routed, bass.IndirectOffsetOnAxis(ap=position[:, t, j:j + 1], axis=0),
                            rows[:, t, j, :], None).then_inc(scattered, 16)

            pool.wait_ge(pool_set_up, 4)
            dispatch(0, 0)
            with pool.Fori(0, (BATCH - 2) // 2) as i:
                dispatch(2 * i + 1, 1)
                dispatch(2 * i + 2, 0)
            dispatch(BATCH - 1, 1)

            def send(k, count):
                need_apart(pool, ey_ready[k], count, passed)
                pool.indirect_dma_start(
                    expert_out, bass.IndirectOffsetOnAxis(ap=out_row[:, k:k + 1], axis=0),
                    ey[k], None, bounds_check=TOKENS * TOPK - 1, oob_is_err=False
                ).then_inc(ey_sent[k], 16)

            with pool.Fori(0, SLOTS // UNROLL) as i:
                count = pool.snap(i + 1)
                for k in range(UNROLL):
                    send(k, count)

            def final(p, par, h):
                pool.wait_ge(y_loaded[2 * par + 1], 16 * (h + 1))
                need(pool, f_summed, p - 1)
                row = rows_y[:, bass.ds(2 * p + 1, 1), :].rearrange("p a n -> p (a n)")
                pool.tensor_tensor(y_half[par][:].rearrange("p c d -> p (c d)"), row[:, 0:2 * DIM],
                                   row[:, 2 * DIM:4 * DIM], ALU.add).then_inc(f_paired, 1)

            pair_loop(pool, final)


_OUT = (BATCH, SEQ, DIM)


def _constants():
    import numpy as np

    c = np.zeros((P, C_END), np.float32)
    c[:, C_ID:C_ID + P] = np.eye(P)
    c[:, C_TRI:C_TRI + P] = np.triu(np.ones((P, P)), 1)
    c[:, C_IOTA:C_IOTA + EXPERTS] = np.arange(EXPERTS)
    c[:, C_SLOT] = np.arange(P)
    slots = np.arange(SLOTS)
    c[slots, C_PACK + slots // PACKED] = EXPERTS ** (slots % PACKED)
    slopes = ((2.0 ** (-8.0 / HEADS)) ** np.arange(1, HEADS + 1)).astype(np.float32)
    dist = (P + np.arange(P))[:, None] - np.arange(SEQ)[None, :]
    root = np.sqrt(np.maximum(dist, 0).astype(np.float32))
    bias = -slopes[None, :, None] * root[:, None, :]
    return c, np.where(dist[:, None, :] >= 0, bias, np.float32(-1e30)).astype(np.float32)


def kernel(L0_attn_x, L0_attn_Wq, L0_attn_Wk, L0_attn_Wv, L0_attn_Wo, L0_ffn_gate_w,
           L0_ffn_w11, L0_ffn_w33, L0_ffn_w22, L0_ffn_sw1, L0_ffn_sw2, L0_ffn_sw3):
    import numpy as np
    import concourse.bacc as bacc
    from concourse.bass_utils import run_bass_kernel_spmd

    def chunks(w):
        t = np.asarray(w).T
        return np.ascontiguousarray(t.reshape(-1, P, t.shape[1]).transpose(1, 0, 2))

    x = np.asarray(L0_attn_x).reshape(TOKENS, DIM)
    wq = np.asarray(L0_attn_Wq).reshape(PAIRS, 2, HD, DIM).transpose(1, 0, 2, 3).reshape(DIM, DIM)
    wk = np.asarray(L0_attn_Wk).reshape(GROUPS, 1, HD, DIM).repeat(2, 1).reshape(P, DIM)
    w13 = np.stack([np.asarray(L0_ffn_w11), np.asarray(L0_ffn_w33)], 1).reshape(EXPERTS, 2 * INTER, KC, P)
    w2 = np.asarray(L0_ffn_w22).transpose(2, 0, 1).reshape(P, -1)
    consts, bias = _constants()
    arrays = {
        "xT": np.ascontiguousarray(x.T), "x": x,
        "wq": chunks(wq), "wk": chunks(wk), "wv": chunks(L0_attn_Wv),
        "wo": chunks(L0_attn_Wo),
        "bias": bias, "consts": consts, "gate_w": chunks(L0_ffn_gate_w),
        "expert_weights": np.concatenate([w13.transpose(3, 0, 2, 1).reshape(P, -1), w2], 1),
        "sw1": chunks(L0_ffn_sw1), "sw3": chunks(L0_ffn_sw3), "sw2": chunks(L0_ffn_sw2),
    }
    nc = bacc.Bacc("TRN2", target_bir_lowering=False, num_devices=1)
    args = {n: nc.dram_tensor(n, a.shape, mybir.dt.from_np(a.dtype), kind="ExternalInput").ap()
            for n, a in arrays.items()}
    out = nc.dram_tensor("out", _OUT, F32, kind="ExternalOutput").ap()
    build(nc, out=out, **args)
    r = run_bass_kernel_spmd(nc, [arrays], core_ids=[0])
    return r.results[0]["out"]
```
